# Optimizing a Trainium2 kernel written in Bass

```python
import numpy as np
import jax
import jax.numpy as jnp

def _softmax(x, axis=-1):
    return jax.nn.softmax(x, axis=axis)

def _gelu(x):
    return jax.nn.gelu(x, approximate=True)

def _silu(x):
    return jax.nn.silu(x)

def _sigmoid(x):
    return jax.nn.sigmoid(x)

def _layernorm(x, axis=-1, eps=1e-05):
    m = jnp.mean(x, axis=axis, keepdims=True)
    v = jnp.var(x, axis=axis, keepdims=True)
    return (x - m) / jnp.sqrt(v + eps)

def _scatter_add(tgt, idx, src, axis=0):
    return tgt.at[idx].add(src)

def _segment_sum(src, seg, n):
    return jax.ops.segment_sum(src, seg, n)
kernel_name = 'mk_adj_preln_d4_adj_r2_6800c9'

def setup_inputs(seed: int=0):
    np.random.seed(seed)
    _w = jnp.asarray

    def _rec_inputs():
        import jax
        import jax.numpy as jnp
        _gk = jax.random.key(seed)
        x = 7.22e-05 + 1 * jax.random.normal(jax.random.fold_in(_gk, 1), (64, 128, 128), jnp.float32)
        _w = (1.0 + jnp.arange(128, dtype=jnp.float32)) ** (-0.5)
        _w = _w / _w.mean()
        _pij = jnp.clip(0.03125 * _w[:, None] * _w[None, :], 0.0, 1.0)
        _a = jax.random.uniform(jax.random.fold_in(_gk, 2), (64, 128, 128)) < _pij
        _af = _a.astype(jnp.float32)
        adj = _af
        _nm = jnp.ones((64, 128), dtype=bool)
        nodemask = jnp.where(_nm, 1.0, 0.0).astype(jnp.float32)
        return (x, adj, nodemask)
    x, adj, nodemask = _rec_inputs()

    def _L0_gnn_setup():
        import jax, jax.numpy as jnp
        import numpy as np
        B, N, D, C, L = (64, 256, 128, 128, 5)
        EDGE_P = 0.02

        def _gru_cell(m, h, w_ih, w_hh, b_ih, b_hh):
            gi = m @ w_ih.T + b_ih
            gh = h @ w_hh.T + b_hh
            i_r, i_z, i_n = jnp.split(gi, 3, axis=-1)
            h_r, h_z, h_n = jnp.split(gh, 3, axis=-1)
            r = jax.nn.sigmoid(i_r + h_r)
            z = jax.nn.sigmoid(i_z + h_z)
            n = jnp.tanh(i_n + r * h_n)
            return (1.0 - z) * n + z * h
        key = jax.random.key(seed)
        ks = jax.random.split(key, 8)
        x = jax.random.normal(ks[0], (B, N, D), dtype=jnp.float32)
        adj = (jax.random.uniform(ks[1], (B, N, N)) < EDGE_P).astype(jnp.float32)
        mask = jnp.ones((B, N), dtype=jnp.float32)
        s = 1.0 / np.sqrt(C).astype(np.float32)
        weight = jax.random.uniform(ks[2], (L, C, C), minval=-s, maxval=s, dtype=jnp.float32)
        w_ih = jax.random.uniform(ks[3], (3 * C, C), minval=-s, maxval=s, dtype=jnp.float32)
        w_hh = jax.random.uniform(ks[4], (3 * C, C), minval=-s, maxval=s, dtype=jnp.float32)
        b_ih = jax.random.uniform(ks[5], (3 * C,), minval=-s, maxval=s, dtype=jnp.float32)
        b_hh = jax.random.uniform(ks[6], (3 * C,), minval=-s, maxval=s, dtype=jnp.float32)
        return dict(x=x, adj=adj, mask=mask, weight=weight, w_ih=w_ih, w_hh=w_hh, b_ih=b_ih, b_hh=b_hh)
    _L0_gnn_all = _L0_gnn_setup()
    _L0_gnn_in = {k: v for k, v in _L0_gnn_all.items() if k in ('weight', 'w_ih', 'w_hh', 'b_ih', 'b_hh')}
    del _L0_gnn_all

    def _L1_gnn_setup():
        import jax, jax.numpy as jnp
        import numpy as np
        B, N, D = (4, 2048, 128)
        DENSITY = 32.0 / N
        key = jax.random.key(seed)
        kx, ka, k1, k2, k3, k4 = jax.random.split(key, 6)
        x = jax.random.normal(kx, (B, N, D), dtype=jnp.float32)
        adj = (jax.random.uniform(ka, (B, N, N)) < DENSITY).astype(jnp.float32)
        scale = 0.02
        theta = scale * jax.random.normal(k1, (D, D), dtype=jnp.float32)
        W_h = scale * jax.random.normal(k2, (D, D), dtype=jnp.float32)
        W_t = scale * jax.random.normal(k3, (D, D), dtype=jnp.float32)
        b_t = scale * jax.random.normal(k4, (D,), dtype=jnp.float32)
        return {'x': x, 'adj': adj, 'theta': theta, 'W_h': W_h, 'W_t': W_t, 'b_t': b_t}
    _L1_gnn_all = _L1_gnn_setup()
    _L1_gnn_in = {k: v for k, v in _L1_gnn_all.items() if k in ('theta', 'W_h', 'W_t', 'b_t')}
    del _L1_gnn_all

    def _L2_gnn_setup():
        import jax, jax.numpy as jnp
        import numpy as np
        GROUPS = [list(range(25)), [0, 1, 2, 3, 4, 5, 6, 7, 8], [0, 9, 10, 11, 12, 13, 14], [6, 7, 8, 12, 13, 14], [3, 4, 5, 9, 10, 11]]
        B, N, D_IN, D_HID = (4096, 25, 128, 256)

        def _graph_conv(x, adj, W, b):
            n = adj.shape[-1]
            A = adj + jnp.eye(n, dtype=adj.dtype)
            deg = jnp.sum(A, axis=-1)
            deg_safe = jnp.where(deg == 0, 1.0, deg)
            dinv = jnp.where(deg == 0, 0.0, deg_safe ** (-0.5))
            norm_adj = dinv[:, :, None] * A * dinv[:, None, :]
            support = jnp.einsum('bnd,de->bne', x, W)
            out = jnp.einsum('bnm,bme->bne', norm_adj, support) + b
            return jax.nn.relu(out)
        key = jax.random.key(seed)
        ks = jax.random.split(key, 7)
        s1 = float(np.sqrt(6.0 / (D_IN + D_HID)))
        s2 = float(np.sqrt(6.0 / (D_HID + D_IN)))
        return {'x': jax.random.normal(ks[0], (B, N, D_IN), dtype=jnp.float32), 'adj': jax.random.uniform(ks[1], (B, N, N), dtype=jnp.float32), 'W1': jax.random.uniform(ks[2], (5, D_IN, D_HID), jnp.float32, -s1, s1), 'b1': jnp.zeros((5, D_HID), dtype=jnp.float32), 'W2': jax.random.uniform(ks[3], (5, D_HID, D_IN), jnp.float32, -s2, s2), 'b2': jnp.zeros((5, D_IN), dtype=jnp.float32), 'fusion_w': jnp.ones((5,), dtype=jnp.float32)}
    _L2_gnn_all = _L2_gnn_setup()
    _L2_gnn_in = {k: v for k, v in _L2_gnn_all.items() if k in ('W1', 'b1', 'W2', 'b2', 'fusion_w')}
    del _L2_gnn_all

    def _L3_gnn_setup():
        import jax, jax.numpy as jnp
        import numpy as np
        EPS = 1e-08
        key = jax.random.key(seed)
        kH, kA, kW = jax.random.split(key, 3)
        B, N, IN, OUT = (32, 256, 128, 128)
        H = jax.random.normal(kH, (B, N, IN), dtype=jnp.float32)
        A = jax.random.uniform(kA, (B, N, N), dtype=jnp.float32)
        mask = jnp.ones((B, N), dtype=jnp.float32)
        W = jax.random.normal(kW, (OUT, IN), dtype=jnp.float32) * (1.0 / np.sqrt(IN))
        b = jnp.zeros((OUT,), dtype=jnp.float32)
        return {'H': H, 'A': A, 'mask': mask, 'W': W, 'b': b}
    _L3_gnn_all = _L3_gnn_setup()
    _L3_gnn_in = {k: v for k, v in _L3_gnn_all.items() if k in ('W', 'b')}
    del _L3_gnn_all
    return {'x': x, 'adj': adj, 'nodemask': nodemask, 'L0_gnn_weight': _L0_gnn_in['weight'], 'L0_gnn_w_ih': _L0_gnn_in['w_ih'], 'L0_gnn_w_hh': _L0_gnn_in['w_hh'], 'L0_gnn_b_ih': _L0_gnn_in['b_ih'], 'L0_gnn_b_hh': _L0_gnn_in['b_hh'], 'L1_gnn_theta': _L1_gnn_in['theta'], 'L1_gnn_W_h': _L1_gnn_in['W_h'], 'L1_gnn_W_t': _L1_gnn_in['W_t'], 'L1_gnn_b_t': _L1_gnn_in['b_t'], 'L2_gnn_W1': _L2_gnn_in['W1'], 'L2_gnn_b1': _L2_gnn_in['b1'], 'L2_gnn_W2': _L2_gnn_in['W2'], 'L2_gnn_b2': _L2_gnn_in['b2'], 'L2_gnn_fusion_w': _L2_gnn_in['fusion_w'], 'L3_gnn_W': _L3_gnn_in['W'], 'L3_gnn_b': _L3_gnn_in['b']}

def reference(x, adj, nodemask, L0_gnn_weight, L0_gnn_w_ih, L0_gnn_w_hh, L0_gnn_b_ih, L0_gnn_b_hh, L1_gnn_theta, L1_gnn_W_h, L1_gnn_W_t, L1_gnn_b_t, L2_gnn_W1, L2_gnn_b1, L2_gnn_W2, L2_gnn_b2, L2_gnn_fusion_w, L3_gnn_W, L3_gnn_b):
    import jax
    import jax.numpy as jnp

    def _L0_gnn_ref(x, adj, mask, weight, w_ih, w_hh, b_ih, b_hh):
        import jax, jax.numpy as jnp
        import numpy as np
        B, N, D, C, L = (64, 256, 128, 128, 5)
        EDGE_P = 0.02

        def _gru_cell(m, h, w_ih, w_hh, b_ih, b_hh):
            gi = m @ w_ih.T + b_ih
            gh = h @ w_hh.T + b_hh
            i_r, i_z, i_n = jnp.split(gi, 3, axis=-1)
            h_r, h_z, h_n = jnp.split(gh, 3, axis=-1)
            r = jax.nn.sigmoid(i_r + h_r)
            z = jax.nn.sigmoid(i_z + h_z)
            n = jnp.tanh(i_n + r * h_n)
            return (1.0 - z) * n + z * h
        A = (adj != 0).astype(x.dtype)
        h = x
        for l in range(weight.shape[0]):
            m = jnp.einsum('bnd,de->bne', h, weight[l])
            agg = jnp.einsum('bij,bid->bjd', A, m)
            h = _gru_cell(agg, h, w_ih, w_hh, b_ih, b_hh)
        return h * mask[..., None]

    def _L1_gnn_ref(x, adj, theta, W_h, W_t, b_t):
        import jax, jax.numpy as jnp
        import numpy as np
        B, N, D = (4, 2048, 128)
        DENSITY = 32.0 / N
        in_degrees = jnp.sum(jnp.abs(adj), axis=-1)
        norm = ((in_degrees + 1e-06) ** (-0.5))[..., None]
        f_hom = jnp.einsum('bnd,de->bne', x, theta) * norm
        f_hom = jnp.einsum('bnm,bmd->bnd', adj, f_hom) * norm
        f_het = jnp.einsum('bnd,de->bne', x, W_h)
        gate = jax.nn.sigmoid(jnp.einsum('bnd,de->bne', x, W_t) + b_t)
        out = gate * f_hom + (1.0 - gate) * f_het
        return jax.nn.elu(out)

    def _L2_gnn_ref(x, adj, W1, b1, W2, b2, fusion_w):
        import jax, jax.numpy as jnp
        import numpy as np
        GROUPS = [list(range(25)), [0, 1, 2, 3, 4, 5, 6, 7, 8], [0, 9, 10, 11, 12, 13, 14], [6, 7, 8, 12, 13, 14], [3, 4, 5, 9, 10, 11]]
        B, N, D_IN, D_HID = (4096, 25, 128, 256)

        def _graph_conv(x, adj, W, b):
            n = adj.shape[-1]
            A = adj + jnp.eye(n, dtype=adj.dtype)
            deg = jnp.sum(A, axis=-1)
            deg_safe = jnp.where(deg == 0, 1.0, deg)
            dinv = jnp.where(deg == 0, 0.0, deg_safe ** (-0.5))
            norm_adj = dinv[:, :, None] * A * dinv[:, None, :]
            support = jnp.einsum('bnd,de->bne', x, W)
            out = jnp.einsum('bnm,bme->bne', norm_adj, support) + b
            return jax.nn.relu(out)
        norm_w = jax.nn.softmax(fusion_w)
        fused = jnp.zeros_like(x)
        for g, idx_list in enumerate(GROUPS):
            idx = jnp.asarray(idx_list)
            x_g = x[:, idx, :]
            adj_g = adj[:, idx][:, :, idx]
            h = _graph_conv(x_g, adj_g, W1[g], b1[g])
            out_g = _graph_conv(h, adj_g, W2[g], b2[g])
            fused = fused.at[:, idx, :].add(norm_w[g] * out_g)
        return fused

    def _L3_gnn_ref(H, A, mask, W, b):
        import jax, jax.numpy as jnp
        import numpy as np
        EPS = 1e-08
        N = A.shape[-1]
        A_hat = A + jnp.eye(N, dtype=A.dtype)
        deg = A_hat.sum(axis=-1)
        dis = (deg + EPS) ** (-0.5)
        A_norm = dis[:, :, None] * A_hat * dis[:, None, :]
        H_lin = jnp.einsum('bni,oi->bno', H, W) + b
        out = jnp.einsum('bnm,bmo->bno', A_norm, H_lin)
        out = out * mask[:, :, None]
        return jax.nn.relu(out)
    h = jnp.maximum(_layernorm(x, axis=-1), 0.0)
    x = x + _L0_gnn_ref(h, adj, nodemask, L0_gnn_weight, L0_gnn_w_ih, L0_gnn_w_hh, L0_gnn_b_ih, L0_gnn_b_hh)
    h = jnp.maximum(_layernorm(x, axis=-1), 0.0)
    x = x + _L1_gnn_ref(h, adj, L1_gnn_theta, L1_gnn_W_h, L1_gnn_W_t, L1_gnn_b_t)
    h = jnp.maximum(_layernorm(x, axis=-1), 0.0)
    x = x + _L2_gnn_ref(h, adj, L2_gnn_W1, L2_gnn_b1, L2_gnn_W2, L2_gnn_b2, L2_gnn_fusion_w)
    h = jnp.maximum(_layernorm(x, axis=-1), 0.0)
    x = x + _L3_gnn_ref(h, adj, nodemask, L3_gnn_W, L3_gnn_b)
    return x

_drawn_inputs = setup_inputs


def setup_inputs(seed=0):
    import zlib

    import numpy as np

    out = dict(_drawn_inputs(seed))
    spreads = {'L2_gnn_b1': (0.0, 0.8),
     'L2_gnn_b2': (0.0, 0.8),
     'L2_gnn_fusion_w': (1.0, 0.6),
     'L3_gnn_b': (0.0, 0.8)}
    factors = {'L1_gnn_W_h': 7.532, 'L1_gnn_b_t': 4.565, 'L2_gnn_W1': 8.0, 'L2_gnn_W2': 8.0}
    for name, (base, spread) in spreads.items():
        noise = np.random.default_rng([zlib.crc32(name.encode()), seed]).standard_normal(out[name].shape)
        drawn = base * np.exp(spread * noise) if base else spread * noise
        out[name] = jnp.asarray(drawn.astype(out[name].dtype))
    for name, factor in factors.items():
        out[name] = (out[name] * factor).astype(out[name].dtype)
    return out
```

```python
import concourse.bass as bass
from concourse import mybir
from contextlib import ExitStack

LN_EPS = 1e-5
QUAD = 4
QUADS = 4
LAYERS = 5
GROUP_RUNS = [[(0, 25)], [(0, 9)], [(0, 1), (9, 15)], [(6, 9), (12, 15)], [(3, 6), (9, 12)]]
GROUP_GRAPHS = [4, 8, 16, 16, 16]
ZONE = 25


def graph_stack(nc, x, adj, nodemask, conv_w, w_ih, w_hh, b_ih, b_hh, theta, W_h, W_t, b_t,
                W1, b1, W2, b2, fusion_w, W3, b3, out):
    f32, f32r = mybir.dt.float32, mybir.dt.float32r
    ALU, ACT, AX = mybir.AluOpType, mybir.ActivationFunctionType, mybir.AxisListType
    B, N, D = x.shape
    RG = QUAD * QUADS
    HALF = RG // 2
    ROUNDS = B // RG
    STEPS = LAYERS * QUADS
    PRODUCED = STEPS + QUADS
    E = W1.shape[2]
    EH = E // 128
    NG = len(GROUP_RUNS)
    SIZE = [sum(b - a for a, b in runs) for runs in GROUP_RUNS]
    TILES = [(g, t * G, G, G * SIZE[g]) for g, G in enumerate(GROUP_GRAPHS) for t in range(RG // G)]
    NT = len(TILES)

    ctx = ExitStack()
    with ctx:
        ctx.enter_context(nc.allow_non_contiguous_dma("small transposed loads at the start"))

        def sb(name, shape, dt=f32):
            return ctx.enter_context(nc.sbuf_tensor(name, shape, dt))

        ident = sb("ident", [128, 128])
        neg_half, eps_ln, eps_deg = (sb(n, [128, RG]) for n in ("neg_half", "eps_ln", "eps_deg"))
        gmask = [sb(f"gmask{g}", [128, GROUP_GRAPHS[g]]) for g in range(NG)]
        mask_nat = sb("mask_nat", [B, 128])
        w3T = sb("w3T", [128, 128])
        mask_all = sb("mask_all", [128, B])
        whh_hi, whh_lo = sb("whh_hi", [128, 3, 128], f32r), sb("whh_lo", [128, 3, 128], f32r)
        wc_hi, wc_lo = sb("wc_hi", [128, LAYERS, 384], f32r), sb("wc_lo", [128, LAYERS, 384], f32r)
        wcur_hi = [sb(f"wcur_hi{i}", [128, 384], f32r) for i in range(2)]
        wcur_lo = [sb(f"wcur_lo{i}", [128, 384], f32r) for i in range(2)]
        bih, bhh, brz = sb("bih", [128, 3]), sb("bhh", [128, 3]), sb("brz", [128, 2])
        brz2 = sb("brz2", [128, 2])
        wl1 = sb("wl1", [128, 384])
        bt_bc, b3_bc = sb("bt_bc", [128, 128]), sb("b3_bc", [128, 128])
        w1_sb, w2_sb = sb("w1_sb", [128, NG, E]), sb("w2_sb", [128, NG, EH, 128])
        b1_sb, b2_sb = sb("b1_sb", [128, NG, EH]), sb("b2_sb", [128, NG])
        fw, fmax, fexp, fsum, finv, fshare = (sb(n, [128, NG if n in ("fw", "fexp", "fshare") else 1])
                                              for n in ("fw", "fmax", "fexp", "fsum", "finv", "fshare"))

        x_in = sb("x_in", [128, RG, 128])
        adj_in = sb("adj_in", [128, RG, 128])
        x_res = sb("x_res", [128, RG, 128])
        edge = sb("edge", [128, RG, 128])
        adjT = sb("adjT", [128, RG, 128])
        adjTI = sb("adjTI", [128, RG, 128])
        conv_nat, wih_nat, whh_nat = adjTI[:, 0:LAYERS, :], adjTI[:, 5:8, :], adjTI[:, 8:11, :]
        w3_nat, convT, wihT = adjTI[:, 11, :], adjT[:, 0:LAYERS, :], adjT[:, 5:8, :]
        mask_r = sb("mask_r", [128, RG])
        deg1, deg3 = sb("deg1", [128, RG]), sb("deg3", [128, RG])
        norm1, dis, dis_mask = sb("norm1", [128, RG]), sb("dis", [128, RG]), sb("dis_mask", [128, RG])
        degs1, degs3 = sb("degs1", [128, RG]), sb("degs3", [128, RG])
        stats = sb("stats", [128, RG, 6])
        mv = sb("mv", [128, RG, 2])
        var_eps, rstd = sb("var_eps", [128, RG]), sb("rstd", [128, RG])
        xn = sb("xn", [128, RG, 128])
        hT = sb("hT", [128, RG, 128])
        h = [sb(f"h{q}", [128, 512]) for q in range(QUADS)]
        h_hi = [sb(f"h_hi{q}", [128, 512], f32r) for q in range(QUADS)]
        h_lo = [sb(f"h_lo{q}", [128, 512], f32r) for q in range(QUADS)]
        hn = [sb(f"hn{i}", [128, QUAD, 128]) for i in range(2)]
        g_hi = [sb(f"g_hi{i}", [128, 512], f32r) for i in range(2)]
        g_lo = [sb(f"g_lo{i}", [128, 512], f32r) for i in range(2)]
        gr, gz, rh, pre, gn, hd, zd = ([sb(f"{n}{i}", [128, 512]) for i in range(2)]
                                       for n in ("gr", "gz", "rh", "pre", "gn", "hd", "zd"))
        f_hom, f_het = sb("f_hom", [128, 2, 512]), sb("f_het", [128, 2, 512])
        gate_pre, gate_th, agg_n, diff, gated, mix, neg, ex = gr, gz, rh, pre, gn, hd, zd, hn
        rows = [sb(f"rows{g}", [128, RG // GROUP_GRAPHS[g], SIZE[g]]) for g in range(NG)]
        deg2, deg_zero, deg_safe, deg_pow, dinv = (sb(n, [128, NT]) for n in
                                                   ("deg2", "deg_zero", "deg_safe", "deg_pow", "dinv"))
        deg_some = sb("deg_some", [128, NT])
        blocks0, blocks = sb("blocks0", [128, NT, 128]), sb("blocks", [128, NT, 128])
        normT = sb("normT", [128, NT, 128])
        packed = sb("packed", [128, NT, 128])
        sup1 = sb("sup1", [128, 2, E])
        hid = sb("hid", [128, 2, EH, 128])
        sup2 = sb("sup2", [128, 2, 128])
        conv2 = sb("conv2", [128, 2, 128])
        fused = sb("fused", [128, ZONE, RG])
        y0, y = hd, zd

        bank = [ctx.enter_context(nc.psum_tensor(f"bank{i}", [128, 512], f32)) for i in range(2)]
        quad_bank = ctx.enter_context(nc.psum_tensor("quad_bank", [128, 4, 512], f32))
        bank += [quad_bank[:, i, :] for i in range(4)]
        bank += [ctx.enter_context(nc.psum_tensor(f"bank{i}", [128, 512], f32)) for i in (6, 7)]
        T_BANK, G_BANK, R_BANK, Z_BANK, H_BANK, I_BANK, A_BANK, B_BANK = bank

        sem = {n: ctx.enter_context(nc.semaphore(n)) for n in (
            "weights_loaded", "x_loaded", "adj_loaded", "rows_loaded", "stored",
            "x_in_free", "adj_in_free", "rows_free", "pe_passed", "dve_passed",
            "consts", "dve_setup", "w_turned", "w_turned_read", "wc_made", "setup_done", "fexp_done",
            "mask_round", "degs", "degs_eps", "norms", "adj_turned", "adjT_ready", "adjTI_ready", "edge_ready",
            "group_sum", "group_safe", "group_pow", "group_dinv", "blocks_half", "blocks_ready",
            "blocks_turned", "normT_ready",
            "wA", "wB", "h_new", "h_hi_new", "h_lo_new", "h_turned", "hn_ready", "g_made", "g_hi_ready",
            "g_lo_ready", "gates_r", "gates_h", "hb_ready", "gates_n", "gates_z", "r_ready", "z_ready", "rh_ready", "pre_ready",
            "n_ready", "hd_ready", "zd_ready",
            "l1_turned", "l1_x", "l1_lin", "l1_gate_pre", "l1_f_hom", "l1_f_het", "l1_gate", "l1_agg",
            "l1_agg_n", "l1_diff", "l1_gated", "l1_mix", "l1_neg", "l1_exp", "l1_elu", "l1_out",
            "zone_turned", "packed_ready", "fused_zero", "l2_sup1", "l2_sup1_read", "l2_hid",
            "l2_hid_read", "l2_sup2", "l2_sup2_read", "l2_conv2", "l2_conv2_read", "l2_added",
            "l2_back", "l2_out",
            "l3_lin", "l3_bias", "l3_y", "l3_agg", "l3_scaled", "out_ready",
        )}
        for L in range(4):
            for n in ("stats", "mv", "var", "rstd", "xn", "turned", "h"):
                sem[f"ln{L}_{n}"] = ctx.enter_context(nc.semaphore(f"ln{L}_{n}"))

        def cols(q):
            return slice(q * QUAD, (q + 1) * QUAD)

        def per_graph(t, q):
            return t[:, cols(q)].unsqueeze(2).to_broadcast([128, QUAD, 128])

        def per_quad(t):
            return t[:].unsqueeze(1).to_broadcast([128, QUAD, 128])

        def quad(t):
            return t.rearrange("p (b d) -> p b d", b=QUAD)

        def pipelined(stages, units=QUADS):
            for turn in range(units + len(stages) - 1):
                for n in reversed(range(len(stages))):
                    if 0 <= turn - n < units and stages[n]:
                        stages[n](turn - n)

        def pause(engine, passed):
            engine.sem_inc(sem[passed], 1)

        N_WEIGHTS = 21
        row_loads = [(g, t, ra, ca) for g in range(NG) for t in range(RG // GROUP_GRAPHS[g])
                     for ra in range(len(GROUP_RUNS[g])) for ca in range(len(GROUP_RUNS[g]))]
        block = ctx.enter_context(nc.Block())

        @block.sync
        def _(sp):
            def load_round(r):
                sp.wait_ge(sem["x_in_free"], r + 1)
                for b in range(0, RG, HALF):
                    sp.dma_start(x_in[:, b:b + HALF], x[bass.ds(r * RG + b, HALF)].rearrange("b n d -> n b d")
                                 ).then_inc(sem["x_loaded"], 16)
                sp.wait_ge(sem["adj_in_free"], 2 * r + 2)
                for b in range(0, RG, HALF):
                    sp.dma_start(adj_in[:, b:b + HALF], adj[bass.ds(r * RG + b, HALF)].rearrange("b n m -> n b m")
                                 ).then_inc(sem["adj_loaded"], 16)
                sp.wait_ge(sem["rows_free"], r + 1)
                for g, t, ra, ca in row_loads:
                    G, runs = GROUP_GRAPHS[g], GROUP_RUNS[g]
                    n0 = sum(b - a for a, b in runs[:ra])
                    m0 = sum(b - a for a, b in runs[:ca])
                    (na, nb), (ma, mb) = runs[ra], runs[ca]
                    sp.dma_start(rows[g][n0 * G:(n0 + nb - na) * G, t, m0:m0 + mb - ma],
                                 adj[bass.ds(r * RG + t * G, G), na:nb, ma:mb].rearrange("b n m -> n b m")
                                 ).then_inc(sem["rows_loaded"], 16)

            def store_round(r):
                for q in range(QUADS):
                    sp.wait_ge(sem["out_ready"], r * QUADS + q + 1)
                    sp.dma_start(out[bass.ds(r * RG + q * QUAD, QUAD)].rearrange("b n d -> n b d"),
                                 x_res[:, cols(q), :]).then_inc(sem["stored"], 16)

            for b in range(0, RG, HALF):
                sp.dma_start(x_in[:, b:b + HALF], x[b:b + HALF].rearrange("b n d -> n b d")).then_inc(sem["x_loaded"], 16)
            w = sem["weights_loaded"]
            sp.dma_start(conv_nat[:], conv_w.rearrange("l d e -> d l e")).then_inc(w, 16)
            sp.dma_start(wih_nat[:], w_ih.rearrange("(g c) e -> c g e", g=3)).then_inc(w, 16)
            sp.dma_start(whh_nat[:], w_hh.rearrange("(g c) e -> c g e", g=3)).then_inc(w, 16)
            sp.dma_start(w3_nat[:], W3).then_inc(w, 16)
            sp.dma_start(mask_nat[:], nodemask).then_inc(w, 16)
            sp.dma_start(bih[:], b_ih.rearrange("(g c) -> c g", g=3)).then_inc(w, 16)
            sp.dma_start(bhh[:], b_hh.rearrange("(g c) -> c g", g=3)).then_inc(w, 16)
            for b in range(0, RG, HALF):
                sp.dma_start(adj_in[:, b:b + HALF], adj[b:b + HALF].rearrange("b n m -> n b m")).then_inc(sem["adj_loaded"], 16)
            for i, t in enumerate((theta, W_h, W_t)):
                sp.dma_start(wl1[:, i * 128:(i + 1) * 128], t).then_inc(w, 16)
            sp.dma_start(bt_bc[:], b_t.partition_broadcast(128)).then_inc(w, 16)
            sp.dma_start(b3_bc[:], b3.partition_broadcast(128)).then_inc(w, 16)
            sp.dma_start(fw[:], fusion_w.partition_broadcast(128)).then_inc(w, 16)
            sp.dma_start(w1_sb[:], W1.rearrange("g d e -> d g e")).then_inc(w, 16)
            for g in range(NG):
                sp.dma_start(w2_sb[:, g], W2[g].rearrange("(k e) d -> e k d", k=EH)).then_inc(w, 16)
            sp.dma_start(b2_sb[:], b2.rearrange("g d -> d g")).then_inc(w, 16)
            sp.dma_start(b1_sb[:], b1.rearrange("g (k e) -> e g k", k=EH)).then_inc(w, 16)
            for g, t, ra, ca in row_loads:
                G, runs = GROUP_GRAPHS[g], GROUP_RUNS[g]
                n0 = sum(b - a for a, b in runs[:ra])
                m0 = sum(b - a for a, b in runs[:ca])
                (na, nb), (ma, mb) = runs[ra], runs[ca]
                sp.dma_start(rows[g][n0 * G:(n0 + nb - na) * G, t, m0:m0 + mb - ma],
                             adj[t * G:(t + 1) * G, na:nb, ma:mb].rearrange("b n m -> n b m")
                             ).then_inc(sem["rows_loaded"], 16)
            with sp.Fori(0, ROUNDS - 1) as r:
                load_round(r + 1)
                store_round(r)
            store_round(ROUNDS - 1)
            sp.wait_ge(sem["stored"], 16 + 16 * QUADS * ROUNDS)

        @block.tensor
        def _(pe):
            pe.wait_ge(sem["consts"], 1)
            pe.wait_ge(sem["weights_loaded"], 16 * N_WEIGHTS)
            for i in range(3):
                nc.tensor.transpose(bank[2][:, i * 128:(i + 1) * 128], wih_nat[:, i, :], ident[:])
            for i in range(3):
                nc.tensor.transpose(bank[3][:, i * 128:(i + 1) * 128], whh_nat[:, i, :], ident[:])
            for i in range(4):
                nc.tensor.transpose(bank[4][:, i * 128:(i + 1) * 128], conv_nat[:, i, :], ident[:])
            nc.tensor.transpose(bank[5][:, 0:128], conv_nat[:, 4, :], ident[:])
            nc.tensor.transpose(bank[5][:, 128:256], w3_nat[:], ident[:])
            nc.tensor.transpose(bank[5][:, 256:256 + B], mask_nat[:], ident[0:B, 0:B]).then_inc(sem["w_turned"], 1)
            pe.wait_ge(sem["w_turned_read"], 1)
            for l in range(LAYERS):
                fold = nc.tensor.matmul(bank[(0, 1, 6, 7, 2)[l]][:, 0:384], convT[:, l, :],
                                        wihT[:, :, :].rearrange("e g c -> e (g c)"), start=True, stop=True)
            fold.then_inc(sem["wc_made"], 1)
            pe.wait_ge(sem["setup_done"], 1)

            with pe.Fori(0, ROUNDS) as r:
                quads = pe.snap(r * QUADS)
                pe.wait_ge(sem["adj_loaded"], r * 32 + 32)
                for q in range(QUADS):
                    for j in range(QUAD):
                        last = nc.tensor.transpose(bank[2 + q][:, j * 128:(j + 1) * 128],
                                                   adj_in[:, q * QUAD + j, :], ident[:])
                    last.then_inc(sem["adj_turned"], 1)
                pe.wait_ge(sem["adj_turned"], quads + QUADS)
                pe.sem_inc(sem["adj_in_free"], 1)

                def turn_norm(L, q, dst):
                    pe.wait_ge(sem[f"ln{L}_xn"], quads + q + 1)
                    for j in range(QUAD):
                        last = nc.tensor.transpose(dst[:, j * 128:(j + 1) * 128], xn[:, q * QUAD + j, :], ident[:])
                    last.then_inc(sem[f"ln{L}_turned"], 1)

                for q in range(QUADS):
                    turn_norm(0, q, (A_BANK, B_BANK, T_BANK, G_BANK)[q])

                def turn_h(new, s):
                    pe.wait_ge(sem["h_new"], new)
                    for j in range(QUAD):
                        last = nc.tensor.transpose(T_BANK[:, j * 128:(j + 1) * 128], h[s][:, j * 128:(j + 1) * 128], ident[:])
                    last.then_inc(sem["h_turned"], 1)

                def aggregate(step, s):
                    pe.wait_ge(sem["hn_ready"], step + 1)
                    for j in range(QUAD):
                        last = nc.tensor.matmul(G_BANK[:, j * 128:(j + 1) * 128], hn[s % 2][:, j, :],
                                                edge[:, s * QUAD + j, :], start=True, stop=True)
                    last.then_inc(sem["g_made"], 1)

                def split_matmul(dst, w_hi, w_lo, m_hi, m_lo, start, stop):
                    nc.tensor.matmul(dst[:], w_hi, m_hi, start=start, stop=False)
                    nc.tensor.matmul(dst[:], w_lo, m_hi, start=False, stop=False)
                    return nc.tensor.matmul(dst[:], w_hi, m_lo, start=False, stop=stop)

                def step_of(steps, new, s, weights, following=True):
                    if following:
                        turn_h(new + s + 2, (s + 1) % QUADS)
                    pe.wait_ge(sem["h_lo_new"], steps + s + 1)
                    pe.wait_ge(sem["hb_ready"], steps + s + 1)
                    split_matmul(H_BANK, whh_hi[:, 2, :], whh_lo[:, 2, :], h_hi[s][:], h_lo[s][:], True, True).then_inc(sem["gates_h"], 1)
                    pe.wait_ge(sem["r_ready"], steps + s + 1)
                    split_matmul(R_BANK, whh_hi[:, 0, :], whh_lo[:, 0, :], h_hi[s][:], h_lo[s][:], True, False)
                    pe.wait_ge(sem["z_ready"], steps + s + 1)
                    split_matmul(Z_BANK, whh_hi[:, 1, :], whh_lo[:, 1, :], h_hi[s][:], h_lo[s][:], True, False)
                    pe.wait_ge(sem["g_lo_ready"], steps + s + 1)
                    if following:
                        aggregate(steps + s + 1, (s + 1) % QUADS)
                    if s % 2 == 0:
                        pe.wait_ge(sem["wA" if s == 0 else "wB"], weights)
                    ch, cl = wcur_hi[s // 2], wcur_lo[s // 2]
                    k = s % 2
                    split_matmul(R_BANK, ch[:, 0:128], cl[:, 0:128], g_hi[k][:], g_lo[k][:], False, True).then_inc(sem["gates_r"], 1)
                    pe.wait_ge(sem["pre_ready"], steps + s + 1)
                    split_matmul(I_BANK, ch[:, 256:384], cl[:, 256:384], g_hi[k][:], g_lo[k][:], True, True).then_inc(sem["gates_n"], 1)
                    split_matmul(Z_BANK, ch[:, 128:256], cl[:, 128:256], g_hi[k][:], g_lo[k][:], False, True).then_inc(sem["gates_z"], 1)

                pe.wait_ge(sem["h_new"], r * PRODUCED + QUADS)
                pe.wait_ge(sem["adjT_ready"], quads + QUADS)
                pe.wait_ge(sem["edge_ready"], quads + QUADS)
                turn_h(r * PRODUCED + 1, 0)
                aggregate(r * STEPS, 0)
                with pe.Fori(0, LAYERS - 1) as l:
                    steps = pe.snap(r * STEPS + l * QUADS)
                    new = pe.snap(r * PRODUCED + l * QUADS)
                    wl = pe.snap(r * LAYERS + l + 1)
                    for s in range(QUADS):
                        step_of(steps, new, s, wl)
                steps = pe.snap(r * STEPS + (STEPS - QUADS))
                new = pe.snap(r * PRODUCED + (STEPS - QUADS))
                for s in range(QUADS):
                    step_of(steps, new, s, r * LAYERS + LAYERS, following=s + 1 < QUADS)

                pe.wait_ge(sem["r_ready"], r * STEPS + STEPS + 1)
                pe.wait_ge(sem["z_ready"], r * STEPS + STEPS + 1)
                pe.wait_ge(sem["pre_ready"], r * STEPS + STEPS + 1)
                pe.wait_ge(sem["hb_ready"], r * STEPS + STEPS + 1)
                pe.wait_ge(sem["blocks_ready"], r + 1)
                for k, (g, b0, G, n) in enumerate(TILES):
                    last = nc.tensor.transpose(bank[2 + k // 4][0:n, (k % 4) * 128:(k % 4) * 128 + n],
                                               blocks[0:n, k, 0:n], ident[0:n, 0:n])
                last.then_inc(sem["blocks_turned"], 1)

                def turn_out(q):
                    pe.wait_ge(sem["h_new"], r * PRODUCED + STEPS + q + 1)
                    for j in range(QUAD):
                        last = nc.tensor.transpose((A_BANK, B_BANK)[q % 2][:, j * 128:(j + 1) * 128],
                                                   h[q][:, j * 128:(j + 1) * 128], ident[:])
                    last.then_inc(sem["l1_turned"], 1)

                def l1_linear(q):
                    pe.wait_ge(sem["ln1_h"], quads + q + 1)
                    if q == 0:
                        pe.wait_ge(sem["normT_ready"], r + 1)
                    else:
                        pe.wait_ge(sem["l1_f_het"], quads + q)
                    for j in range(QUAD):
                        last = nc.tensor.matmul(quad_bank[:, j, 0:384], hT[:, q * QUAD + j, :], wl1[:],
                                                start=True, stop=True)
                    last.then_inc(sem["l1_lin"], 1)

                def l1_aggregate(q):
                    pe.wait_ge(sem["l1_f_hom"], quads + q + 1)
                    for j in range(QUAD):
                        last = nc.tensor.matmul(G_BANK[:, j * 128:(j + 1) * 128], adjT[:, q * QUAD + j, :],
                                                f_hom[:, q % 2, j * 128:(j + 1) * 128], start=True, stop=True)
                    last.then_inc(sem["l1_agg"], 1)

                pipelined([turn_out, lambda q: turn_norm(1, q, T_BANK), l1_linear, l1_aggregate])

                for q in range(QUADS):
                    pe.wait_ge(sem["ln2_xn"], quads + q + 1)
                    pause(pe, "pe_passed")
                    for j in range(QUAD):
                        b = q * QUAD + j
                        last = nc.tensor.transpose(T_BANK[:, b * ZONE:(b + 1) * ZONE], xn[0:ZONE, b, :],
                                                   ident[0:ZONE, 0:ZONE])
                last.then_inc(sem["zone_turned"], 1)
                tiles = pe.snap(r * NT)

                def l2_support(k):
                    g, b0, G, n = TILES[k]
                    if k == 0:
                        pe.wait_ge(sem["packed_ready"], r + 1)
                    nc.tensor.matmul(R_BANK[0:n, 0:E], packed[:, k, 0:n], w1_sb[:, g, :],
                                     start=True, stop=True).then_inc(sem["l2_sup1"], 1)

                def l2_hidden(k):
                    g, b0, G, n = TILES[k]
                    pe.wait_ge(sem["l2_sup1_read"], tiles + k + 1)
                    for e in range(EH):
                        last = nc.tensor.matmul(Z_BANK[:, e * 128:e * 128 + n], sup1[0:n, k % 2, e * 128:(e + 1) * 128],
                                                normT[0:n, k, 0:n], start=True, stop=True)
                    last.then_inc(sem["l2_hid"], 1)

                def l2_support2(k):
                    g, b0, G, n = TILES[k]
                    pe.wait_ge(sem["l2_hid_read"], tiles + k + 1)
                    for e in range(EH):
                        last = nc.tensor.matmul(H_BANK[0:n, 0:128], hid[:, k % 2, e, 0:n], w2_sb[:, g, e, :],
                                                start=(e == 0), stop=(e == EH - 1))
                    last.then_inc(sem["l2_sup2"], 1)

                def l2_conv2(k):
                    g, b0, G, n = TILES[k]
                    pe.wait_ge(sem["l2_sup2_read"], tiles + k + 1)
                    if k:
                        pe.wait_ge(sem["l2_conv2_read"], tiles + k)
                    nc.tensor.matmul(I_BANK[:, 0:n], sup2[0:n, k % 2, :], normT[0:n, k, 0:n],
                                     start=True, stop=True).then_inc(sem["l2_conv2"], 1)

                pipelined([l2_support, l2_hidden, l2_support2, l2_conv2], NT)
                pe.wait_ge(sem["l2_added"], tiles + NT)
                for q in range(QUADS):
                    if q >= 2:
                        pe.wait_ge(sem["l2_out"], quads + q - 1)
                    for j in range(QUAD):
                        last = nc.tensor.transpose((A_BANK, B_BANK)[q % 2][0:ZONE, j * 128:(j + 1) * 128],
                                                   fused[:, :, q * QUAD + j], ident[:])
                    last.then_inc(sem["l2_back"], 1)

                def l3_linear(q):
                    pe.wait_ge(sem["ln3_h"], quads + q + 1)
                    for j in range(QUAD):
                        last = nc.tensor.matmul(G_BANK[:, j * 128:(j + 1) * 128], hT[:, q * QUAD + j, :], w3T[:],
                                                start=True, stop=True)
                    last.then_inc(sem["l3_lin"], 1)

                def l3_aggregate(q):
                    pe.wait_ge(sem["l3_y"], quads + q + 1)
                    if q >= 2:
                        pe.wait_ge(sem["out_ready"], quads + q - 1)
                    for j in range(QUAD):
                        last = nc.tensor.matmul((R_BANK, Z_BANK)[q % 2][:, j * 128:(j + 1) * 128],
                                                adjTI[:, q * QUAD + j, :], y[q % 2][:, j * 128:(j + 1) * 128],
                                                start=True, stop=True)
                    last.then_inc(sem["l3_agg"], 1)

                pe.wait_ge(sem["adjTI_ready"], quads + QUADS)
                pipelined([None, lambda q: turn_norm(3, q, T_BANK), l3_linear, l3_aggregate])
                pe.wait_ge(sem["out_ready"], quads + QUADS)

        @block.scalar
        def _(act):
            act.wait_ge(sem["dve_setup"], 1)
            nc.scalar.activation(fexp[:], fw[:], ACT.Exp, bias=fmax[:]).then_inc(sem["fexp_done"], 1)
            with act.Fori(0, ROUNDS) as r:
                quads = act.snap(r * QUADS)
                for q in range(QUADS):
                    act.wait_ge(sem["adj_turned"], quads + q + 1)
                    nc.scalar.activation(adjT[:, cols(q), :], quad(bank[2 + q]), ACT.Copy).then_inc(sem["adjT_ready"], 1)
                for q in range(QUADS):
                    src = (A_BANK, B_BANK, T_BANK, G_BANK)[q]
                    act.wait_ge(sem["ln0_turned"], quads + q + 1)
                    nc.scalar.activation(h[q][:], src[:], ACT.Relu).then_inc(sem["h_new"], 1)

                def turned_h(step, s):
                    act.wait_ge(sem["h_turned"], step + 1)
                    nc.scalar.activation(hn[s % 2][:], quad(T_BANK[:, :]), ACT.Copy).then_inc(sem["hn_ready"], 1)

                def aggregate_hi(step, s):
                    act.wait_ge(sem["g_made"], step + 1)
                    nc.scalar.activation(g_hi[s % 2][:], G_BANK[:], ACT.Copy).then_inc(sem["g_hi_ready"], 1)

                def step_of(steps, s, following=True):
                    k = s % 2
                    if following:
                        turned_h(steps + s + 1, (s + 1) % QUADS)
                    act.wait_ge(sem["gates_h"], steps + s + 1)
                    nc.scalar.activation(rh[k][:], H_BANK[:], ACT.Identity, bias=bhh[:, 2:3]).then_inc(sem["hb_ready"], 1)
                    if following:
                        aggregate_hi(steps + s + 1, (s + 1) % QUADS)
                    act.wait_ge(sem["gates_r"], steps + s + 1)
                    nc.scalar.activation(gr[k][:], R_BANK[:], ACT.Tanh, bias=brz[:, 0:1], scale=0.5).then_inc(sem["r_ready"], 1)
                    act.wait_ge(sem["gates_z"], steps + s + 1)
                    nc.scalar.activation(gz[k][:], Z_BANK[:], ACT.Tanh, bias=brz[:, 1:2], scale=0.5).then_inc(sem["z_ready"], 1)
                    act.wait_ge(sem["pre_ready"], steps + s + 2)
                    nc.scalar.activation(gn[k][:], pre[k][:], ACT.Tanh, bias=bih[:, 2:3]).then_inc(sem["n_ready"], 1)

                turned_h(r * STEPS, 0)
                aggregate_hi(r * STEPS, 0)
                with act.Fori(0, LAYERS - 1) as l:
                    steps = act.snap(r * STEPS + l * QUADS)
                    for s in range(QUADS):
                        step_of(steps, s)
                steps = act.snap(r * STEPS + (STEPS - QUADS))
                for s in range(QUADS):
                    step_of(steps, s, following=s + 1 < QUADS)

                act.wait_ge(sem["blocks_turned"], r + 1)
                for k, (g, b0, G, n) in enumerate(TILES):
                    last = nc.scalar.activation(normT[0:n, k, 0:n], bank[2 + k // 4][0:n, (k % 4) * 128:(k % 4) * 128 + n],
                                                ACT.Copy, scale=dinv[0:n, k:k + 1])
                last.then_inc(sem["normT_ready"], 1)

                def relu_norm(L, q):
                    act.wait_ge(sem[f"ln{L}_turned"], quads + q + 1)
                    nc.scalar.activation(hT[:, cols(q), :], quad(T_BANK[:, :]), ACT.Relu).then_inc(sem[f"ln{L}_h"], 1)

                def l1_het_and_gate(q):
                    k = q % 2
                    act.wait_ge(sem["l1_f_hom"], quads + q + 1)
                    nc.scalar.activation(quad(f_het[:, k, :]), quad_bank[:, :, 128:256], ACT.Copy).then_inc(sem["l1_f_het"], 1)
                    nc.scalar.activation(gate_th[k][:], gate_pre[k][:], ACT.Tanh, scale=0.5).then_inc(sem["l1_gate"], 1)

                def l1_elu(q):
                    k = q % 2
                    act.wait_ge(sem["l1_mix"], quads + q + 1)
                    nc.scalar.activation(neg[k][:], mix[k][:], ACT.Relu, scale=-1.0).then_inc(sem["l1_neg"], 1)
                    act.wait_ge(sem["l1_neg"], quads + q + 1)
                    nc.scalar.activation(ex[k][:], quad(neg[k][:, :]), ACT.Exp, scale=-1.0).then_inc(sem["l1_exp"], 1)

                pipelined([None, lambda q: relu_norm(1, q), l1_het_and_gate, l1_elu])

                act.wait_ge(sem["zone_turned"], r + 1)
                zone = T_BANK[:, 0:RG * ZONE].rearrange("d (b n) -> d b n", b=RG)
                for g, G in enumerate(GROUP_GRAPHS):
                    for k in (k for k, t in enumerate(TILES) if t[0] == g):
                        b0, m0 = TILES[k][1], 0
                        for a, b in GROUP_RUNS[g]:
                            last = nc.scalar.activation(
                                packed[:, k, m0 * G:(m0 + b - a) * G].rearrange("d (n b) -> d n b", b=G),
                                zone[:, b0:b0 + G, a:b].rearrange("d b n -> d n b"), ACT.Relu)
                            m0 += b - a
                last.then_inc(sem["packed_ready"], 1)
                tiles = act.snap(r * NT)

                def read_support(k):
                    n = TILES[k][3]
                    act.wait_ge(sem["l2_sup1"], tiles + k + 1)
                    nc.scalar.activation(sup1[0:n, k % 2, :], R_BANK[0:n, 0:E], ACT.Copy).then_inc(sem["l2_sup1_read"], 1)

                def read_hidden(k):
                    g, b0, G, n = TILES[k]
                    act.wait_ge(sem["l2_hid"], tiles + k + 1)
                    for e in range(EH):
                        last = nc.scalar.activation(hid[:, k % 2, e, 0:n], Z_BANK[:, e * 128:e * 128 + n], ACT.Relu,
                                                    bias=b1_sb[:, g, e:e + 1])
                    last.then_inc(sem["l2_hid_read"], 1)

                pipelined([read_support, read_hidden], NT)
                pipelined([None, lambda q: relu_norm(3, q)])

        @block.gpsimd
        def _(pool):
            nc.gpsimd.memset(neg_half[:], -0.5)
            nc.gpsimd.memset(eps_ln[:], LN_EPS)
            nc.gpsimd.memset(eps_deg[:], 1e-6)
            nc.gpsimd.memset(deg2[:], 1.0)
            nc.gpsimd.memset(ident[:], 0.0).then_inc(sem["fused_zero"], 1)
            pool.wait_ge(sem["fused_zero"], 1)
            nc.gpsimd.affine_select(out=ident[:], in_=ident[:], compare_op=ALU.not_equal, fill=1.0, base=0,
                                    pattern=[[-1, 128]], channel_multiplier=1).then_inc(sem["consts"], 1)
            pool.wait_ge(sem["consts"], 1)
            pool.sem_inc(sem["x_in_free"], 1)
            pool.sem_inc(sem["adj_in_free"], 2)
            pool.sem_inc(sem["rows_free"], 1)
            pool.sem_inc(sem["stored"], 16)
            for n in ("hb_ready", "r_ready", "z_ready", "pre_ready"):
                pool.sem_inc(sem[n], 1)
            pool.wait_ge(sem["setup_done"], 1)

            def power(L, q):
                c = cols(q)
                pool.wait_ge(sem[f"ln{L}_mv"], quads + q + 1)
                nc.gpsimd.tensor_tensor(var_eps[:, c], mv[:, c, 1], eps_ln[:, c], ALU.add).then_inc(sem[f"ln{L}_var"], 1)
                pool.wait_ge(sem[f"ln{L}_var"], quads + q + 1)
                nc.gpsimd.tensor_tensor(rstd[:, c], var_eps[:, c], neg_half[:, c], ALU.pow).then_inc(sem[f"ln{L}_rstd"], 1)

            with pool.Fori(0, ROUNDS) as r:
                quads = pool.snap(r * QUADS)
                for q in range(QUADS):
                    power(0, q)
                def low_half(new, s):
                    pool.wait_ge(sem["h_hi_new"], new + 1)
                    nc.gpsimd.tensor_tensor(h_lo[s][:], h[s][:], h_hi[s][:].bitcast(f32), ALU.subtract).then_inc(sem["h_lo_new"], 1)

                for s in range(QUADS):
                    low_half(r * STEPS + s, s)
                with pool.Fori(0, LAYERS - 1) as l:
                    new = pool.snap(r * STEPS + l * QUADS)
                    for s in range(QUADS):
                        low_half(new + QUADS + s, s)
                nc.gpsimd.tensor_copy(mask_r[:], mask_all[:, bass.ds(r * RG, RG)]).then_inc(sem["mask_round"], 1)
                for q in range(QUADS):
                    pool.wait_ge(sem["adjT_ready"], quads + q + 1)
                    nc.gpsimd.tensor_tensor(adjTI[:, cols(q), :], adjT[:, cols(q), :],
                                            per_quad(ident),
                                            ALU.add).then_inc(sem["adjTI_ready"], 1)
                pool.wait_ge(sem["degs"], r + 1)
                nc.gpsimd.tensor_tensor(degs1[:], deg1[:], eps_deg[:], ALU.add)
                nc.gpsimd.tensor_scalar(degs3[:], deg3[:], 1.0, 1e-8, ALU.add, ALU.add).then_inc(sem["degs_eps"], 1)
                pool.wait_ge(sem["group_safe"], r + 1)
                nc.gpsimd.tensor_tensor(deg_pow[:], deg_safe[:], neg_half[:, 0:NT], ALU.pow).then_inc(sem["group_pow"], 1)
                pool.wait_ge(sem["degs_eps"], r + 1)
                nc.gpsimd.tensor_tensor(norm1[:], degs1[:], neg_half[:], ALU.pow)
                nc.gpsimd.tensor_tensor(dis[:], degs3[:], neg_half[:], ALU.pow).then_inc(sem["norms"], 1)
                pool.wait_ge(sem["norms"], 2 * r + 1)
                pool.wait_ge(sem["mask_round"], r + 1)
                nc.gpsimd.tensor_tensor(dis_mask[:], dis[:], mask_r[:], ALU.mult).then_inc(sem["norms"], 1)
                nc.gpsimd.memset(fused[:], 0.0).then_inc(sem["fused_zero"], 1)
                for q in range(QUADS):
                    power(1, q)
                for q in range(QUADS):
                    power(2, q)
                for q in range(QUADS):
                    power(3, q)

        @block.vector
        def _(dve):
            dve.wait_ge(sem["weights_loaded"], 16 * N_WEIGHTS)
            dve.wait_ge(sem["consts"], 1)
            nc.vector.tensor_reduce(out=fmax[:], in_=fw[:], op=ALU.max, axis=AX.X, negate=True).then_inc(sem["dve_setup"], 1)
            nc.vector.tensor_tensor(brz2[:], bih[:, 0:2], bhh[:, 0:2], ALU.add).then_inc(sem["dve_setup"], 1)
            for g, G in enumerate(GROUP_GRAPHS):
                n = G * SIZE[g]
                nc.vector.tensor_reduce(out=gmask[g][0:n, :], in_=ident[0:n, 0:n].rearrange("p (m b) -> p b m", b=G),
                                        op=ALU.add, axis=AX.X)
            dve.wait_ge(sem["dve_setup"], 2)
            nc.vector.tensor_scalar(brz[:], brz2[:], 0.5, None, ALU.mult)
            dve.wait_ge(sem["w_turned"], 1)
            nc.vector.tensor_copy(wihT[:], bank[2][:, 0:384].rearrange("e (g c) -> e g c", g=3))
            nc.vector.tensor_copy(whh_hi[:], bank[3][:, 0:384].rearrange("e (g c) -> e g c", g=3)).then_inc(sem["dve_setup"], 1)
            nc.vector.tensor_copy(convT[:, 0:4, :], quad(bank[4]))
            nc.vector.tensor_copy(convT[:, 4, :], bank[5][:, 0:128])
            nc.vector.tensor_copy(w3T[:], bank[5][:, 128:256])
            nc.vector.tensor_copy(mask_all[:], bank[5][:, 256:256 + B])
            dve.wait_ge(sem["dve_setup"], 3)
            nc.vector.tensor_tensor(whh_lo[:], bank[3][:, 0:384].rearrange("e (g c) -> e g c", g=3),
                                    whh_hi[:].bitcast(f32), ALU.subtract).then_inc(sem["w_turned_read"], 1)
            dve.wait_ge(sem["fexp_done"], 1)
            nc.vector.reduce_sum(fsum[:], fexp[:], axis=AX.X).then_inc(sem["dve_setup"], 1)
            dve.wait_ge(sem["dve_setup"], 4)
            nc.vector.reciprocal(finv[:], fsum[:]).then_inc(sem["dve_setup"], 1)
            dve.wait_ge(sem["dve_setup"], 5)
            nc.vector.tensor_scalar(fshare[:], fexp[:], finv[:], None, ALU.mult)
            dve.wait_ge(sem["wc_made"], 1)
            for l in range(LAYERS):
                nc.vector.tensor_copy(wc_hi[:, l, :], bank[(0, 1, 6, 7, 2)[l]][:, 0:384]).then_inc(sem["dve_setup"], 1)
            for l in range(LAYERS):
                dve.wait_ge(sem["dve_setup"], 6 + l)
                last = nc.vector.tensor_tensor(wc_lo[:, l, :], bank[(0, 1, 6, 7, 2)[l]][:, 0:384],
                                               wc_hi[:, l, :].bitcast(f32), ALU.subtract)
            last.then_inc(sem["setup_done"], 1)

            with dve.Fori(0, ROUNDS) as r:
                quads = dve.snap(r * QUADS)

                def norm_stats(L, q, src, parts=128):
                    for j in range(QUAD):
                        last = nc.vector.bn_stats(stats[0:parts, q * QUAD + j, :], src[0:parts, q * QUAD + j, :])
                    last.then_inc(sem[f"ln{L}_stats"], 1)
                    dve.wait_ge(sem[f"ln{L}_stats"], quads + q + 1)
                    pause(dve, "dve_passed")
                    for j in range(QUAD):
                        last = nc.vector.bn_aggr(mv[0:parts, q * QUAD + j, :], stats[0:parts, q * QUAD + j, :])
                    last.then_inc(sem[f"ln{L}_mv"], 1)

                def normalise(L, q, src, parts=128):
                    dve.wait_ge(sem[f"ln{L}_rstd"], quads + q + 1)
                    for j in range(QUAD):
                        b = q * QUAD + j
                        last = nc.vector.tensor_scalar(xn[0:parts, b, :], src[0:parts, b, :], mv[0:parts, b, 0:1],
                                                       rstd[0:parts, b:b + 1], ALU.subtract, ALU.mult)
                    last.then_inc(sem[f"ln{L}_xn"], 1)

                def layer_weights(layer, which):
                    name = "wA" if which == 0 else "wB"
                    nc.vector.tensor_copy(wcur_hi[which][:], wc_hi[:, bass.ds(layer, 1), :].bitcast(f32).rearrange("p a c -> p (a c)"))
                    nc.vector.tensor_copy(wcur_lo[which][:], wc_lo[:, bass.ds(layer, 1), :].bitcast(f32).rearrange("p a c -> p (a c)")
                                          ).then_inc(sem[name], 1)

                dve.wait_ge(sem["x_loaded"], r * 32 + 32)
                for q in range(QUADS):
                    norm_stats(0, q, x_in)
                for q in range(QUADS):
                    normalise(0, q, x_in)

                def edges(q):
                    nc.vector.tensor_scalar(edge[:, cols(q), :], adj_in[:, cols(q), :], 0.0, None,
                                            ALU.not_equal).then_inc(sem["edge_ready"], 1)

                def split_h(new, s):
                    dve.wait_ge(sem["h_new"], new + 1)
                    nc.vector.tensor_copy(h_hi[s][:], h[s][:]).then_inc(sem["h_hi_new"], 1)

                dve.wait_ge(sem["adj_loaded"], r * 32 + 32)
                for q in range(QUADS):
                    edges(q)
                    split_h(r * PRODUCED + q, q)
                layer_weights(0, 0)

                def degrees():
                    nc.vector.tensor_reduce(out=deg1[:], in_=adj_in[:], op=ALU.add, axis=AX.X, apply_absolute_value=True)
                    nc.vector.tensor_reduce(out=deg3[:], in_=adj_in[:], op=ALU.add, axis=AX.X).then_inc(sem["degs"], 1)
                    dve.wait_ge(sem["degs"], r + 1)
                    dve.sem_inc(sem["adj_in_free"], 1)

                def group_degrees():
                    dve.wait_ge(sem["rows_loaded"], (r + 1) * (16 * len(row_loads)))
                    for k, (g, b0, G, n) in enumerate(TILES):
                        last = nc.vector.reduce_sum(deg2[0:n, k:k + 1], rows[g][0:n, b0 // G, :], axis=AX.X)
                    last.then_inc(sem["group_sum"], 1)
                    dve.wait_ge(sem["group_sum"], 3 * r + 1)
                    nc.vector.tensor_scalar(deg_zero[:], deg2[:], -1.0, None, ALU.is_equal)
                    nc.vector.tensor_scalar(deg_some[:], deg2[:], -1.0, None, ALU.not_equal).then_inc(sem["group_sum"], 1)
                    dve.wait_ge(sem["group_sum"], 3 * r + 2)
                    nc.vector.scalar_tensor_tensor(deg_safe[:], deg2[:], 1.0, deg_zero[:], ALU.add, ALU.add).then_inc(sem["group_safe"], 1)

                def group_norms():
                    dve.wait_ge(sem["group_pow"], r + 1)
                    nc.vector.tensor_tensor(dinv[:], deg_pow[:], deg_some[:], ALU.mult).then_inc(sem["group_sum"], 1)

                def group_blocks():
                    dve.wait_ge(sem["group_sum"], 3 * r + 3)
                    for k, (g, b0, G, n) in enumerate(TILES):
                        m = SIZE[g]
                        last = nc.vector.scalar_tensor_tensor(
                            blocks0[0:n, k, 0:n].rearrange("p (m b) -> p m b", b=G),
                            rows[g][0:n, b0 // G, :].unsqueeze(2).to_broadcast([n, m, G]), dinv[0:n, k:k + 1],
                            gmask[g][0:n, :].unsqueeze(1).to_broadcast([n, m, G]), ALU.mult, ALU.mult)
                    last.then_inc(sem["blocks_half"], 1)
                    dve.wait_ge(sem["blocks_half"], r + 1)
                    dve.sem_inc(sem["rows_free"], 1)
                    for k, (g, b0, G, n) in enumerate(TILES):
                        last = nc.vector.scalar_tensor_tensor(blocks[0:n, k, 0:n], ident[0:n, 0:n], dinv[0:n, k:k + 1],
                                                              blocks0[0:n, k, 0:n], ALU.mult, ALU.add)
                    last.then_inc(sem["blocks_ready"], 1)

                adjacency_steps = [degrees, group_degrees, group_norms, group_blocks]

                def aggregate_lo(step, s):
                    dve.wait_ge(sem["g_hi_ready"], step + 1)
                    nc.vector.tensor_tensor(g_lo[s % 2][:], G_BANK[:], g_hi[s % 2][:].bitcast(f32),
                                            ALU.subtract).then_inc(sem["g_lo_ready"], 1)

                def step_of(steps, new, s, layer, following=True, last_layer=False):
                    k = s % 2
                    dve.wait_ge(sem["hb_ready"], steps + s + 2)
                    dve.wait_ge(sem["r_ready"], steps + s + 2)
                    nc.vector.scalar_tensor_tensor(rh[k][:], gr[k][:], 1.0, rh[k][:], ALU.add, ALU.mult
                                                   ).then_inc(sem["rh_ready"], 1)
                    dve.wait_ge(sem["rh_ready"], steps + s + 1)
                    dve.wait_ge(sem["gates_n"], steps + s + 1)
                    nc.vector.scalar_tensor_tensor(pre[k][:], rh[k][:], 0.5, I_BANK[:], ALU.mult, ALU.add
                                                   ).then_inc(sem["pre_ready"], 1)
                    if following:
                        aggregate_lo(steps + s + 1, (s + 1) % QUADS)
                    if s == 1:
                        layer_weights(layer, 1)
                    if s == 3 and not last_layer:
                        layer_weights(layer + 1, 0)
                    dve.wait_ge(sem["n_ready"], steps + s + 1)
                    nc.vector.tensor_tensor(hd[k][:], h[s][:], gn[k][:], ALU.subtract).then_inc(sem["hd_ready"], 1)
                    dve.wait_ge(sem["hd_ready"], steps + s + 1)
                    dve.wait_ge(sem["z_ready"], steps + s + 2)
                    nc.vector.scalar_tensor_tensor(zd[k][:], gz[k][:], 1.0, hd[k][:], ALU.add, ALU.mult).then_inc(sem["zd_ready"], 1)
                    dve.wait_ge(sem["zd_ready"], steps + s + 1)
                    nc.vector.scalar_tensor_tensor(h[s][:], zd[k][:], 0.5, gn[k][:], ALU.mult, ALU.add).then_inc(sem["h_new"], 1)
                    if last_layer:
                        adjacency_steps[s]()
                    else:
                        split_h(new + QUADS + s, s)

                aggregate_lo(r * STEPS, 0)
                with dve.Fori(0, LAYERS - 1) as l:
                    steps = dve.snap(r * STEPS + l * QUADS)
                    new = dve.snap(r * PRODUCED + l * QUADS)
                    for s in range(QUADS):
                        step_of(steps, new, s, l)
                steps = dve.snap(r * STEPS + (STEPS - QUADS))
                new = dve.snap(r * PRODUCED + (STEPS - QUADS))
                for s in range(QUADS):
                    step_of(steps, new, s, LAYERS - 1, following=s + 1 < QUADS, last_layer=True)

                def l1_residual(q):
                    if q == 0:
                        dve.wait_ge(sem["mask_round"], r + 1)
                        dve.wait_ge(sem["stored"], r * (16 * QUADS) + 16)
                        dve.wait_ge(sem["norms"], 2 * r + 2)
                    dve.wait_ge(sem["l1_turned"], quads + q + 1)
                    src = (A_BANK, B_BANK)[q % 2]
                    for j in range(QUAD):
                        b = q * QUAD + j
                        last = nc.vector.scalar_tensor_tensor(x_res[:, b, :], src[:, j * 128:(j + 1) * 128],
                                                              mask_r[:, b:b + 1], x_in[:, b, :], ALU.mult, ALU.add)
                    last.then_inc(sem["l1_x"], 1)
                    dve.wait_ge(sem["l1_x"], quads + q + 1)
                    if q == QUADS - 1:
                        dve.sem_inc(sem["x_in_free"], 1)
                    norm_stats(1, q, x_res)

                def l1_split(q):
                    k = q % 2
                    dve.wait_ge(sem["l1_lin"], quads + q + 1)
                    nc.vector.tensor_tensor(quad(gate_pre[k][:, :]), quad_bank[:, :, 256:384], per_quad(bt_bc), ALU.add)
                    nc.vector.tensor_tensor(quad(f_hom[:, k, :]), quad_bank[:, :, 0:128], per_graph(norm1, q),
                                            ALU.mult).then_inc(sem["l1_f_hom"], 1)

                def l1_gate(q):
                    k = q % 2
                    dve.wait_ge(sem["l1_agg"], quads + q + 1)
                    nc.vector.tensor_tensor(quad(agg_n[k][:, :]), quad(G_BANK[:, :]), per_graph(norm1, q),
                                            ALU.mult).then_inc(sem["l1_agg_n"], 1)
                    dve.wait_ge(sem["l1_agg_n"], quads + q + 1)
                    dve.wait_ge(sem["l1_gate"], quads + q + 1)
                    nc.vector.tensor_tensor(diff[k][:], agg_n[k][:], f_het[:, k, :], ALU.subtract).then_inc(sem["l1_diff"], 1)
                    dve.wait_ge(sem["l1_diff"], quads + q + 1)
                    nc.vector.scalar_tensor_tensor(gated[k][:], gate_th[k][:], 1.0, diff[k][:], ALU.add, ALU.mult
                                                   ).then_inc(sem["l1_gated"], 1)
                    dve.wait_ge(sem["l1_gated"], quads + q + 1)
                    nc.vector.scalar_tensor_tensor(mix[k][:], gated[k][:], 0.5, f_het[:, k, :], ALU.mult, ALU.add
                                                   ).then_inc(sem["l1_mix"], 1)

                def l1_finish(q):
                    k = q % 2
                    dve.wait_ge(sem["l1_exp"], quads + q + 1)
                    nc.vector.scalar_tensor_tensor(gated[k][:], mix[k][:], 0.0, ex[k][:, :, :].rearrange("p b d -> p (b d)"),
                                                   ALU.max, ALU.add).then_inc(sem["l1_elu"], 1)
                    dve.wait_ge(sem["l1_elu"], quads + q + 1)
                    nc.vector.scalar_tensor_tensor(x_res[:, cols(q), :], quad(gated[k][:, :]), -1.0, x_res[:, cols(q), :],
                                                   ALU.add, ALU.add).then_inc(sem["l1_out"], 1)
                    dve.wait_ge(sem["l1_out"], quads + q + 1)
                    norm_stats(2, q, x_res, ZONE)

                pipelined([l1_residual, lambda q: normalise(1, q, x_res), l1_split, l1_gate, l1_finish])
                for q in range(QUADS):
                    normalise(2, q, x_res, ZONE)

                tiles = dve.snap(r * NT)
                dve.wait_ge(sem["fused_zero"], r + 2)

                def read_support2(k):
                    n = TILES[k][3]
                    dve.wait_ge(sem["l2_sup2"], tiles + k + 1)
                    nc.vector.tensor_copy(sup2[0:n, k % 2, :], H_BANK[0:n, 0:128]).then_inc(sem["l2_sup2_read"], 1)

                def add_group(k):
                    g, b0, G, n = TILES[k]
                    dve.wait_ge(sem["l2_conv2"], tiles + k + 1)
                    nc.vector.tensor_scalar(conv2[:, k % 2, 0:n], I_BANK[:, 0:n], b2_sb[:, g:g + 1], 0.0,
                                            ALU.add, ALU.max).then_inc(sem["l2_conv2_read"], 1)
                    dve.wait_ge(sem["l2_conv2_read"], tiles + k + 1)
                    if k:
                        dve.wait_ge(sem["l2_added"], tiles + k)
                    m0 = 0
                    for a, b in GROUP_RUNS[g]:
                        dst = fused[:, a:b, b0:b0 + G]
                        last = nc.vector.scalar_tensor_tensor(
                            dst, conv2[:, k % 2, m0 * G:(m0 + b - a) * G].rearrange("d (n b) -> d n b", b=G),
                            fshare[:, g:g + 1], dst, ALU.mult, ALU.add)
                        m0 += b - a
                    last.then_inc(sem["l2_added"], 1)

                pipelined([read_support2, add_group], NT)

                def l2_residual(q):
                    dve.wait_ge(sem["l2_back"], quads + q + 1)
                    nc.vector.tensor_tensor(x_res[0:ZONE, cols(q), :], quad((A_BANK, B_BANK)[q % 2][:, :])[0:ZONE],
                                            x_res[0:ZONE, cols(q), :], ALU.add).then_inc(sem["l2_out"], 1)
                    dve.wait_ge(sem["l2_out"], quads + q + 1)
                    norm_stats(3, q, x_res)

                def l3_scale(q):
                    k = q % 2
                    dve.wait_ge(sem["l3_lin"], quads + q + 1)
                    nc.vector.tensor_tensor(quad(y0[k][:, :]), quad(G_BANK[:, :]), per_quad(b3_bc), ALU.add).then_inc(sem["l3_bias"], 1)
                    dve.wait_ge(sem["l3_bias"], quads + q + 1)
                    nc.vector.tensor_tensor(quad(y[k][:, :]), quad(y0[k][:, :]), per_graph(dis, q), ALU.mult).then_inc(sem["l3_y"], 1)

                def l3_finish(q):
                    k = q % 2
                    dve.wait_ge(sem["l3_agg"], quads + q + 1)
                    nc.vector.tensor_tensor(quad(rh[k][:, :]), quad((R_BANK, Z_BANK)[k][:, :]), per_graph(dis_mask, q),
                                            ALU.mult).then_inc(sem["l3_scaled"], 1)
                    dve.wait_ge(sem["l3_scaled"], quads + q + 1)
                    nc.vector.scalar_tensor_tensor(x_res[:, cols(q), :], quad(rh[k][:, :]), 0.0, x_res[:, cols(q), :],
                                                   ALU.max, ALU.add).then_inc(sem["out_ready"], 1)

                pipelined([l2_residual, lambda q: normalise(3, q, x_res), l3_scale, l3_finish])


_INS = ['x', 'adj', 'nodemask', 'L0_gnn_weight', 'L0_gnn_w_ih', 'L0_gnn_w_hh', 'L0_gnn_b_ih', 'L0_gnn_b_hh',
        'L1_gnn_theta', 'L1_gnn_W_h', 'L1_gnn_W_t', 'L1_gnn_b_t', 'L2_gnn_W1', 'L2_gnn_b1', 'L2_gnn_W2',
        'L2_gnn_b2', 'L2_gnn_fusion_w', 'L3_gnn_W', 'L3_gnn_b']


def kernel(**inputs):
    import numpy as np
    import concourse.bacc as bacc
    from concourse.bass_utils import run_bass_kernel_spmd

    nc = bacc.Bacc("TRN2", target_bir_lowering=False, num_devices=1)
    arrays, args = {}, []
    for name in _INS:
        a = np.ascontiguousarray(inputs[name])
        arrays[f"in_{name}"] = a
        args.append(nc.dram_tensor(f"in_{name}", a.shape, mybir.dt.from_np(a.dtype), kind="ExternalInput").ap())
    shape = tuple(inputs["x"].shape)
    args.append(nc.dram_tensor("out_x", shape, mybir.dt.float32, kind="ExternalOutput").ap())
    graph_stack(nc, *args)
    result = run_bass_kernel_spmd(nc, [arrays], core_ids=[0])
    return result.results[0]["out_x"]
```

```python
import concourse.bass as bass
from concourse import mybir
from contextlib import ExitStack

LN_EPS = 1e-5
QUAD = 4
QUADS = 4
LAYERS = 5
GROUP_RUNS = [[(0, 25)], [(0, 9)], [(0, 1), (9, 15)], [(6, 9), (12, 15)], [(3, 6), (9, 12)]]
GROUP_GRAPHS = [4, 8, 16, 16, 16]
ZONE = 25


def graph_stack(nc, x, adj, nodemask, conv_w, w_ih, w_hh, b_ih, b_hh, theta, W_h, W_t, b_t,
                W1, b1, W2, b2, fusion_w, W3, b3, out):
    f32, f32r = mybir.dt.float32, mybir.dt.float32r
    ALU, ACT, AX = mybir.AluOpType, mybir.ActivationFunctionType, mybir.AxisListType
    B, N, D = x.shape
    RG = QUAD * QUADS
    HALF = RG // 2
    ROUNDS = B // RG
    STEPS = LAYERS * QUADS
    PRODUCED = STEPS + QUADS
    E = W1.shape[2]
    EH = E // 128
    NG = len(GROUP_RUNS)
    SIZE = [sum(b - a for a, b in runs) for runs in GROUP_RUNS]
    TILES = [(g, t * G, G, G * SIZE[g]) for g, G in enumerate(GROUP_GRAPHS) for t in range(RG // G)]
    NT = len(TILES)

    ctx = ExitStack()
    with ctx:
        ctx.enter_context(nc.allow_non_contiguous_dma("small transposed loads at the start"))

        def sb(name, shape, dt=f32):
            return ctx.enter_context(nc.sbuf_tensor(name, shape, dt))

        ident = sb("ident", [128, 128])
        neg_half, neg_one, eps_ln, eps_deg = (sb(n, [128, RG]) for n in ("neg_half", "neg_one", "eps_ln", "eps_deg"))
        top_ones = sb("top_ones", [128, 128])
        gmask = [sb(f"gmask{g}", [128, GROUP_GRAPHS[g]]) for g in range(NG)]
        mask_nat = sb("mask_nat", [B, 128])
        w3T = sb("w3T", [128, 128])
        mask_all = sb("mask_all", [128, B])
        whh_hi, whh_lo = sb("whh_hi", [128, 3, 128], f32r), sb("whh_lo", [128, 3, 128], f32r)
        wc_hi, wc_lo = sb("wc_hi", [128, LAYERS, 384], f32r), sb("wc_lo", [128, LAYERS, 384], f32r)
        wcur_hi = [sb(f"wcur_hi{i}", [128, 384], f32r) for i in range(2)]
        wcur_lo = [sb(f"wcur_lo{i}", [128, 384], f32r) for i in range(2)]
        bih, bhh, brz = sb("bih", [128, 3]), sb("bhh", [128, 3]), sb("brz", [128, 2])
        brz2 = sb("brz2", [128, 2])
        wl1 = sb("wl1", [128, 384])
        bt_bc, b3_bc = sb("bt_bc", [128, 128]), sb("b3_bc", [128, 128])
        w1_sb, w2_sb = sb("w1_sb", [128, NG, E]), sb("w2_sb", [128, NG, EH, 128])
        b1_sb, b2_sb = sb("b1_sb", [128, NG, EH]), sb("b2_sb", [128, NG])
        fw, fmax, fexp, fsum, finv, fshare = (sb(n, [128, NG if n in ("fw", "fexp", "fshare") else 1])
                                              for n in ("fw", "fmax", "fexp", "fsum", "finv", "fshare"))

        x_in = sb("x_in", [128, RG, 128])
        adj_in = sb("adj_in", [128, RG, 128])
        x_res = sb("x_res", [128, RG, 128])
        edge = sb("edge", [128, RG, 128])
        adjT = sb("adjT", [128, RG, 128])
        adjTI = sb("adjTI", [128, RG, 128])
        conv_nat, wih_nat, whh_nat = adjTI[:, 0:LAYERS, :], adjTI[:, 5:8, :], adjTI[:, 8:11, :]
        w3_nat, convT, wihT = adjTI[:, 11, :], adjT[:, 0:LAYERS, :], adjT[:, 5:8, :]
        mask_r = sb("mask_r", [128, RG])
        deg1, deg3 = sb("deg1", [128, RG]), sb("deg3", [128, RG])
        norm1, dis, dis_mask = sb("norm1", [128, RG]), sb("dis", [128, RG]), sb("dis_mask", [128, RG])
        degs1, degs3 = sb("degs1", [128, RG]), sb("degs3", [128, RG])
        stats = [sb(f"stats{i}", [128, RG, 6]) for i in range(2)]
        mv = [sb(f"mv{i}", [128, RG, 2]) for i in range(2)]
        var_eps, neg_mean, rstd, shift = ([sb(f"{n}{i}", [128, RG]) for i in range(2)]
                                          for n in ("var_eps", "neg_mean", "rstd", "shift"))
        xn = sb("xn", [128, RG, 128])
        hT = sb("hT", [128, RG, 128])
        h = [sb(f"h{q}", [128, 512]) for q in range(QUADS)]
        h_hi = [sb(f"h_hi{q}", [128, 512], f32r) for q in range(QUADS)]
        h_lo = [sb(f"h_lo{q}", [128, 512], f32r) for q in range(QUADS)]
        hn = [sb(f"hn{i}", [128, QUAD, 128]) for i in range(2)]
        g_hi = [sb(f"g_hi{i}", [128, 512], f32r) for i in range(2)]
        g_lo = [sb(f"g_lo{i}", [128, 512], f32r) for i in range(2)]
        gr, gz, rh, pre, gn, hd, zd = ([sb(f"{n}{i}", [128, 512]) for i in range(2)]
                                       for n in ("gr", "gz", "rh", "pre", "gn", "hd", "zd"))
        f_hom, f_het = sb("f_hom", [128, 2, 512]), sb("f_het", [128, 2, 512])
        gate_th, diff, gated, mix, neg, ex = gz, pre, gn, hd, zd, hn
        xn0 = [gr[0], gr[1], gn[0], gn[1]]
        rows = [sb(f"rows{g}", [128, RG // GROUP_GRAPHS[g], SIZE[g]]) for g in range(NG)]
        deg2, deg_zero, deg_safe, deg_pow, dinv = (sb(n, [128, NT]) for n in
                                                   ("deg2", "deg_zero", "deg_safe", "deg_pow", "dinv"))
        deg_some = sb("deg_some", [128, NT])
        blocks0, blocks = sb("blocks0", [128, NT, 128]), sb("blocks", [128, NT, 128])
        normT = sb("normT", [128, NT, 128])
        packed = sb("packed", [128, NT, 128])
        sup1 = sb("sup1", [128, 2, E])
        hid = sb("hid", [128, 2, EH, 128])
        sup2 = sb("sup2", [128, 2, 128])
        conv2 = sb("conv2", [128, 2, 128])
        fused = sb("fused", [128, ZONE, RG])
        y, scaled = zd, hd

        bank = [ctx.enter_context(nc.psum_tensor(f"bank{i}", [128, 512], f32)) for i in range(2)]
        quad_bank = ctx.enter_context(nc.psum_tensor("quad_bank", [128, 4, 512], f32))
        bank += [quad_bank[:, i, :] for i in range(4)]
        bank += [ctx.enter_context(nc.psum_tensor(f"bank{i}", [128, 512], f32)) for i in (6, 7)]
        T_BANK, G_BANK, R_BANK, Z_BANK, H_BANK, I_BANK, A_BANK, B_BANK = bank

        sem = {n: ctx.enter_context(nc.semaphore(n)) for n in (
            "weights_loaded", "late_weights_loaded", "x_loaded", "adj_loaded", "rows_loaded", "stored",
            "x_in_free", "adj_in_free", "rows_free", "pe_passed", "dve_passed",
            "cleared", "consts", "dve_setup", "dve_turns", "w_turned", "w_turned_read", "wc_made", "setup_done", "fexp_done",
            "mask_round", "degs", "degs_eps", "norms", "adj_turned", "adjT_ready", "adjTI_made",
            "adjT_scaled", "adjTI_scaled", "edge_ready",
            "group_sum", "group_safe", "group_pow", "blocks_half", "blocks_ready",
            "blocks_turned", "normT_ready",
            "wA", "wB", "h_new", "h_hi_new", "h_lo_new", "h_turned", "hn_ready", "g_made", "g_hi_ready",
            "g_lo_ready", "gates_r", "gates_h", "hb_ready", "gates_n", "gates_z", "r_ready", "z_ready",
            "rh_ready", "pre_ready", "n_ready", "hd_ready", "zd_ready",
            "l1_turned", "l1_x", "l1_lin", "l1_f_hom", "l1_f_het", "l1_gate", "l1_agg",
            "l1_diff", "l1_gated", "l1_mix", "l1_neg", "l1_exp", "l1_elu", "l1_out",
            "zone_turned", "packed_ready", "fused_zero", "l2_sup1", "l2_sup1_read", "l2_hid",
            "l2_hid_read", "l2_sup2", "l2_sup2_read", "l2_conv2", "l2_conv2_read", "l2_added",
            "l2_back", "l2_out",
            "l3_lin", "l3_y", "l3_agg", "l3_scaled", "out_ready",
        )}
        for L in range(4):
            for n in ("stats", "mv", "var", "pow", "rstd", "xn", "turned", "h"):
                sem[f"ln{L}_{n}"] = ctx.enter_context(nc.semaphore(f"ln{L}_{n}"))

        def cols(q):
            return slice(q * QUAD, (q + 1) * QUAD)

        def per_graph(t, q):
            return t[:, cols(q)].unsqueeze(2).to_broadcast([128, QUAD, 128])

        def per_quad(t):
            return t[:].unsqueeze(1).to_broadcast([128, QUAD, 128])

        def quad(t):
            return t.rearrange("p (b d) -> p b d", b=QUAD)

        def pipelined(stages, units=QUADS, between=()):
            for turn in range(units + len(stages) - 1):
                for n in reversed(range(len(stages))):
                    if 0 <= turn - n < units and stages[n]:
                        stages[n](turn - n)
                if turn < len(between) and between[turn]:
                    between[turn]()

        def pause(engine, passed):
            engine.sem_inc(sem[passed], 1)

        def snap(engine, value):
            return value if isinstance(value, int) else engine.snap(value)

        def every_round(engine, work):
            with engine.Fori(0, ROUNDS - 1) as r:
                work(r, True)
            work(ROUNDS - 1, False)

        BLOCK_AT, used = [], [0, 0]
        for _, _, _, n in TILES:
            half = 0 if used[0] + n <= 512 else 1
            BLOCK_AT.append((half, used[half]))
            used[half] += n

        N_EARLY, N_LATE = 7, 14
        row_loads = [(g, t, ra, ca) for g in range(NG) for t in range(RG // GROUP_GRAPHS[g])
                     for ra in range(len(GROUP_RUNS[g])) for ca in range(len(GROUP_RUNS[g]))]
        block = ctx.enter_context(nc.Block())

        @block.sync
        def _(sp):
            def load_adjacency(r):
                for b in range(0, RG, HALF):
                    sp.dma_start(adj_in[:, b:b + HALF], adj[bass.ds(r * RG + b, HALF)].rearrange("b n m -> n b m")
                                 ).then_inc(sem["adj_loaded"], 16)

            def load_rows(r):
                for g, t, ra, ca in row_loads:
                    G, runs = GROUP_GRAPHS[g], GROUP_RUNS[g]
                    n0 = sum(b - a for a, b in runs[:ra])
                    m0 = sum(b - a for a, b in runs[:ca])
                    (na, nb), (ma, mb) = runs[ra], runs[ca]
                    sp.dma_start(rows[g][n0 * G:(n0 + nb - na) * G, t, m0:m0 + mb - ma],
                                 adj[bass.ds(r * RG + t * G, G), na:nb, ma:mb].rearrange("b n m -> n b m")
                                 ).then_inc(sem["rows_loaded"], 16)

            def load_x(r):
                for b in range(0, RG, HALF):
                    sp.dma_start(x_in[:, b:b + HALF], x[bass.ds(r * RG + b, HALF)].rearrange("b n d -> n b d")
                                 ).then_inc(sem["x_loaded"], 16)

            load_x(0)
            w = sem["weights_loaded"]
            sp.dma_start(conv_nat[:], conv_w.rearrange("l d e -> d l e")).then_inc(w, 16)
            sp.dma_start(wih_nat[:], w_ih.rearrange("(g c) e -> c g e", g=3)).then_inc(w, 16)
            sp.dma_start(whh_nat[:], w_hh.rearrange("(g c) e -> c g e", g=3)).then_inc(w, 16)
            sp.dma_start(w3_nat[:], W3).then_inc(w, 16)
            sp.dma_start(mask_nat[:], nodemask).then_inc(w, 16)
            sp.dma_start(bih[:], b_ih.rearrange("(g c) -> c g", g=3)).then_inc(w, 16)
            sp.dma_start(bhh[:], b_hh.rearrange("(g c) -> c g", g=3)).then_inc(w, 16)
            load_adjacency(0)
            load_rows(0)
            w = sem["late_weights_loaded"]
            sp.dma_start(fw[:], fusion_w.partition_broadcast(128)).then_inc(w, 16)
            for i, t in enumerate((theta, W_h, W_t)):
                sp.dma_start(wl1[:, i * 128:(i + 1) * 128], t).then_inc(w, 16)
            sp.dma_start(bt_bc[:], b_t.partition_broadcast(128)).then_inc(w, 16)
            sp.dma_start(b3_bc[:], b3.partition_broadcast(128)).then_inc(w, 16)
            sp.dma_start(w1_sb[:], W1.rearrange("g d e -> d g e")).then_inc(w, 16)
            for g in range(NG):
                sp.dma_start(w2_sb[:, g], W2[g].rearrange("(k e) d -> e k d", k=EH)).then_inc(w, 16)
            sp.dma_start(b2_sb[:], b2.rearrange("g d -> d g")).then_inc(w, 16)
            sp.dma_start(b1_sb[:], b1.rearrange("g (k e) -> e g k", k=EH)).then_inc(w, 16)

            def round_of_transfers(r, following):
                if following:
                    sp.wait_ge(sem["adj_in_free"], 2 * r + 2)
                    load_adjacency(r + 1)
                    sp.wait_ge(sem["rows_free"], r + 1)
                    load_rows(r + 1)
                    sp.wait_ge(sem["x_in_free"], r + 1)
                    load_x(r + 1)
                for q in range(QUADS):
                    sp.wait_ge(sem["out_ready"], r * QUADS + q + 1)
                    sp.dma_start(out[bass.ds(r * RG + q * QUAD, QUAD)].rearrange("b n d -> n b d"),
                                 x_res[:, cols(q), :]).then_inc(sem["stored"], 16)

            every_round(sp, round_of_transfers)
            sp.wait_ge(sem["stored"], 16 + 16 * QUADS * ROUNDS)

        @block.tensor
        def _(pe):
            def turn_adjacency(r, q):
                dst = (T_BANK, G_BANK)[q % 2]
                pe.wait_ge(sem["adj_loaded"], r * 32 + 32)
                if q >= 2:
                    pe.wait_ge(sem["adjT_ready"], r * QUADS + q - 1)
                for j in range(QUAD):
                    last = nc.tensor.transpose(dst[:, j * 128:(j + 1) * 128], adj_in[:, q * QUAD + j, :], ident[:])
                last.then_inc(sem["adj_turned"], 1)
                if q == QUADS - 1:
                    pe.wait_ge(sem["adj_turned"], r * QUADS + QUADS)
                    pe.sem_inc(sem["adj_in_free"], 1)

            def turn_first_norm(r, q):
                pe.wait_ge(sem["ln0_xn"], r * QUADS + q + 1)
                if q >= 2:
                    pe.wait_ge(sem["h_new"], r * PRODUCED + q - 1)
                for j in range(QUAD):
                    last = nc.tensor.transpose((H_BANK, I_BANK)[q % 2][:, j * 128:(j + 1) * 128],
                                               xn0[q][:, j * 128:(j + 1) * 128], ident[:])
                last.then_inc(sem["ln0_turned"], 1)

            def turn_blocks(r):
                pe.wait_ge(sem["blocks_ready"], r + 1)
                for k, (g, b0, G, n) in enumerate(TILES):
                    half, at = BLOCK_AT[k]
                    last = nc.tensor.transpose((R_BANK, Z_BANK)[half][0:n, at:at + n], blocks[0:n, k, 0:n], ident[0:n, 0:n])
                last.then_inc(sem["blocks_turned"], 1)

            def turn_h(new, s):
                pe.wait_ge(sem["h_new"], new)
                for j in range(QUAD):
                    last = nc.tensor.transpose(T_BANK[:, j * 128:(j + 1) * 128], h[s][:, j * 128:(j + 1) * 128], ident[:])
                last.then_inc(sem["h_turned"], 1)

            def aggregate(step, s):
                pe.wait_ge(sem["hn_ready"], step + 1)
                for j in range(QUAD):
                    last = nc.tensor.matmul(G_BANK[:, j * 128:(j + 1) * 128], hn[s % 2][:, j, :],
                                            edge[:, s * QUAD + j, :], start=True, stop=True)
                last.then_inc(sem["g_made"], 1)

            def split_matmul(dst, w_hi, w_lo, m_hi, m_lo, start, stop):
                nc.tensor.matmul(dst[:], w_hi, m_hi, start=start, stop=False)
                nc.tensor.matmul(dst[:], w_lo, m_hi, start=False, stop=False)
                return nc.tensor.matmul(dst[:], w_hi, m_lo, start=False, stop=stop)

            def step_of(steps, new, s, weights, following=True):
                if following:
                    turn_h(new + s + 2, (s + 1) % QUADS)
                pe.wait_ge(sem["h_lo_new"], steps + s + 1)
                pe.wait_ge(sem["hb_ready"], steps + s + 1)
                split_matmul(H_BANK, whh_hi[:, 2, :], whh_lo[:, 2, :], h_hi[s][:], h_lo[s][:], True, True).then_inc(sem["gates_h"], 1)
                pe.wait_ge(sem["r_ready"], steps + s + 1)
                split_matmul(R_BANK, whh_hi[:, 0, :], whh_lo[:, 0, :], h_hi[s][:], h_lo[s][:], True, False)
                pe.wait_ge(sem["z_ready"], steps + s + 1)
                split_matmul(Z_BANK, whh_hi[:, 1, :], whh_lo[:, 1, :], h_hi[s][:], h_lo[s][:], True, False)
                pe.wait_ge(sem["g_lo_ready"], steps + s + 1)
                if following:
                    aggregate(steps + s + 1, (s + 1) % QUADS)
                if s % 2 == 0:
                    pe.wait_ge(sem["wA" if s == 0 else "wB"], weights)
                ch, cl = wcur_hi[s // 2], wcur_lo[s // 2]
                k = s % 2
                split_matmul(R_BANK, ch[:, 0:128], cl[:, 0:128], g_hi[k][:], g_lo[k][:], False, True).then_inc(sem["gates_r"], 1)
                pe.wait_ge(sem["pre_ready"], steps + s + 1)
                split_matmul(I_BANK, ch[:, 256:384], cl[:, 256:384], g_hi[k][:], g_lo[k][:], True, True).then_inc(sem["gates_n"], 1)
                split_matmul(Z_BANK, ch[:, 128:256], cl[:, 128:256], g_hi[k][:], g_lo[k][:], False, True).then_inc(sem["gates_z"], 1)


            pe.wait_ge(sem["consts"], 1)
            for q in range(QUADS):
                turn_first_norm(0, q)
            pe.wait_ge(sem["weights_loaded"], 16 * N_EARLY)
            pe.wait_ge(sem["h_new"], QUADS)
            for i in range(3):
                nc.tensor.transpose(bank[2][:, i * 128:(i + 1) * 128], wih_nat[:, i, :], ident[:])
            for i in range(3):
                nc.tensor.transpose(bank[3][:, i * 128:(i + 1) * 128], whh_nat[:, i, :], ident[:])
            for i in range(4):
                nc.tensor.transpose(bank[4][:, i * 128:(i + 1) * 128], conv_nat[:, i, :], ident[:])
            nc.tensor.transpose(bank[5][:, 0:128], conv_nat[:, 4, :], ident[:])
            nc.tensor.transpose(bank[5][:, 128:256], w3_nat[:], ident[:])
            nc.tensor.transpose(bank[5][:, 256:256 + B], mask_nat[:], ident[0:B, 0:B]).then_inc(sem["w_turned"], 1)
            pe.wait_ge(sem["w_turned_read"], 1)
            for l in range(LAYERS):
                fold = nc.tensor.matmul(bank[(0, 1, 6, 7, 2)[l]][:, 0:384], convT[:, l, :],
                                        wihT[:, :, :].rearrange("e g c -> e (g c)"), start=True, stop=True)
            fold.then_inc(sem["wc_made"], 1)
            pe.wait_ge(sem["setup_done"], 1)
            for q in range(QUADS):
                turn_adjacency(0, q)
            turn_blocks(0)
            pe.wait_ge(sem["adjT_ready"], QUADS)
            pe.wait_ge(sem["late_weights_loaded"], 16 * N_LATE)

            def round_of_products(r, following):
                quads = snap(pe, r * QUADS)

                def turn_norm(L, q, dst):
                    pe.wait_ge(sem[f"ln{L}_xn"], quads + q + 1)
                    if q:
                        pe.wait_ge(sem[f"ln{L}_h"], quads + q)
                    for j in range(QUAD):
                        last = nc.tensor.transpose(dst[:, j * 128:(j + 1) * 128], xn[:, q * QUAD + j, :], ident[:])
                    last.then_inc(sem[f"ln{L}_turned"], 1)

                pe.wait_ge(sem["h_new"], r * PRODUCED + QUADS)
                pe.wait_ge(sem["normT_ready"], r + 1)
                pe.wait_ge(sem["edge_ready"], quads + QUADS)
                turn_h(r * PRODUCED + 1, 0)
                aggregate(r * STEPS, 0)
                with pe.Fori(0, LAYERS - 1) as l:
                    steps = pe.snap(r * STEPS + l * QUADS)
                    new = pe.snap(r * PRODUCED + l * QUADS)
                    wl = pe.snap(r * LAYERS + l + 1)
                    for s in range(QUADS):
                        step_of(steps, new, s, wl)
                steps = snap(pe, r * STEPS + (STEPS - QUADS))
                new = snap(pe, r * PRODUCED + (STEPS - QUADS))
                for s in range(QUADS):
                    step_of(steps, new, s, r * LAYERS + LAYERS, following=s + 1 < QUADS)

                def turn_out(q):
                    pe.wait_ge(sem["h_new"], r * PRODUCED + STEPS + q + 1)
                    if q >= 2:
                        pe.wait_ge(sem["l1_x"], quads + q - 1)
                    for j in range(QUAD):
                        last = nc.tensor.transpose((A_BANK, B_BANK)[q % 2][:, j * 128:(j + 1) * 128],
                                                   h[q][:, j * 128:(j + 1) * 128], ident[:])
                    last.then_inc(sem["l1_turned"], 1)

                def l1_linear(q):
                    if q == 0:
                        for n in ("r_ready", "z_ready", "hb_ready", "pre_ready"):
                            pe.wait_ge(sem[n], r * STEPS + STEPS + 1)
                    else:
                        pe.wait_ge(sem["l1_f_het"], quads + q)
                    pe.wait_ge(sem["ln1_h"], quads + q + 1)
                    for j in range(QUAD):
                        nc.tensor.matmul(quad_bank[:, j, 0:384], hT[:, q * QUAD + j, :], wl1[:], start=True, stop=False)
                        last = nc.tensor.matmul(quad_bank[:, j, 256:384], top_ones[:], bt_bc[:], start=False, stop=True)
                    last.then_inc(sem["l1_lin"], 1)

                def l1_aggregate(q):
                    if q == 0:
                        pe.wait_ge(sem["adjT_scaled"], quads + QUADS)
                    else:
                        pe.wait_ge(sem["l1_diff"], quads + q)
                    pe.wait_ge(sem["l1_f_hom"], quads + q + 1)
                    for j in range(QUAD):
                        last = nc.tensor.matmul(G_BANK[:, j * 128:(j + 1) * 128], adjT[:, q * QUAD + j, :],
                                                f_hom[:, q % 2, j * 128:(j + 1) * 128], start=True, stop=True)
                    last.then_inc(sem["l1_agg"], 1)

                pipelined([turn_out, None, lambda q: turn_norm(1, q, T_BANK), l1_linear, l1_aggregate])

                for q in range(QUADS):
                    pe.wait_ge(sem["ln2_xn"], quads + q + 1)
                    pause(pe, "pe_passed")
                    for j in range(QUAD):
                        b = q * QUAD + j
                        last = nc.tensor.transpose(T_BANK[:, b * ZONE:(b + 1) * ZONE], xn[0:ZONE, b, :],
                                                   ident[0:ZONE, 0:ZONE])
                last.then_inc(sem["zone_turned"], 1)
                tiles = snap(pe, r * NT)

                def l2_support(k):
                    g, b0, G, n = TILES[k]
                    if k == 0:
                        pe.wait_ge(sem["packed_ready"], r + 1)
                    nc.tensor.matmul(R_BANK[0:n, 0:E], packed[:, k, 0:n], w1_sb[:, g, :],
                                     start=True, stop=True).then_inc(sem["l2_sup1"], 1)

                def l2_hidden(k):
                    g, b0, G, n = TILES[k]
                    pe.wait_ge(sem["l2_sup1_read"], tiles + k + 1)
                    for e in range(EH):
                        last = nc.tensor.matmul(Z_BANK[:, e * 128:e * 128 + n], sup1[0:n, k % 2, e * 128:(e + 1) * 128],
                                                normT[0:n, k, 0:n], start=True, stop=True)
                    last.then_inc(sem["l2_hid"], 1)

                def l2_support2(k):
                    g, b0, G, n = TILES[k]
                    pe.wait_ge(sem["l2_hid_read"], tiles + k + 1)
                    for e in range(EH):
                        last = nc.tensor.matmul(H_BANK[0:n, 0:128], hid[:, k % 2, e, 0:n], w2_sb[:, g, e, :],
                                                start=(e == 0), stop=(e == EH - 1))
                    last.then_inc(sem["l2_sup2"], 1)

                def l2_conv2(k):
                    g, b0, G, n = TILES[k]
                    pe.wait_ge(sem["l2_sup2_read"], tiles + k + 1)
                    if k:
                        pe.wait_ge(sem["l2_conv2_read"], tiles + k)
                    nc.tensor.matmul(I_BANK[:, 0:n], sup2[0:n, k % 2, :], normT[0:n, k, 0:n],
                                     start=True, stop=True).then_inc(sem["l2_conv2"], 1)

                adjacency = [None] * 8
                if following:
                    for q in range(QUADS):
                        adjacency[2 * q + 1] = lambda q=q: turn_adjacency(r + 1, q)
                pipelined([l2_support, l2_hidden, l2_support2, l2_conv2], NT, adjacency)
                pe.wait_ge(sem["l2_added"], tiles + NT)

                def l3_back(q):
                    if q >= 2:
                        pe.wait_ge(sem["l2_out"], quads + q - 1)
                    for j in range(QUAD):
                        last = nc.tensor.transpose((A_BANK, B_BANK)[q % 2][0:ZONE, j * 128:(j + 1) * 128],
                                                   fused[:, :, q * QUAD + j], ident[:])
                    last.then_inc(sem["l2_back"], 1)

                def l3_linear(q):
                    pe.wait_ge(sem["ln3_h"], quads + q + 1)
                    if q:
                        pe.wait_ge(sem["l3_y"], quads + q)
                    for j in range(QUAD):
                        nc.tensor.matmul(G_BANK[:, j * 128:(j + 1) * 128], hT[:, q * QUAD + j, :], w3T[:],
                                         start=True, stop=False)
                        last = nc.tensor.matmul(G_BANK[:, j * 128:(j + 1) * 128], top_ones[:], b3_bc[:],
                                                start=False, stop=True)
                    last.then_inc(sem["l3_lin"], 1)

                def l3_aggregate(q):
                    pe.wait_ge(sem["l3_y"], quads + q + 1)
                    if q == 0:
                        pe.wait_ge(sem["l2_out"], quads + QUADS)
                        pe.wait_ge(sem["adjTI_scaled"], quads + QUADS)
                    if q >= 2:
                        pe.wait_ge(sem["out_ready"], quads + q - 1)
                    for j in range(QUAD):
                        last = nc.tensor.matmul((A_BANK, B_BANK)[q % 2][:, j * 128:(j + 1) * 128],
                                                adjTI[:, q * QUAD + j, :], y[q % 2][:, j * 128:(j + 1) * 128],
                                                start=True, stop=True)
                    last.then_inc(sem["l3_agg"], 1)

                def turn_norms(q):
                    turn_norm(3, q, T_BANK)
                    if following:
                        turn_first_norm(r + 1, q)

                if following:
                    pe.wait_ge(sem["adjT_ready"], quads + 2 * QUADS)
                pipelined([l3_back, None, turn_norms, l3_linear, l3_aggregate],
                          between=[None, lambda: turn_blocks(r + 1)] if following else ())

            every_round(pe, round_of_products)

        @block.scalar
        def _(act):
            def norm_relu(L, r, q, src, dst, parts=128):
                i = 0 if L == 0 else 1
                act.wait_ge(sem[f"ln{L}_rstd"], r * QUADS + q + 1)
                for j in range(QUAD):
                    b = q * QUAD + j
                    last = nc.scalar.activation(dst[0:parts, j, :], src[0:parts, b, :], ACT.Relu,
                                                bias=shift[i][0:parts, b:b + 1], scale=rstd[i][0:parts, b:b + 1])
                last.then_inc(sem[f"ln{L}_xn"], 1)

            def first_h(r, q):
                act.wait_ge(sem["ln0_turned"], r * QUADS + q + 1)
                nc.scalar.activation(h[q][:], (H_BANK, I_BANK)[q % 2][:], ACT.Copy).then_inc(sem["h_new"], 1)

            def read_adjacency(r, q):
                act.wait_ge(sem["adj_turned"], r * QUADS + q + 1)
                nc.scalar.activation(adjT[:, cols(q), :], quad((T_BANK, G_BANK)[q % 2][:, :]), ACT.Copy
                                     ).then_inc(sem["adjT_ready"], 1)

            def read_blocks(r):
                act.wait_ge(sem["blocks_turned"], r + 1)
                for k, (g, b0, G, n) in enumerate(TILES):
                    half, at = BLOCK_AT[k]
                    last = nc.scalar.activation(normT[0:n, k, 0:n], (R_BANK, Z_BANK)[half][0:n, at:at + n],
                                                ACT.Copy, scale=dinv[0:n, k:k + 1])
                last.then_inc(sem["normT_ready"], 1)

            def turned_h(step, s):
                act.wait_ge(sem["h_turned"], step + 1)
                nc.scalar.activation(hn[s % 2][:], quad(T_BANK[:, :]), ACT.Copy).then_inc(sem["hn_ready"], 1)

            def aggregate_hi(step, s):
                act.wait_ge(sem["g_made"], step + 1)
                nc.scalar.activation(g_hi[s % 2][:], G_BANK[:], ACT.Copy).then_inc(sem["g_hi_ready"], 1)

            def step_of(steps, s, following=True):
                k = s % 2
                if following:
                    turned_h(steps + s + 1, (s + 1) % QUADS)
                act.wait_ge(sem["gates_h"], steps + s + 1)
                nc.scalar.activation(rh[k][:], H_BANK[:], ACT.Identity, bias=bhh[:, 2:3]).then_inc(sem["hb_ready"], 1)
                if following:
                    aggregate_hi(steps + s + 1, (s + 1) % QUADS)
                act.wait_ge(sem["gates_r"], steps + s + 1)
                nc.scalar.activation(gr[k][:], R_BANK[:], ACT.Tanh, bias=brz[:, 0:1], scale=0.5).then_inc(sem["r_ready"], 1)
                act.wait_ge(sem["gates_z"], steps + s + 1)
                nc.scalar.activation(gz[k][:], Z_BANK[:], ACT.Tanh, bias=brz[:, 1:2], scale=0.5).then_inc(sem["z_ready"], 1)
                act.wait_ge(sem["pre_ready"], steps + s + 2)
                nc.scalar.activation(gn[k][:], pre[k][:], ACT.Tanh, bias=bih[:, 2:3]).then_inc(sem["n_ready"], 1)


            for q in range(QUADS):
                norm_relu(0, 0, q, x_in, quad(xn0[q][:, :]))
            for q in range(QUADS):
                first_h(0, q)
            for q in range(QUADS):
                read_adjacency(0, q)
            act.wait_ge(sem["dve_setup"], 1)
            nc.scalar.activation(fexp[:], fw[:], ACT.Exp, bias=fmax[:]).then_inc(sem["fexp_done"], 1)
            read_blocks(0)

            def round_of_activations(r, following):
                quads = snap(act, r * QUADS)
                turned_h(r * STEPS, 0)
                aggregate_hi(r * STEPS, 0)
                with act.Fori(0, LAYERS - 1) as l:
                    steps = act.snap(r * STEPS + l * QUADS)
                    for s in range(QUADS):
                        step_of(steps, s)
                steps = snap(act, r * STEPS + (STEPS - QUADS))
                for s in range(QUADS):
                    step_of(steps, s, following=s + 1 < QUADS)

                def turned_norm(L, q):
                    act.wait_ge(sem[f"ln{L}_turned"], quads + q + 1)
                    nc.scalar.activation(hT[:, cols(q), :], quad(T_BANK[:, :]), ACT.Copy).then_inc(sem[f"ln{L}_h"], 1)

                def l1_read_linear(q):
                    k = q % 2
                    act.wait_ge(sem["l1_lin"], quads + q + 1)
                    if q >= 2:
                        act.wait_ge(sem["l1_mix"], quads + q - 1)
                    nc.scalar.activation(quad(f_hom[:, k, :]), quad_bank[:, :, 0:128], ACT.Copy).then_inc(sem["l1_f_hom"], 1)
                    nc.scalar.activation(quad(gate_th[k][:, :]), quad_bank[:, :, 256:384], ACT.Tanh, scale=0.5).then_inc(sem["l1_gate"], 1)
                    nc.scalar.activation(quad(f_het[:, k, :]), quad_bank[:, :, 128:256], ACT.Copy).then_inc(sem["l1_f_het"], 1)

                def l1_exp(q):
                    k = q % 2
                    act.wait_ge(sem["l1_mix"], quads + q + 1)
                    nc.scalar.activation(neg[k][:], mix[k][:], ACT.Relu, scale=-1.0).then_inc(sem["l1_neg"], 1)
                    act.wait_ge(sem["l1_neg"], quads + q + 1)
                    if q >= 2:
                        act.wait_ge(sem["l1_elu"], quads + q - 1)
                    nc.scalar.activation(ex[k][:], quad(neg[k][:, :]), ACT.Exp, scale=-1.0).then_inc(sem["l1_exp"], 1)

                pipelined([None, lambda q: norm_relu(1, r, q, x_res, xn[:, cols(q), :]), lambda q: turned_norm(1, q),
                           l1_read_linear, None, l1_exp, None,
                           lambda q: norm_relu(2, r, q, x_res, xn[:, cols(q), :], ZONE)])

                act.wait_ge(sem["zone_turned"], r + 1)
                zone = T_BANK[:, 0:RG * ZONE].rearrange("d (b n) -> d b n", b=RG)
                for g, G in enumerate(GROUP_GRAPHS):
                    for k in (k for k, t in enumerate(TILES) if t[0] == g):
                        b0, m0 = TILES[k][1], 0
                        for a, b in GROUP_RUNS[g]:
                            last = nc.scalar.activation(
                                packed[:, k, m0 * G:(m0 + b - a) * G].rearrange("d (n b) -> d n b", b=G),
                                zone[:, b0:b0 + G, a:b].rearrange("d b n -> d n b"), ACT.Relu)
                            m0 += b - a
                last.then_inc(sem["packed_ready"], 1)
                tiles = snap(act, r * NT)

                def read_support(k):
                    n = TILES[k][3]
                    act.wait_ge(sem["l2_sup1"], tiles + k + 1)
                    nc.scalar.activation(sup1[0:n, k % 2, :], R_BANK[0:n, 0:E], ACT.Copy).then_inc(sem["l2_sup1_read"], 1)

                def read_hidden(k):
                    g, b0, G, n = TILES[k]
                    act.wait_ge(sem["l2_hid"], tiles + k + 1)
                    for e in range(EH):
                        last = nc.scalar.activation(hid[:, k % 2, e, 0:n], Z_BANK[:, e * 128:e * 128 + n], ACT.Relu,
                                                    bias=b1_sb[:, g, e:e + 1])
                    last.then_inc(sem["l2_hid_read"], 1)

                adjacency = [None] * 9
                if following:
                    for q in range(QUADS):
                        adjacency[2 * q + 2] = lambda q=q: read_adjacency(r + 1, q)
                pipelined([read_support, read_hidden], NT, adjacency)

                def normalise(q):
                    norm_relu(3, r, q, x_res, xn[:, cols(q), :])
                    if following:
                        norm_relu(0, r + 1, q, x_in, quad(xn0[q][:, :]))

                def read_norms(q):
                    turned_norm(3, q)
                    if following:
                        first_h(r + 1, q)

                def l3_read_linear(q):
                    act.wait_ge(sem["l3_lin"], quads + q + 1)
                    if q >= 2:
                        act.wait_ge(sem["l3_agg"], quads + q - 1)
                    nc.scalar.activation(y[q % 2][:], G_BANK[:], ACT.Copy).then_inc(sem["l3_y"], 1)

                pipelined([None, normalise, read_norms, l3_read_linear],
                          between=[None, lambda: read_blocks(r + 1)] if following else ())

            every_round(act, round_of_activations)

        @block.gpsimd
        def _(pool):
            nc.gpsimd.memset(neg_half[:], -0.5)
            nc.gpsimd.memset(neg_one[:], -1.0)
            nc.gpsimd.memset(eps_ln[:], LN_EPS)
            nc.gpsimd.memset(eps_deg[:], 1e-6)
            nc.gpsimd.memset(deg2[:], 1.0)
            nc.gpsimd.memset(top_ones[:], 1.0)
            nc.gpsimd.memset(ident[:], 0.0).then_inc(sem["cleared"], 1)
            pool.wait_ge(sem["cleared"], 1)
            nc.gpsimd.affine_select(out=top_ones[:], in_=top_ones[:], compare_op=ALU.is_equal, fill=0.0, base=0,
                                    pattern=[[0, 128]], channel_multiplier=1)
            nc.gpsimd.affine_select(out=ident[:], in_=ident[:], compare_op=ALU.not_equal, fill=1.0, base=0,
                                    pattern=[[-1, 128]], channel_multiplier=1).then_inc(sem["consts"], 1)
            pool.wait_ge(sem["consts"], 1)
            pool.sem_inc(sem["stored"], 16)
            for n in ("hb_ready", "r_ready", "z_ready", "pre_ready"):
                pool.sem_inc(sem[n], 1)

            def power(L, r, q):
                c, i = cols(q), 0 if L == 0 else 1
                pool.wait_ge(sem[f"ln{L}_mv"], r * QUADS + q + 1)
                nc.gpsimd.tensor_tensor(var_eps[i][:, c], mv[i][:, c, 1], eps_ln[:, c], ALU.add)
                nc.gpsimd.tensor_tensor(neg_mean[i][:, c], mv[i][:, c, 0], neg_one[:, c], ALU.mult).then_inc(sem[f"ln{L}_var"], 1)
                pool.wait_ge(sem[f"ln{L}_var"], r * QUADS + q + 1)
                nc.gpsimd.tensor_tensor(rstd[i][:, c], var_eps[i][:, c], neg_half[:, c], ALU.pow).then_inc(sem[f"ln{L}_pow"], 1)
                pool.wait_ge(sem[f"ln{L}_pow"], r * QUADS + q + 1)
                nc.gpsimd.tensor_tensor(shift[i][:, c], neg_mean[i][:, c], rstd[i][:, c], ALU.mult).then_inc(sem[f"ln{L}_rstd"], 1)

            def group_power(r):
                pool.wait_ge(sem["group_safe"], r + 1)
                nc.gpsimd.tensor_tensor(deg_pow[:], deg_safe[:], neg_half[:, 0:NT], ALU.pow).then_inc(sem["group_pow"], 1)

            def low_half(new, s):
                pool.wait_ge(sem["h_hi_new"], new + 1)
                nc.gpsimd.tensor_tensor(h_lo[s][:], h[s][:], h_hi[s][:].bitcast(f32), ALU.subtract).then_inc(sem["h_lo_new"], 1)

            for q in range(QUADS):
                power(0, 0, q)
            for q in range(QUADS):
                low_half(q, q)
            group_power(0)

            def round_of_small_work(r, following):
                quads = snap(pool, r * QUADS)
                with pool.Fori(0, LAYERS - 1) as l:
                    new = pool.snap(r * STEPS + l * QUADS)
                    for s in range(QUADS):
                        low_half(new + QUADS + s, s)
                nc.gpsimd.tensor_copy(mask_r[:], mask_all[:, bass.ds(r * RG, RG)]).then_inc(sem["mask_round"], 1)
                for q in range(QUADS):
                    pool.wait_ge(sem["adjT_ready"], quads + q + 1)
                    nc.gpsimd.tensor_tensor(adjTI[:, cols(q), :], adjT[:, cols(q), :],
                                            per_quad(ident), ALU.add).then_inc(sem["adjTI_made"], 1)
                pool.wait_ge(sem["degs"], r + 1)
                nc.gpsimd.tensor_tensor(degs1[:], deg1[:], eps_deg[:], ALU.add)
                nc.gpsimd.tensor_scalar(degs3[:], deg3[:], 1.0, 1e-8, ALU.add, ALU.add).then_inc(sem["degs_eps"], 1)
                pool.wait_ge(sem["degs_eps"], r + 1)
                nc.gpsimd.tensor_tensor(norm1[:], degs1[:], neg_half[:], ALU.pow)
                nc.gpsimd.tensor_tensor(dis[:], degs3[:], neg_half[:], ALU.pow).then_inc(sem["norms"], 1)
                pool.wait_ge(sem["norms"], 2 * r + 1)
                pool.wait_ge(sem["mask_round"], r + 1)
                nc.gpsimd.tensor_tensor(dis_mask[:], dis[:], mask_r[:], ALU.mult).then_inc(sem["norms"], 1)
                for q in range(QUADS):
                    pool.wait_ge(sem["adjTI_made"], quads + q + 1)
                    nc.gpsimd.tensor_tensor(adjT[:, cols(q), :], adjT[:, cols(q), :], per_graph(norm1, q),
                                            ALU.mult).then_inc(sem["adjT_scaled"], 1)
                for q in range(QUADS):
                    nc.gpsimd.tensor_tensor(adjTI[:, cols(q), :], adjTI[:, cols(q), :], per_graph(dis, q),
                                            ALU.mult).then_inc(sem["adjTI_scaled"], 1)
                nc.gpsimd.memset(fused[:], 0.0).then_inc(sem["fused_zero"], 1)
                pipelined([lambda q: power(1, r, q), None, None, None, None, None, lambda q: power(2, r, q)])
                if following:
                    group_power(r + 1)
                    pipelined([lambda q: power(3, r, q), lambda q: power(0, r + 1, q), None,
                               lambda q: low_half(r * STEPS + (STEPS + q), q)])
                    pool.wait_ge(sem["out_ready"], quads + QUADS)
                else:
                    for q in range(QUADS):
                        power(3, r, q)

            every_round(pool, round_of_small_work)

        @block.vector
        def _(dve):
            def norm_stats(L, r, q, src, parts=128):
                i = 0 if L == 0 else 1
                for j in range(QUAD):
                    last = nc.vector.bn_stats(stats[i][0:parts, q * QUAD + j, :], src[0:parts, q * QUAD + j, :])
                last.then_inc(sem[f"ln{L}_stats"], 1)
                dve.wait_ge(sem[f"ln{L}_stats"], r * QUADS + q + 1)
                pause(dve, "dve_passed")
                for j in range(QUAD):
                    last = nc.vector.bn_aggr(mv[i][0:parts, q * QUAD + j, :], stats[i][0:parts, q * QUAD + j, :])
                last.then_inc(sem[f"ln{L}_mv"], 1)

            def layer_weights(layer, which):
                name = "wA" if which == 0 else "wB"
                nc.vector.tensor_copy(wcur_hi[which][:], wc_hi[:, bass.ds(layer, 1), :].bitcast(f32).rearrange("p a c -> p (a c)"))
                nc.vector.tensor_copy(wcur_lo[which][:], wc_lo[:, bass.ds(layer, 1), :].bitcast(f32).rearrange("p a c -> p (a c)")
                                      ).then_inc(sem[name], 1)

            def edges(r, q):
                if q == 0:
                    dve.wait_ge(sem["adj_loaded"], r * 32 + 32)
                nc.vector.tensor_scalar(edge[:, cols(q), :], adj_in[:, cols(q), :], 0.0, None,
                                        ALU.not_equal).then_inc(sem["edge_ready"], 1)

            def degrees_abs(r):
                nc.vector.tensor_reduce(out=deg1[:], in_=adj_in[:], op=ALU.add, axis=AX.X, apply_absolute_value=True)

            def degrees(r):
                nc.vector.tensor_reduce(out=deg3[:], in_=adj_in[:], op=ALU.add, axis=AX.X).then_inc(sem["degs"], 1)
                dve.wait_ge(sem["degs"], r + 1)
                dve.sem_inc(sem["adj_in_free"], 1)

            def group_degrees(r):
                dve.wait_ge(sem["rows_loaded"], (r + 1) * (16 * len(row_loads)))
                for k, (g, b0, G, n) in enumerate(TILES):
                    last = nc.vector.reduce_sum(deg2[0:n, k:k + 1], rows[g][0:n, b0 // G, :], axis=AX.X)
                last.then_inc(sem["group_sum"], 1)
                dve.wait_ge(sem["group_sum"], 3 * r + 1)
                nc.vector.tensor_scalar(deg_zero[:], deg2[:], -1.0, None, ALU.is_equal)
                nc.vector.tensor_scalar(deg_some[:], deg2[:], -1.0, None, ALU.not_equal).then_inc(sem["group_sum"], 1)
                dve.wait_ge(sem["group_sum"], 3 * r + 2)
                nc.vector.scalar_tensor_tensor(deg_safe[:], deg2[:], 1.0, deg_zero[:], ALU.add, ALU.add).then_inc(sem["group_safe"], 1)

            def group_norms(r):
                dve.wait_ge(sem["group_pow"], r + 1)
                nc.vector.tensor_tensor(dinv[:], deg_pow[:], deg_some[:], ALU.mult).then_inc(sem["group_sum"], 1)
                dve.wait_ge(sem["group_sum"], 3 * r + 3)

            def group_blocks(r, half):
                for k, (g, b0, G, n) in list(enumerate(TILES))[(NT // 2) * half:NT // 2 if half == 0 else NT]:
                    m = SIZE[g]
                    last = nc.vector.scalar_tensor_tensor(
                        blocks0[0:n, k, 0:n].rearrange("p (m b) -> p m b", b=G),
                        rows[g][0:n, b0 // G, :].unsqueeze(2).to_broadcast([n, m, G]), dinv[0:n, k:k + 1],
                        gmask[g][0:n, :].unsqueeze(1).to_broadcast([n, m, G]), ALU.mult, ALU.mult)
                last.then_inc(sem["blocks_half"], 1)

            def group_identity(r, half):
                dve.wait_ge(sem["blocks_half"], 2 * r + 1 + half)
                if half:
                    dve.sem_inc(sem["rows_free"], 1)
                for k, (g, b0, G, n) in list(enumerate(TILES))[(NT // 2) * half:NT // 2 if half == 0 else NT]:
                    last = nc.vector.scalar_tensor_tensor(blocks[0:n, k, 0:n], ident[0:n, 0:n], dinv[0:n, k:k + 1],
                                                          blocks0[0:n, k, 0:n], ALU.mult, ALU.add)
                if half:
                    last.then_inc(sem["blocks_ready"], 1)

            def split_h(new, s):
                dve.wait_ge(sem["h_new"], new + 1)
                nc.vector.tensor_copy(h_hi[s][:], h[s][:]).then_inc(sem["h_hi_new"], 1)

            def aggregate_lo(step, s):
                dve.wait_ge(sem["g_hi_ready"], step + 1)
                nc.vector.tensor_tensor(g_lo[s % 2][:], G_BANK[:], g_hi[s % 2][:].bitcast(f32),
                                        ALU.subtract).then_inc(sem["g_lo_ready"], 1)

            def step_of(steps, new, s, layer, following=True, last_layer=False):
                k = s % 2
                dve.wait_ge(sem["hb_ready"], steps + s + 2)
                dve.wait_ge(sem["r_ready"], steps + s + 2)
                nc.vector.scalar_tensor_tensor(rh[k][:], gr[k][:], 1.0, rh[k][:], ALU.add, ALU.mult
                                               ).then_inc(sem["rh_ready"], 1)
                dve.wait_ge(sem["rh_ready"], steps + s + 1)
                dve.wait_ge(sem["gates_n"], steps + s + 1)
                nc.vector.scalar_tensor_tensor(pre[k][:], rh[k][:], 0.5, I_BANK[:], ALU.mult, ALU.add
                                               ).then_inc(sem["pre_ready"], 1)
                if following:
                    aggregate_lo(steps + s + 1, (s + 1) % QUADS)
                if s == 1:
                    layer_weights(layer, 1)
                if s == 3 and not last_layer:
                    layer_weights(layer + 1, 0)
                dve.wait_ge(sem["n_ready"], steps + s + 1)
                nc.vector.tensor_tensor(hd[k][:], h[s][:], gn[k][:], ALU.subtract).then_inc(sem["hd_ready"], 1)
                dve.wait_ge(sem["hd_ready"], steps + s + 1)
                dve.wait_ge(sem["z_ready"], steps + s + 2)
                nc.vector.scalar_tensor_tensor(zd[k][:], gz[k][:], 1.0, hd[k][:], ALU.add, ALU.mult).then_inc(sem["zd_ready"], 1)
                dve.wait_ge(sem["zd_ready"], steps + s + 1)
                nc.vector.scalar_tensor_tensor(h[s][:], zd[k][:], 0.5, gn[k][:], ALU.mult, ALU.add).then_inc(sem["h_new"], 1)
                if not last_layer:
                    split_h(new + QUADS + s, s)

            dve.wait_ge(sem["x_loaded"], 32)
            for q in range(QUADS):
                norm_stats(0, 0, q, x_in)
            dve.wait_ge(sem["weights_loaded"], 16 * N_EARLY)
            dve.wait_ge(sem["consts"], 1)
            nc.vector.tensor_tensor(brz2[:], bih[:, 0:2], bhh[:, 0:2], ALU.add).then_inc(sem["dve_turns"], 1)
            for g, G in enumerate(GROUP_GRAPHS):
                n = G * SIZE[g]
                nc.vector.tensor_reduce(out=gmask[g][0:n, :], in_=ident[0:n, 0:n].rearrange("p (m b) -> p b m", b=G),
                                        op=ALU.add, axis=AX.X)
            dve.wait_ge(sem["dve_turns"], 1)
            nc.vector.tensor_scalar(brz[:], brz2[:], 0.5, None, ALU.mult)
            dve.wait_ge(sem["w_turned"], 1)
            nc.vector.tensor_copy(wihT[:], bank[2][:, 0:384].rearrange("e (g c) -> e g c", g=3))
            nc.vector.tensor_copy(whh_hi[:], bank[3][:, 0:384].rearrange("e (g c) -> e g c", g=3)).then_inc(sem["dve_turns"], 1)
            nc.vector.tensor_copy(convT[:, 0:4, :], quad(bank[4]))
            nc.vector.tensor_copy(convT[:, 4, :], bank[5][:, 0:128])
            nc.vector.tensor_copy(w3T[:], bank[5][:, 128:256])
            nc.vector.tensor_copy(mask_all[:], bank[5][:, 256:256 + B])
            dve.wait_ge(sem["dve_turns"], 2)
            nc.vector.tensor_tensor(whh_lo[:], bank[3][:, 0:384].rearrange("e (g c) -> e g c", g=3),
                                    whh_hi[:].bitcast(f32), ALU.subtract).then_inc(sem["w_turned_read"], 1)
            for q in range(QUADS):
                split_h(q, q)
            for q in range(QUADS):
                edges(0, q)
            degrees_abs(0)
            dve.wait_ge(sem["wc_made"], 1)
            for l in range(LAYERS):
                nc.vector.tensor_copy(wc_hi[:, l, :], bank[(0, 1, 6, 7, 2)[l]][:, 0:384]).then_inc(sem["dve_turns"], 1)
            for l in range(LAYERS):
                dve.wait_ge(sem["dve_turns"], 3 + l)
                last = nc.vector.tensor_tensor(wc_lo[:, l, :], bank[(0, 1, 6, 7, 2)[l]][:, 0:384],
                                               wc_hi[:, l, :].bitcast(f32), ALU.subtract)
            last.then_inc(sem["setup_done"], 1)
            dve.wait_ge(sem["setup_done"], 1)
            layer_weights(0, 0)
            degrees(0)
            group_degrees(0)
            dve.wait_ge(sem["late_weights_loaded"], 16 * N_LATE)
            nc.vector.tensor_reduce(out=fmax[:], in_=fw[:], op=ALU.max, axis=AX.X, negate=True).then_inc(sem["dve_setup"], 1)
            dve.wait_ge(sem["fexp_done"], 1)
            nc.vector.reduce_sum(fsum[:], fexp[:], axis=AX.X).then_inc(sem["dve_setup"], 1)
            dve.wait_ge(sem["dve_setup"], 2)
            nc.vector.reciprocal(finv[:], fsum[:]).then_inc(sem["dve_setup"], 1)
            dve.wait_ge(sem["dve_setup"], 3)
            nc.vector.tensor_scalar(fshare[:], fexp[:], finv[:], None, ALU.mult)
            group_norms(0)
            for half in range(2):
                group_blocks(0, half)
                group_identity(0, half)

            def round_of_elementwise(r, following):
                quads = snap(dve, r * QUADS)

                aggregate_lo(r * STEPS, 0)
                with dve.Fori(0, LAYERS - 1) as l:
                    steps = dve.snap(r * STEPS + l * QUADS)
                    new = dve.snap(r * PRODUCED + l * QUADS)
                    for s in range(QUADS):
                        step_of(steps, new, s, l)
                steps = snap(dve, r * STEPS + (STEPS - QUADS))
                new = snap(dve, r * PRODUCED + (STEPS - QUADS))
                for s in range(QUADS):
                    step_of(steps, new, s, LAYERS - 1, following=s + 1 < QUADS, last_layer=True)

                def l1_residual(q):
                    if q == 0:
                        dve.wait_ge(sem["mask_round"], r + 1)
                        dve.wait_ge(sem["norms"], 2 * r + 2)
                        dve.wait_ge(sem["stored"], r * (16 * QUADS) + 16)
                    dve.wait_ge(sem["l1_turned"], quads + q + 1)
                    src = (A_BANK, B_BANK)[q % 2]
                    for j in range(QUAD):
                        b = q * QUAD + j
                        last = nc.vector.scalar_tensor_tensor(x_res[:, b, :], src[:, j * 128:(j + 1) * 128],
                                                              mask_r[:, b:b + 1], x_in[:, b, :], ALU.mult, ALU.add)
                    last.then_inc(sem["l1_x"], 1)
                    dve.wait_ge(sem["l1_x"], quads + q + 1)
                    if following and q == QUADS - 1:
                        dve.sem_inc(sem["x_in_free"], 1)
                    norm_stats(1, r, q, x_res)

                def l1_gate(q):
                    k = q % 2
                    dve.wait_ge(sem["l1_f_het"], quads + q + 1)
                    dve.wait_ge(sem["l1_agg"], quads + q + 1)
                    for j in range(QUAD):
                        part = slice(j * 128, (j + 1) * 128)
                        last = nc.vector.scalar_tensor_tensor(diff[k][:, part], G_BANK[:, part],
                                                              norm1[:, q * QUAD + j:q * QUAD + j + 1],
                                                              f_het[:, k, part], ALU.mult, ALU.subtract)
                    last.then_inc(sem["l1_diff"], 1)
                    dve.wait_ge(sem["l1_diff"], quads + q + 1)
                    nc.vector.scalar_tensor_tensor(gated[k][:], gate_th[k][:], 1.0, diff[k][:], ALU.add, ALU.mult
                                                   ).then_inc(sem["l1_gated"], 1)
                    dve.wait_ge(sem["l1_gated"], quads + q + 1)
                    if q >= 2:
                        dve.wait_ge(sem["l1_neg"], quads + q - 1)
                    nc.vector.scalar_tensor_tensor(mix[k][:], gated[k][:], 0.5, f_het[:, k, :], ALU.mult, ALU.add
                                                   ).then_inc(sem["l1_mix"], 1)

                def l1_finish(q):
                    k = q % 2
                    dve.wait_ge(sem["l1_exp"], quads + q + 1)
                    nc.vector.scalar_tensor_tensor(gated[k][:], mix[k][:], 0.0, ex[k][:, :, :].rearrange("p b d -> p (b d)"),
                                                   ALU.max, ALU.add).then_inc(sem["l1_elu"], 1)
                    dve.wait_ge(sem["l1_elu"], quads + q + 1)
                    nc.vector.scalar_tensor_tensor(x_res[:, cols(q), :], quad(gated[k][:, :]), -1.0, x_res[:, cols(q), :],
                                                   ALU.add, ALU.add).then_inc(sem["l1_out"], 1)
                    dve.wait_ge(sem["l1_out"], quads + q + 1)
                    norm_stats(2, r, q, x_res, ZONE)

                pipelined([l1_residual, None, None, None, l1_gate, None, l1_finish])

                tiles = snap(dve, r * NT)
                dve.wait_ge(sem["fused_zero"], r + 1)

                def read_support2(k):
                    n = TILES[k][3]
                    dve.wait_ge(sem["l2_sup2"], tiles + k + 1)
                    nc.vector.tensor_copy(sup2[0:n, k % 2, :], H_BANK[0:n, 0:128]).then_inc(sem["l2_sup2_read"], 1)

                def add_group(k):
                    g, b0, G, n = TILES[k]
                    dve.wait_ge(sem["l2_conv2"], tiles + k + 1)
                    nc.vector.tensor_scalar(conv2[:, k % 2, 0:n], I_BANK[:, 0:n], b2_sb[:, g:g + 1], 0.0,
                                            ALU.add, ALU.max).then_inc(sem["l2_conv2_read"], 1)
                    dve.wait_ge(sem["l2_conv2_read"], tiles + k + 1)
                    if k:
                        dve.wait_ge(sem["l2_added"], tiles + k)
                    m0 = 0
                    for a, b in GROUP_RUNS[g]:
                        dst = fused[:, a:b, b0:b0 + G]
                        last = nc.vector.scalar_tensor_tensor(
                            dst, conv2[:, k % 2, m0 * G:(m0 + b - a) * G].rearrange("d (n b) -> d n b", b=G),
                            fshare[:, g:g + 1], dst, ALU.mult, ALU.add)
                        m0 += b - a
                    last.then_inc(sem["l2_added"], 1)

                adjacency = [lambda: edges(r + 1, 0), lambda: edges(r + 1, 1), lambda: edges(r + 1, 2),
                             lambda: edges(r + 1, 3), lambda: degrees_abs(r + 1), lambda: degrees(r + 1),
                             lambda: group_degrees(r + 1), None, lambda: group_norms(r + 1),
                             lambda: group_blocks(r + 1, 0), lambda: group_identity(r + 1, 0),
                             lambda: group_blocks(r + 1, 1)] if following else ()
                pipelined([None, None, read_support2, add_group], NT, adjacency)

                def l2_residual(q):
                    dve.wait_ge(sem["l2_back"], quads + q + 1)
                    nc.vector.tensor_tensor(x_res[0:ZONE, cols(q), :], quad((A_BANK, B_BANK)[q % 2][:, :])[0:ZONE],
                                            x_res[0:ZONE, cols(q), :], ALU.add).then_inc(sem["l2_out"], 1)
                    dve.wait_ge(sem["l2_out"], quads + q + 1)
                    norm_stats(3, r, q, x_res)
                    if following and q == 0:
                        group_identity(r + 1, 1)
                        dve.wait_ge(sem["x_loaded"], r * 32 + 64)
                    if following:
                        norm_stats(0, r + 1, q, x_in)

                def l3_split(q):
                    if following:
                        split_h(r * PRODUCED + (PRODUCED + q), q)

                def l3_finish(q):
                    k = q % 2
                    dve.wait_ge(sem["l3_agg"], quads + q + 1)
                    nc.vector.tensor_tensor(quad(scaled[k][:, :]), quad((A_BANK, B_BANK)[k][:, :]), per_graph(dis_mask, q),
                                            ALU.mult).then_inc(sem["l3_scaled"], 1)
                    dve.wait_ge(sem["l3_scaled"], quads + q + 1)
                    nc.vector.scalar_tensor_tensor(x_res[:, cols(q), :], quad(scaled[k][:, :]), 0.0, x_res[:, cols(q), :],
                                                   ALU.max, ALU.add).then_inc(sem["out_ready"], 1)

                pipelined([l2_residual, None, None, l3_split, l3_finish])
                if following:
                    layer_weights(0, 0)

            every_round(dve, round_of_elementwise)


_INS = ['x', 'adj', 'nodemask', 'L0_gnn_weight', 'L0_gnn_w_ih', 'L0_gnn_w_hh', 'L0_gnn_b_ih', 'L0_gnn_b_hh',
        'L1_gnn_theta', 'L1_gnn_W_h', 'L1_gnn_W_t', 'L1_gnn_b_t', 'L2_gnn_W1', 'L2_gnn_b1', 'L2_gnn_W2',
        'L2_gnn_b2', 'L2_gnn_fusion_w', 'L3_gnn_W', 'L3_gnn_b']


def kernel(**inputs):
    import numpy as np
    import concourse.bacc as bacc
    from concourse.bass_utils import run_bass_kernel_spmd

    nc = bacc.Bacc("TRN2", target_bir_lowering=False, num_devices=1)
    arrays, args = {}, []
    for name in _INS:
        a = np.ascontiguousarray(inputs[name])
        arrays[f"in_{name}"] = a
        args.append(nc.dram_tensor(f"in_{name}", a.shape, mybir.dt.from_np(a.dtype), kind="ExternalInput").ap())
    shape = tuple(inputs["x"].shape)
    args.append(nc.dram_tensor("out_x", shape, mybir.dt.float32, kind="ExternalOutput").ap())
    graph_stack(nc, *args)
    result = run_bass_kernel_spmd(nc, [arrays], core_ids=[0])
    return result.results[0]["out_x"]
```

```python
import concourse.bass as bass
from concourse import mybir
from contextlib import ExitStack

LN_EPS = 1e-5
QUAD = 4
QUADS = 4
LAYERS = 5
GROUP_RUNS = [[(0, 25)], [(0, 9)], [(0, 1), (9, 15)], [(6, 9), (12, 15)], [(3, 6), (9, 12)]]
GROUP_GRAPHS = [4, 8, 16, 16, 16]
ZONE = 25


def graph_stack(nc, x, adj, nodemask, conv_w, w_ih, w_hh, b_ih, b_hh, theta, W_h, W_t, b_t,
                W1, b1, W2, b2, fusion_w, W3, b3, out):
    f32, f32r = mybir.dt.float32, mybir.dt.float32r
    ALU, ACT, AX = mybir.AluOpType, mybir.ActivationFunctionType, mybir.AxisListType
    B, N, D = x.shape
    RG = QUAD * QUADS
    HALF = RG // 2
    ROUNDS = B // RG
    STEPS = LAYERS * QUADS
    PRODUCED = STEPS + QUADS
    E = W1.shape[2]
    EH = E // 128
    NG = len(GROUP_RUNS)
    SIZE = [sum(b - a for a, b in runs) for runs in GROUP_RUNS]
    TILES = [(g, t * G, G, G * SIZE[g]) for g, G in enumerate(GROUP_GRAPHS) for t in range(RG // G)]
    TILES.sort(key=lambda tile: tile[1] + tile[2])
    NT = len(TILES)

    ctx = ExitStack()
    with ctx:
        ctx.enter_context(nc.allow_non_contiguous_dma("small transposed loads at the start"))

        def sb(name, shape, dt=f32):
            return ctx.enter_context(nc.sbuf_tensor(name, shape, dt))

        ident = sb("ident", [128, 128])
        neg_half, neg_one, eps_ln, eps_deg = (sb(n, [128, RG]) for n in ("neg_half", "neg_one", "eps_ln", "eps_deg"))
        top_ones = sb("top_ones", [128, 128])
        gmask = [sb(f"gmask{g}", [128, GROUP_GRAPHS[g]]) for g in range(NG)]
        mask_nat = sb("mask_nat", [B, 128])
        w3T = sb("w3T", [128, 128])
        mask_all = sb("mask_all", [128, B])
        whh_hi, whh_lo = sb("whh_hi", [128, 3, 128], f32r), sb("whh_lo", [128, 3, 128], f32r)
        wc_hi, wc_lo = sb("wc_hi", [128, LAYERS, 384], f32r), sb("wc_lo", [128, LAYERS, 384], f32r)
        bih, bhh, brz = sb("bih", [128, 3]), sb("bhh", [128, 3]), sb("brz", [128, 2])
        brz2 = sb("brz2", [128, 2])
        wl1 = sb("wl1", [128, 384])
        bt_bc, b3_bc = sb("bt_bc", [128, 128]), sb("b3_bc", [128, 128])
        w1_sb, w2_sb = sb("w1_sb", [128, NG, E]), sb("w2_sb", [128, NG, EH, 128])
        b1_sb, b2_sb = sb("b1_sb", [128, NG, EH]), sb("b2_sb", [128, NG])
        fw, fmax, fexp, fsum, finv, fshare = (sb(n, [128, NG if n in ("fw", "fexp", "fshare") else 1])
                                              for n in ("fw", "fmax", "fexp", "fsum", "finv", "fshare"))

        x_in = sb("x_in", [128, RG, 128])
        adj_in = sb("adj_in", [128, RG, 128])
        x_res = sb("x_res", [128, RG, 128])
        edge = sb("edge", [128, RG, 128])
        adjT = sb("adjT", [128, RG, 128])
        adjTI = sb("adjTI", [128, RG, 128])
        conv_nat, wih_nat, whh_nat = adjTI[:, 0:LAYERS, :], adjTI[:, 5:8, :], adjTI[:, 8:11, :]
        w3_nat, convT, wihT = adjTI[:, 11, :], adjT[:, 0:LAYERS, :], adjT[:, 5:8, :]
        mask_r = sb("mask_r", [128, RG])
        deg1, deg3 = sb("deg1", [128, RG]), sb("deg3", [128, RG])
        norm1, dis, dis_mask = sb("norm1", [128, RG]), sb("dis", [128, RG]), sb("dis_mask", [128, RG])
        degs1, degs3 = sb("degs1", [128, RG]), sb("degs3", [128, RG])
        stats = [sb(f"stats{i}", [128, RG, 6]) for i in range(2)]
        mv = [sb(f"mv{i}", [128, RG, 2]) for i in range(2)]
        var_eps, neg_mean, rstd, shift = ([sb(f"{n}{i}", [128, RG]) for i in range(2)]
                                          for n in ("var_eps", "neg_mean", "rstd", "shift"))
        xn0 = sb("xn0", [128, RG, 128])
        xn = sb("xn", [128, RG, 128])
        hT = sb("hT", [128, RG, 128])
        h = [sb(f"h{q}", [128, 512]) for q in range(QUADS)]
        h_hi = [sb(f"h_hi{q}", [128, 512], f32r) for q in range(QUADS)]
        h_lo = [sb(f"h_lo{q}", [128, 512], f32r) for q in range(QUADS)]
        hn = [sb(f"hn{i}", [128, QUAD, 128]) for i in range(2)]
        g_hi = [sb(f"g_hi{i}", [128, 512], f32r) for i in range(2)]
        g_lo = [sb(f"g_lo{i}", [128, 512], f32r) for i in range(2)]
        gr, gz, rh, pre, gn, hd, zd = ([sb(f"{n}{i}", [128, 512]) for i in range(2)]
                                       for n in ("gr", "gz", "rh", "pre", "gn", "hd", "zd"))
        f_hom = sb("f_hom", [128, 2, 512])
        gate_th, agg_n, diff, gated, mix, neg, ex = gz, rh, pre, gn, hd, zd, hn
        rows = [sb(f"rows{g}", [128, RG // GROUP_GRAPHS[g], SIZE[g]]) for g in range(NG)]
        deg2, deg_zero, deg_safe, deg_pow, dinv = (sb(n, [128, NT]) for n in
                                                   ("deg2", "deg_zero", "deg_safe", "deg_pow", "dinv"))
        deg_some = sb("deg_some", [128, NT])
        blocks0, blocks = sb("blocks0", [128, NT, 128]), sb("blocks", [128, NT, 128])
        normT = sb("normT", [128, NT, 128])
        packed = sb("packed", [128, NT, 128])
        sup1 = sb("sup1", [128, 2, E])
        hid = sb("hid", [128, 2, EH, 128])
        sup2 = sb("sup2", [128, 2, 128])
        conv2 = sb("conv2", [128, 2, 128])
        fused = sb("fused", [128, ZONE, RG])
        y = [hT[:, q * QUAD:(q + 1) * QUAD, :] for q in range(QUADS)]
        scaled = [packed[:, 4 * i:4 * i + QUAD, :] for i in range(2)]

        bank = [ctx.enter_context(nc.psum_tensor(f"bank{i}", [128, 512], f32)) for i in range(2)]
        quad_bank = ctx.enter_context(nc.psum_tensor("quad_bank", [128, 4, 512], f32))
        bank += [quad_bank[:, i, :] for i in range(4)]
        bank += [ctx.enter_context(nc.psum_tensor(f"bank{i}", [128, 512], f32)) for i in (6, 7)]
        T_BANK, G_BANK, R_BANK, Z_BANK, H_BANK, I_BANK, A_BANK, B_BANK = bank

        sem = {n: ctx.enter_context(nc.semaphore(n)) for n in (
            "weights_loaded", "late_weights_loaded", "x_loaded", "adj_loaded", "rows_loaded", "stored",
            "x_res_loaded", "adj_in_free", "rows_free", "pe_passed", "dve_passed",
            "cleared", "consts", "dve_setup", "dve_turns", "w_turned", "w_turned_read", "wc_made", "wc_hi_made", "setup_done", "fexp_done",
            "mask_round", "degs", "degs_eps", "norm1_ready", "dis_ready", "norms", "adj_turned", "adjT_ready", "adjTI_made",
            "adjT_scaled", "adjTI_scaled", "edge_ready",
            "group_sum", "group_safe", "group_pow", "blocks_half", "blocks_ready",
            "blocks_turned", "normT_ready",
            "h_new", "h_hi_new", "h_lo_new", "h_turned", "hn_ready", "g_made", "g_hi_ready",
            "g_lo_ready", "gates_r", "gates_h", "hb_ready", "gates_n", "gates_z", "r_ready", "z_ready",
            "rh_ready", "pre_ready", "n_ready", "hd_ready", "zd_ready",
            "l1_turned", "l1_x", "l1_hom_lin", "l1_gate_lin", "l1_het_lin", "l1_f_hom", "l1_gate", "l1_agg", "l1_agg_n",
            "l1_diff", "l1_gated", "l1_mix", "l1_neg", "l1_exp", "l1_elu", "l1_out",
            "zone_turned", "packed_ready", "fused_zero", "l2_sup1", "l2_sup1_read", "l2_hid",
            "l2_hid_read", "l2_sup2", "l2_sup2_read", "l2_conv2", "l2_conv2_read", "l2_added",
            "l2_back", "l2_out",
            "l3_lin", "l3_y", "l3_agg", "l3_scaled", "out_ready",
        )}
        for L in range(4):
            for n in ("stats", "mv", "var", "pow", "rstd", "xn", "turned", "h"):
                sem[f"ln{L}_{n}"] = ctx.enter_context(nc.semaphore(f"ln{L}_{n}"))

        def cols(q):
            return slice(q * QUAD, (q + 1) * QUAD)

        def per_graph(t, q):
            return t[:, cols(q)].unsqueeze(2).to_broadcast([128, QUAD, 128])

        def per_quad(t):
            return t[:].unsqueeze(1).to_broadcast([128, QUAD, 128])

        def quad(t):
            return t.rearrange("p (b d) -> p b d", b=QUAD)

        def turns(stages, units=QUADS):
            def turn_of(turn):
                for n in reversed(range(len(stages))):
                    if 0 <= turn - n < units and stages[n]:
                        stages[n](turn - n)
            return [lambda turn=turn: turn_of(turn) for turn in range(units + len(stages) - 1)]

        def pipelined(stages, units=QUADS):
            for turn in turns(stages, units):
                turn()

        def middle_layers(second_layer, turn_zone, grouped):
            begun = {ENDS: (), ENDS + 1: (0,), ENDS + 2: (1,), ENDS + 3: range(2, len(grouped))}
            for t in range(3, ENDS + QUADS):
                second_layer[t]()
                if t >= ENDS:
                    if turn_zone:
                        turn_zone(t - ENDS)
                    for u in begun[t]:
                        grouped[u]()

        def both(first, second):
            def work():
                first()
                second()
            return work

        def pause(engine, passed):
            engine.sem_inc(sem[passed], 1)

        def snap(engine, value):
            return value if isinstance(value, int) else engine.snap(value)

        def every_round(engine, work):
            work(0, False, True)
            with engine.Fori(1, ROUNDS - 1) as r:
                work(r, True, True)
            work(ROUNDS - 1, True, False)

        BLOCK_AT, used = [], [0, 0]
        for _, _, _, n in TILES:
            half = 0 if used[0] + n <= 512 else 1
            BLOCK_AT.append((half, used[half]))
            used[half] += n

        LAST_LAYER_STEPS = 15
        ENDS = 7
        N_EARLY, N_LATE = 8, 13
        row_loads = [(g, t, ra, ca) for g in range(NG) for t in range(RG // GROUP_GRAPHS[g])
                     for ra in range(len(GROUP_RUNS[g])) for ca in range(len(GROUP_RUNS[g]))]
        block = ctx.enter_context(nc.Block())

        @block.sync
        def _(sp):
            def load_adjacency(r):
                for b in range(0, RG, HALF):
                    sp.dma_start(adj_in[:, b:b + HALF], adj[bass.ds(r * RG + b, HALF)].rearrange("b n m -> n b m")
                                 ).then_inc(sem["adj_loaded"], 16)

            def load_rows(r):
                for g, t, ra, ca in row_loads:
                    G, runs = GROUP_GRAPHS[g], GROUP_RUNS[g]
                    n0 = sum(b - a for a, b in runs[:ra])
                    m0 = sum(b - a for a, b in runs[:ca])
                    (na, nb), (ma, mb) = runs[ra], runs[ca]
                    sp.dma_start(rows[g][n0 * G:(n0 + nb - na) * G, t, m0:m0 + mb - ma],
                                 adj[bass.ds(r * RG + t * G, G), na:nb, ma:mb].rearrange("b n m -> n b m")
                                 ).then_inc(sem["rows_loaded"], 16)

            def load_x(r):
                for b in range(0, RG, HALF):
                    sp.dma_start(x_in[:, b:b + HALF], x[bass.ds(r * RG + b, HALF)].rearrange("b n d -> n b d")
                                 ).then_inc(sem["x_loaded"], 16)

            load_x(0)
            w = sem["weights_loaded"]
            sp.dma_start(conv_nat[:], conv_w.rearrange("l d e -> d l e")).then_inc(w, 16)
            sp.dma_start(wih_nat[:], w_ih.rearrange("(g c) e -> c g e", g=3)).then_inc(w, 16)
            sp.dma_start(whh_nat[:], w_hh.rearrange("(g c) e -> c g e", g=3)).then_inc(w, 16)
            sp.dma_start(w3_nat[:], W3).then_inc(w, 16)
            sp.dma_start(mask_nat[:], nodemask).then_inc(w, 16)
            sp.dma_start(bih[:], b_ih.rearrange("(g c) -> c g", g=3)).then_inc(w, 16)
            sp.dma_start(bhh[:], b_hh.rearrange("(g c) -> c g", g=3)).then_inc(w, 16)
            sp.dma_start(fw[:], fusion_w.partition_broadcast(128)).then_inc(w, 16)
            load_adjacency(0)
            load_rows(0)
            w = sem["late_weights_loaded"]
            for i, t in enumerate((theta, W_h, W_t)):
                sp.dma_start(wl1[:, i * 128:(i + 1) * 128], t).then_inc(w, 16)
            sp.dma_start(bt_bc[:], b_t.partition_broadcast(128)).then_inc(w, 16)
            sp.dma_start(b3_bc[:], b3.partition_broadcast(128)).then_inc(w, 16)
            sp.dma_start(w1_sb[:], W1.rearrange("g d e -> d g e")).then_inc(w, 16)
            for g in range(NG):
                sp.dma_start(w2_sb[:, g], W2[g].rearrange("(k e) d -> e k d", k=EH)).then_inc(w, 16)
            sp.dma_start(b2_sb[:], b2.rearrange("g d -> d g")).then_inc(w, 16)
            sp.dma_start(b1_sb[:], b1.rearrange("g (k e) -> e g k", k=EH)).then_inc(w, 16)

            def store_round(done):
                for q in range(QUADS):
                    sp.wait_ge(sem["out_ready"], done * QUADS + (q + 1 - QUADS))
                    sp.dma_start(out[bass.ds(done * RG + (q * QUAD - RG), QUAD)].rearrange("b n d -> n b d"),
                                 x_res[:, cols(q), :]).then_inc(sem["stored"], 16)

            def round_of_transfers(r, before, following):
                if following:
                    sp.wait_ge(sem["ln0_xn"], r * QUADS + QUADS)
                    load_x(r + 1)
                    sp.wait_ge(sem["adj_in_free"], 2 * r + 2)
                    load_adjacency(r + 1)
                if before:
                    store_round(r)
                sp.wait_ge(sem["stored"], r * (16 * QUADS) + 16)
                for b in range(0, RG, HALF):
                    sp.dma_start(x_res[:, b:b + HALF], x[bass.ds(r * RG + b, HALF)].rearrange("b n d -> n b d")
                                 ).then_inc(sem["x_res_loaded"], 16)
                if following:
                    sp.wait_ge(sem["rows_free"], r + 1)
                    load_rows(r + 1)

            every_round(sp, round_of_transfers)
            store_round(ROUNDS)
            sp.wait_ge(sem["stored"], 16 + 16 * QUADS * ROUNDS)

        @block.tensor
        def _(pe):
            def turn_adjacency(r, q):
                dst = (A_BANK, B_BANK)[q % 2]
                pe.wait_ge(sem["adj_loaded"], r * 32 + 32)
                if q >= 2:
                    pe.wait_ge(sem["adjT_ready"], r * QUADS + q - 1)
                for j in range(QUAD):
                    last = nc.tensor.transpose(dst[:, j * 128:(j + 1) * 128], adj_in[:, q * QUAD + j, :], ident[:])
                last.then_inc(sem["adj_turned"], 1)
                if q == QUADS - 1:
                    pe.wait_ge(sem["adj_turned"], r * QUADS + QUADS)
                    pe.sem_inc(sem["adj_in_free"], 1)

            def turn_first_norm(r, q, after_adjacency=True):
                pe.wait_ge(sem["ln0_xn"], r * QUADS + q + 1)
                if q >= 2:
                    pe.wait_ge(sem["h_new"], r * PRODUCED + q - 1)
                elif after_adjacency:
                    pe.wait_ge(sem["adjT_ready"], r * QUADS + (QUADS - 1 + q))
                for j in range(QUAD):
                    last = nc.tensor.transpose((A_BANK, B_BANK)[q % 2][:, j * 128:(j + 1) * 128],
                                               xn0[:, q * QUAD + j, :], ident[:])
                last.then_inc(sem["ln0_turned"], 1)

            def turn_blocks(r, before):
                if before:
                    pe.wait_ge(sem["l3_scaled"], r * QUADS)
                pe.wait_ge(sem["adjT_ready"], r * QUADS + QUADS)
                pe.wait_ge(sem["blocks_ready"], r + 1)
                for k, (g, b0, G, n) in enumerate(TILES):
                    half, at = BLOCK_AT[k]
                    last = nc.tensor.transpose((A_BANK, B_BANK)[half][0:n, at:at + n], blocks[0:n, k, 0:n], ident[0:n, 0:n])
                last.then_inc(sem["blocks_turned"], 1)

            def turn_h(new, s):
                pe.wait_ge(sem["h_new"], new)
                for j in range(QUAD):
                    last = nc.tensor.transpose(T_BANK[:, j * 128:(j + 1) * 128], h[s][:, j * 128:(j + 1) * 128], ident[:])
                last.then_inc(sem["h_turned"], 1)

            def aggregate(step, s):
                pe.wait_ge(sem["hn_ready"], step + 1)
                for j in range(QUAD):
                    last = nc.tensor.matmul(G_BANK[:, j * 128:(j + 1) * 128], hn[s % 2][:, j, :],
                                            edge[:, s * QUAD + j, :], start=True, stop=True)
                last.then_inc(sem["g_made"], 1)

            def split_matmul(dst, w_hi, w_lo, m_hi, m_lo, start, stop):
                nc.tensor.matmul(dst[:], w_hi, m_hi, start=start, stop=False)
                nc.tensor.matmul(dst[:], w_lo, m_hi, start=False, stop=False)
                return nc.tensor.matmul(dst[:], w_hi, m_lo, start=False, stop=stop)

            def step_of(steps, new, n, following=True, middle=None):
                s, layer, k = n % QUADS, n // QUADS, n % 2
                if following:
                    turn_h(new + n + 2, (n + 1) % QUADS)
                pe.wait_ge(sem["h_lo_new"], steps + n + 1)
                pe.wait_ge(sem["hb_ready"], steps + n + 1)
                split_matmul(H_BANK, whh_hi[:, 2, :], whh_lo[:, 2, :], h_hi[s][:], h_lo[s][:], True, True).then_inc(sem["gates_h"], 1)
                pe.wait_ge(sem["r_ready"], steps + n + 1)
                split_matmul(R_BANK, whh_hi[:, 0, :], whh_lo[:, 0, :], h_hi[s][:], h_lo[s][:], True, False)
                pe.wait_ge(sem["z_ready"], steps + n + 1)
                split_matmul(Z_BANK, whh_hi[:, 1, :], whh_lo[:, 1, :], h_hi[s][:], h_lo[s][:], True, False)
                if middle:
                    middle()
                pe.wait_ge(sem["g_lo_ready"], steps + n + 1)
                if following:
                    aggregate(steps + n + 1, (n + 1) % QUADS)
                ch, cl = wc_hi[:, layer, :], wc_lo[:, layer, :]
                split_matmul(R_BANK, ch[:, 0:128], cl[:, 0:128], g_hi[k][:], g_lo[k][:], False, True).then_inc(sem["gates_r"], 1)
                pe.wait_ge(sem["pre_ready"], steps + n + 1)
                split_matmul(I_BANK, ch[:, 256:384], cl[:, 256:384], g_hi[k][:], g_lo[k][:], True, True).then_inc(sem["gates_n"], 1)
                split_matmul(Z_BANK, ch[:, 128:256], cl[:, 128:256], g_hi[k][:], g_lo[k][:], False, True).then_inc(sem["gates_z"], 1)

            pe.wait_ge(sem["consts"], 1)
            pe.wait_ge(sem["weights_loaded"], 16 * N_EARLY)
            for i in range(3):
                nc.tensor.transpose(bank[2][:, i * 128:(i + 1) * 128], wih_nat[:, i, :], ident[:])
            for i in range(3):
                nc.tensor.transpose(bank[3][:, i * 128:(i + 1) * 128], whh_nat[:, i, :], ident[:])
            for i in range(4):
                nc.tensor.transpose(bank[4][:, i * 128:(i + 1) * 128], conv_nat[:, i, :], ident[:])
            nc.tensor.transpose(bank[5][:, 0:128], conv_nat[:, 4, :], ident[:])
            nc.tensor.transpose(bank[5][:, 128:256], w3_nat[:], ident[:])
            nc.tensor.transpose(bank[5][:, 256:256 + B], mask_nat[:], ident[0:B, 0:B]).then_inc(sem["w_turned"], 1)
            for q in range(QUADS):
                turn_first_norm(0, q, False)
            pe.wait_ge(sem["h_new"], QUADS)
            pe.wait_ge(sem["w_turned_read"], 1)
            for l in range(LAYERS):
                fold = nc.tensor.matmul(bank[(0, 1, 6, 7, 2)[l]][:, 0:384], convT[:, l, :],
                                        wihT[:, :, :].rearrange("e g c -> e (g c)"), start=True, stop=True)
                fold.then_inc(sem["wc_made"], 1)
            pe.wait_ge(sem["setup_done"], 1)

            def last_layer(done):
                middle, after = [None] * STEPS, [None] * STEPS

                def number(q):
                    return done * QUADS + (q + 1 - QUADS)

                def back(q):
                    if q == 0:
                        pe.wait_ge(sem["l2_added"], done * NT)
                    if q >= 2:
                        pe.wait_ge(sem["l2_out"], number(q - 2))
                    for j in range(QUAD):
                        last = nc.tensor.transpose((A_BANK, B_BANK)[q % 2][0:ZONE, j * 128:(j + 1) * 128], fused[:, :, q * QUAD + j], ident[:])
                    last.then_inc(sem["l2_back"], 1)

                def turn(q):
                    pe.wait_ge(sem["ln3_xn"], number(q))
                    if q:
                        pe.wait_ge(sem["ln3_h"], number(q - 1))
                    else:
                        pe.wait_ge(sem["l2_out"], number(QUADS - 1))
                    for j in range(QUAD):
                        last = nc.tensor.transpose(B_BANK[:, j * 128:(j + 1) * 128], xn[:, q * QUAD + j, :], ident[:])
                    last.then_inc(sem["ln3_turned"], 1)

                def linear(q):
                    pe.wait_ge(sem["ln3_h"], number(q))
                    if q:
                        pe.wait_ge(sem["l3_y"], number(q - 1))
                    for j in range(QUAD):
                        nc.tensor.matmul(A_BANK[:, j * 128:(j + 1) * 128], hT[:, q * QUAD + j, :], w3T[:],
                                         start=True, stop=False)
                        last = nc.tensor.matmul(A_BANK[:, j * 128:(j + 1) * 128], top_ones[:], b3_bc[:],
                                                start=False, stop=True)
                    last.then_inc(sem["l3_lin"], 1)

                def aggregate_last(q):
                    if q == 0:
                        pe.wait_ge(sem["adjTI_scaled"], number(QUADS - 1))
                        pe.wait_ge(sem["ln3_h"], number(QUADS - 1))
                    if q == 1:
                        pe.wait_ge(sem["l3_y"], number(QUADS - 1))
                    if q >= 2:
                        pe.wait_ge(sem["l3_scaled"], number(q - 2))
                    pe.wait_ge(sem["l3_y"], number(q))
                    for j in range(QUAD):
                        last = nc.tensor.matmul((B_BANK, A_BANK)[q % 2][:, j * 128:(j + 1) * 128], adjTI[:, q * QUAD + j, :], y[q][:, j, :],
                                                start=True, stop=True)
                    last.then_inc(sem["l3_agg"], 1)

                for q in range(QUADS):
                    after[q] = lambda q=q: back(q)
                    middle[6 + q] = lambda q=q: turn(q)
                    after[7 + q] = lambda q=q: linear(q)
                for q in range(QUADS):
                    after[10 + q] = both(after[10], lambda: aggregate_last(0)) if q == 0 else lambda q=q: aggregate_last(q)
                return middle, after

            def round_of_products(r, before, following):
                quads = snap(pe, r * QUADS)

                def turn_norm(L, q, dst):
                    pe.wait_ge(sem[f"ln{L}_xn"], quads + q + 1)
                    if q:
                        pe.wait_ge(sem[f"ln{L}_h"], quads + q)
                    for j in range(QUAD):
                        last = nc.tensor.transpose(dst[:, j * 128:(j + 1) * 128], xn[:, q * QUAD + j, :], ident[:])
                    last.then_inc(sem[f"ln{L}_turned"], 1)

                def turn_out(q):
                    pe.wait_ge(sem["h_new"], r * PRODUCED + STEPS + q + 1)
                    if q >= 2:
                        pe.wait_ge(sem["l1_x"], quads + q - 1)
                    elif q == 0:
                        pe.wait_ge(sem["normT_ready"], r + 1)
                    for j in range(QUAD):
                        last = nc.tensor.transpose((A_BANK, B_BANK)[q % 2][:, j * 128:(j + 1) * 128],
                                                   h[q][:, j * 128:(j + 1) * 128], ident[:])
                    last.then_inc(sem["l1_turned"], 1)

                def l1_linear(q):
                    if q == 0:
                        pe.wait_ge(sem["late_weights_loaded"], 16 * N_LATE)
                    pe.wait_ge(sem["ln1_h"], quads + q + 1)
                    if q == 0:
                        pe.wait_ge(sem["r_ready"], r * STEPS + STEPS + 1)
                    else:
                        pe.wait_ge(sem["l1_f_hom"], quads + q)
                    for j in range(QUAD):
                        last = nc.tensor.matmul(R_BANK[:, j * 128:(j + 1) * 128], hT[:, q * QUAD + j, :], wl1[:, 0:128],
                                                start=True, stop=True)
                    last.then_inc(sem["l1_hom_lin"], 1)
                    if q == 0:
                        pe.wait_ge(sem["z_ready"], r * STEPS + STEPS + 1)
                    else:
                        pe.wait_ge(sem["l1_gate"], quads + q)
                    for j in range(QUAD):
                        nc.tensor.matmul(Z_BANK[:, j * 128:(j + 1) * 128], hT[:, q * QUAD + j, :], wl1[:, 256:384],
                                         start=True, stop=False)
                        last = nc.tensor.matmul(Z_BANK[:, j * 128:(j + 1) * 128], top_ones[:], bt_bc[:],
                                                start=False, stop=True)
                    last.then_inc(sem["l1_gate_lin"], 1)
                    if q < 2:
                        pe.wait_ge(sem["hb_ready" if q == 0 else "pre_ready"], r * STEPS + STEPS + 1)
                    else:
                        pe.wait_ge(sem["l1_mix"], quads + q - 1)
                    for j in range(QUAD):
                        last = nc.tensor.matmul((H_BANK, I_BANK)[q % 2][:, j * 128:(j + 1) * 128], hT[:, q * QUAD + j, :],
                                                wl1[:, 128:256], start=True, stop=True)
                    last.then_inc(sem["l1_het_lin"], 1)

                def l1_aggregate(q):
                    if q == 0:
                        pe.wait_ge(sem["adjT_scaled"], quads + QUADS)
                    else:
                        pe.wait_ge(sem["l1_diff"], quads + q)
                    pe.wait_ge(sem["l1_f_hom"], quads + q + 1)
                    for j in range(QUAD):
                        last = nc.tensor.matmul(G_BANK[:, j * 128:(j + 1) * 128], adjT[:, q * QUAD + j, :],
                                                f_hom[:, q % 2, j * 128:(j + 1) * 128], start=True, stop=True)
                    last.then_inc(sem["l1_agg"], 1)

                second_layer = turns([turn_out, None, lambda q: turn_norm(1, q, T_BANK), l1_linear, l1_aggregate,
                                      None, None, None])

                pe.wait_ge(sem["h_new"], r * PRODUCED + QUADS)
                pe.wait_ge(sem["edge_ready"], quads + QUADS)
                if before:
                    pe.wait_ge(sem["l2_conv2_read"], r * NT)
                if not before:
                    turn_h(r * PRODUCED + 1, 0)
                    aggregate(r * STEPS, 0)
                middle, after = last_layer(r) if before else ([None] * STEPS, [None] * STEPS)
                if not before:
                    for q in range(QUADS):
                        after[1 + q] = lambda q=q: turn_adjacency(r, q)
                after[15] = lambda: turn_blocks(r, before)
                after[17:] = second_layer[0:3]
                for k in range(STEPS):
                    step_of(r * STEPS, r * PRODUCED, k, k + 1 < STEPS, middle[k])
                    if after[k]:
                        after[k]()

                def turn_zone(q):
                    pe.wait_ge(sem["ln2_xn"], quads + q + 1)
                    pause(pe, "pe_passed")
                    for j in range(QUAD):
                        b = q * QUAD + j
                        last = nc.tensor.transpose(T_BANK[:, b * ZONE:(b + 1) * ZONE], xn[0:ZONE, b, :],
                                                   ident[0:ZONE, 0:ZONE])
                    last.then_inc(sem["zone_turned"], 1)

                tiles = snap(pe, r * NT)

                def l2_support(k):
                    g, b0, G, n = TILES[k]
                    pe.wait_ge(sem["packed_ready"], tiles + k + 1)
                    nc.tensor.matmul(R_BANK[0:n, 0:E], packed[:, k, 0:n], w1_sb[:, g, :],
                                     start=True, stop=True).then_inc(sem["l2_sup1"], 1)

                def l2_hidden(k):
                    g, b0, G, n = TILES[k]
                    pe.wait_ge(sem["l2_sup1_read"], tiles + k + 1)
                    for e in range(EH):
                        last = nc.tensor.matmul(Z_BANK[:, e * 128:e * 128 + n], sup1[0:n, k % 2, e * 128:(e + 1) * 128],
                                                normT[0:n, k, 0:n], start=True, stop=True)
                    last.then_inc(sem["l2_hid"], 1)

                def l2_support2(k):
                    g, b0, G, n = TILES[k]
                    pe.wait_ge(sem["l2_hid_read"], tiles + k + 1)
                    for e in range(EH):
                        last = nc.tensor.matmul(H_BANK[0:n, 0:128], hid[:, k % 2, e, 0:n], w2_sb[:, g, e, :],
                                                start=(e == 0), stop=(e == EH - 1))
                    last.then_inc(sem["l2_sup2"], 1)

                def l2_conv2(k):
                    g, b0, G, n = TILES[k]
                    pe.wait_ge(sem["l2_sup2_read"], tiles + k + 1)
                    if k:
                        pe.wait_ge(sem["l2_conv2_read"], tiles + k)
                    nc.tensor.matmul(I_BANK[:, 0:n], sup2[0:n, k % 2, :], normT[0:n, k, 0:n],
                                     start=True, stop=True).then_inc(sem["l2_conv2"], 1)

                grouped = turns([l2_support, l2_hidden, l2_support2, l2_conv2], NT)
                if following:
                    for q in range(QUADS):
                        grouped[1 + q] = both(grouped[1 + q], lambda q=q: turn_adjacency(r + 1, q))
                        grouped[5 + q] = both(grouped[5 + q], lambda q=q: turn_first_norm(r + 1, q))
                    def begin_aggregate():
                        pe.wait_ge(sem["edge_ready"], quads + (QUADS + 1))
                        aggregate(r * STEPS + STEPS, 0)
                    grouped[9] = both(grouped[9], lambda: turn_h(r * PRODUCED + (PRODUCED + 1), 0))
                    grouped[11] = both(grouped[11], begin_aggregate)
                middle_layers(second_layer, turn_zone, grouped)

            every_round(pe, round_of_products)
            middle, after = last_layer(ROUNDS)
            for k in range(LAST_LAYER_STEPS):
                for piece in (middle[k], after[k]):
                    if piece:
                        piece()

        @block.scalar
        def _(act):
            def norm_relu(L, r, q, src, dst, parts=128, graphs=range(QUAD)):
                i = 0 if L == 0 else 1
                if graphs[0] == 0:
                    act.wait_ge(sem[f"ln{L}_rstd"], r * QUADS + q + 1)
                for j in graphs:
                    b = q * QUAD + j
                    last = nc.scalar.activation(dst[0:parts, j, :], src[0:parts, b, :], ACT.Relu,
                                                bias=shift[i][0:parts, b:b + 1], scale=rstd[i][0:parts, b:b + 1])
                if graphs[-1] == QUAD - 1:
                    last.then_inc(sem[f"ln{L}_xn"], 1)

            def first_h(r, q):
                act.wait_ge(sem["ln0_turned"], r * QUADS + q + 1)
                nc.scalar.activation(h[q][:], (A_BANK, B_BANK)[q % 2][:], ACT.Copy).then_inc(sem["h_new"], 1)

            def read_adjacency(r, q):
                act.wait_ge(sem["adj_turned"], r * QUADS + q + 1)
                nc.scalar.activation(adjT[:, cols(q), :], quad((A_BANK, B_BANK)[q % 2][:, :]), ACT.Copy
                                     ).then_inc(sem["adjT_ready"], 1)

            def read_blocks(r, tiles):
                if tiles[0] == 0:
                    act.wait_ge(sem["blocks_turned"], r + 1)
                for k in tiles:
                    n, (half, at) = TILES[k][3], BLOCK_AT[k]
                    last = nc.scalar.activation(normT[0:n, k, 0:n], (A_BANK, B_BANK)[half][0:n, at:at + n],
                                                ACT.Copy, scale=dinv[0:n, k:k + 1])
                if tiles[-1] == NT - 1:
                    last.then_inc(sem["normT_ready"], 1)

            def turned_h(step, s):
                act.wait_ge(sem["h_turned"], step + 1)
                nc.scalar.activation(hn[s % 2][:], quad(T_BANK[:, :]), ACT.Copy).then_inc(sem["hn_ready"], 1)

            def aggregate_hi(step, s):
                act.wait_ge(sem["g_made"], step + 1)
                nc.scalar.activation(g_hi[s % 2][:], G_BANK[:], ACT.Copy).then_inc(sem["g_hi_ready"], 1)

            def step_of(steps, n, following=True, early=(), late=()):
                k = n % 2
                act.wait_ge(sem["gates_h"], steps + n + 1)
                nc.scalar.activation(rh[k][:], H_BANK[:], ACT.Identity, bias=bhh[:, 2:3]).then_inc(sem["hb_ready"], 1)
                for piece in early:
                    piece()
                if following:
                    aggregate_hi(steps + n + 1, (n + 1) % QUADS)
                act.wait_ge(sem["gates_r"], steps + n + 1)
                nc.scalar.activation(gr[k][:], R_BANK[:], ACT.Tanh, bias=brz[:, 0:1], scale=0.5).then_inc(sem["r_ready"], 1)
                act.wait_ge(sem["gates_z"], steps + n + 1)
                nc.scalar.activation(gz[k][:], Z_BANK[:], ACT.Tanh, bias=brz[:, 1:2], scale=0.5).then_inc(sem["z_ready"], 1)
                if n + 2 < STEPS:
                    turned_h(steps + n + 2, (n + 2) % QUADS)
                for piece in late:
                    piece()
                act.wait_ge(sem["pre_ready"], steps + n + 2)
                nc.scalar.activation(gn[k][:], pre[k][:], ACT.Tanh, bias=bih[:, 2:3]).then_inc(sem["n_ready"], 1)

            for q in range(QUADS):
                norm_relu(0, 0, q, x_in, xn0[:, cols(q), :])
            for q in range(QUADS):
                first_h(0, q)
            for l in range(LAYERS):
                act.wait_ge(sem["wc_made"], l + 1)
                nc.scalar.activation(wc_hi[:, l, :], bank[(0, 1, 6, 7, 2)[l]][:, 0:384], ACT.Copy).then_inc(sem["wc_hi_made"], 1)
            act.wait_ge(sem["dve_setup"], 1)
            nc.scalar.activation(fexp[:], fw[:], ACT.Exp, bias=fmax[:]).then_inc(sem["fexp_done"], 1)

            def last_layer(done):
                early, late = [()] * STEPS, [()] * STEPS

                def normalise(q, graphs):
                    norm_relu(3, done - 1, q, x_res, xn[:, cols(q), :], graphs=graphs)

                def read_norm(q):
                    act.wait_ge(sem["ln3_turned"], done * QUADS + (q + 1 - QUADS))
                    nc.scalar.activation(hT[:, cols(q), :], quad(B_BANK[:, :]), ACT.Copy).then_inc(sem["ln3_h"], 1)

                def read_linear(q):
                    act.wait_ge(sem["l3_lin"], done * QUADS + (q + 1 - QUADS))
                    nc.scalar.activation(y[q], quad(A_BANK[:, :]), ACT.Copy).then_inc(sem["l3_y"], 1)

                for q in range(QUADS):
                    early[4 + q] += (lambda q=q: normalise(q, range(0, 2)),)
                    late[6 + q] = (lambda q=q: read_norm(q),)
                    early[8 + q] += (lambda q=q: read_linear(q),)
                for q in range(QUADS):
                    late[4 + q] += (lambda q=q: normalise(q, range(2, 4)),)
                return early, late

            def round_of_activations(r, before, following):
                quads = snap(act, r * QUADS)
                def turned_norm(L, q):
                    act.wait_ge(sem[f"ln{L}_turned"], quads + q + 1)
                    nc.scalar.activation(hT[:, cols(q), :], quad(T_BANK[:, :]), ACT.Copy).then_inc(sem[f"ln{L}_h"], 1)

                def l1_read_linear(q):
                    k = q % 2
                    act.wait_ge(sem["l1_hom_lin"], quads + q + 1)
                    if q >= 2:
                        act.wait_ge(sem["l1_mix"], quads + q - 1)
                    nc.scalar.activation(f_hom[:, k, :], R_BANK[:], ACT.Copy).then_inc(sem["l1_f_hom"], 1)
                    act.wait_ge(sem["l1_gate_lin"], quads + q + 1)
                    nc.scalar.activation(gate_th[k][:], Z_BANK[:], ACT.Tanh, scale=0.5).then_inc(sem["l1_gate"], 1)

                def l1_exp(q):
                    k = q % 2
                    act.wait_ge(sem["l1_mix"], quads + q + 1)
                    nc.scalar.activation(neg[k][:], mix[k][:], ACT.Relu, scale=-1.0).then_inc(sem["l1_neg"], 1)
                    act.wait_ge(sem["l1_neg"], quads + q + 1)
                    if q >= 2:
                        act.wait_ge(sem["l1_elu"], quads + q - 1)
                    nc.scalar.activation(ex[k][:], quad(neg[k][:, :]), ACT.Exp, scale=-1.0).then_inc(sem["l1_exp"], 1)

                second_layer = turns([None, lambda q: norm_relu(1, r, q, x_res, xn[:, cols(q), :]),
                                      lambda q: turned_norm(1, q) if q else None, l1_read_linear, None, l1_exp, None,
                                      lambda q: norm_relu(2, r, q, x_res, xn[:, cols(q), :], ZONE)])

                if not before:
                    turned_h(r * STEPS, 0)
                    aggregate_hi(r * STEPS, 0)
                turned_h(r * STEPS + 1, 1)
                early, late = last_layer(r) if before else ([()] * STEPS, [()] * STEPS)
                if not before:
                    for q in range(QUADS):
                        early[2 + q] = (lambda q=q: read_adjacency(r, q),)
                if following:
                    for b in range(RG):
                        def norm_graph(q=b // QUAD, j=b % QUAD):
                            norm_relu(0, r + 1, q, x_in, xn0[:, cols(q), :], graphs=[j])
                        (late if b % 2 else early)[7 + b // 2] += (norm_graph,)
                for i in range(3):
                    part = range(NT * i // 3, NT * (i + 1) // 3)
                    (late if i % 2 else early)[16 + i // 2] = (lambda part=part: read_blocks(r, part),)
                late[STEPS - 1] += (lambda: turned_norm(1, 0),)
                for k in range(STEPS):
                    step_of(r * STEPS, k, k + 1 < STEPS, early[k], late[k])
                    if k >= 17:
                        second_layer[k - 17]()

                def pack_zone(q):
                    act.wait_ge(sem["zone_turned"], quads + q + 1)
                    zone = T_BANK[:, 0:RG * ZONE].rearrange("d (b n) -> d b n", b=RG)
                    for k, (g, b0, G, n) in enumerate(TILES):
                        if b0 + G != (q + 1) * QUAD:
                            continue
                        m0 = 0
                        for a, b in GROUP_RUNS[g]:
                            last = nc.scalar.activation(
                                packed[:, k, m0 * G:(m0 + b - a) * G].rearrange("d (n b) -> d n b", b=G),
                                zone[:, b0:b0 + G, a:b].rearrange("d b n -> d n b"), ACT.Copy)
                            m0 += b - a
                        last.then_inc(sem["packed_ready"], 1)

                tiles = snap(act, r * NT)

                def read_support(k):
                    n = TILES[k][3]
                    act.wait_ge(sem["l2_sup1"], tiles + k + 1)
                    nc.scalar.activation(sup1[0:n, k % 2, :], R_BANK[0:n, 0:E], ACT.Copy).then_inc(sem["l2_sup1_read"], 1)

                def read_hidden(k):
                    g, b0, G, n = TILES[k]
                    act.wait_ge(sem["l2_hid"], tiles + k + 1)
                    for e in range(EH):
                        last = nc.scalar.activation(hid[:, k % 2, e, 0:n], Z_BANK[:, e * 128:e * 128 + n], ACT.Relu,
                                                    bias=b1_sb[:, g, e:e + 1])
                    last.then_inc(sem["l2_hid_read"], 1)

                act.wait_ge(sem["late_weights_loaded"], 16 * N_LATE)
                grouped = turns([read_support, read_hidden, None, None], NT)
                if following:
                    for q in range(QUADS):
                        grouped[2 + q] = both(grouped[2 + q], lambda q=q: read_adjacency(r + 1, q))
                        grouped[6 + q] = both(grouped[6 + q], lambda q=q: first_h(r + 1, q))
                    grouped[10] = both(grouped[10], lambda: turned_h(r * STEPS + STEPS, 0))
                    grouped[11] = both(grouped[11], lambda: aggregate_hi(r * STEPS + STEPS, 0))
                middle_layers(second_layer, pack_zone, grouped)

            every_round(act, round_of_activations)
            early, late = last_layer(ROUNDS)
            for k in range(LAST_LAYER_STEPS):
                for piece in early[k] + late[k]:
                    piece()

        @block.gpsimd
        def _(pool):
            nc.gpsimd.memset(neg_half[:], -0.5)
            nc.gpsimd.memset(neg_one[:], -1.0)
            nc.gpsimd.memset(eps_ln[:], LN_EPS)
            nc.gpsimd.memset(eps_deg[:], 1e-6)
            nc.gpsimd.memset(deg2[:], 1.0)
            nc.gpsimd.memset(top_ones[:], 1.0)
            nc.gpsimd.memset(ident[:], 0.0).then_inc(sem["cleared"], 1)
            pool.wait_ge(sem["cleared"], 1)
            nc.gpsimd.affine_select(out=top_ones[:], in_=top_ones[:], compare_op=ALU.is_equal, fill=0.0, base=0,
                                    pattern=[[0, 128]], channel_multiplier=1)
            nc.gpsimd.affine_select(out=ident[:], in_=ident[:], compare_op=ALU.not_equal, fill=1.0, base=0,
                                    pattern=[[-1, 128]], channel_multiplier=1).then_inc(sem["consts"], 1)
            pool.wait_ge(sem["consts"], 1)
            pool.sem_inc(sem["stored"], 16)
            for n in ("hb_ready", "r_ready", "z_ready", "pre_ready"):
                pool.sem_inc(sem[n], 1)

            def power(L, r, q):
                c, i = cols(q), 0 if L == 0 else 1
                pool.wait_ge(sem[f"ln{L}_mv"], r * QUADS + q + 1)
                nc.gpsimd.tensor_tensor(var_eps[i][:, c], mv[i][:, c, 1], eps_ln[:, c], ALU.add)
                nc.gpsimd.tensor_tensor(neg_mean[i][:, c], mv[i][:, c, 0], neg_one[:, c], ALU.mult).then_inc(sem[f"ln{L}_var"], 1)
                pool.wait_ge(sem[f"ln{L}_var"], r * QUADS + q + 1)
                nc.gpsimd.tensor_tensor(rstd[i][:, c], var_eps[i][:, c], neg_half[:, c], ALU.pow).then_inc(sem[f"ln{L}_pow"], 1)
                pool.wait_ge(sem[f"ln{L}_pow"], r * QUADS + q + 1)
                nc.gpsimd.tensor_tensor(shift[i][:, c], neg_mean[i][:, c], rstd[i][:, c], ALU.mult).then_inc(sem[f"ln{L}_rstd"], 1)

            def group_power(r):
                pool.wait_ge(sem["group_safe"], r + 1)
                nc.gpsimd.tensor_tensor(deg_pow[:], deg_safe[:], neg_half[:, 0:NT], ALU.pow).then_inc(sem["group_pow"], 1)

            def low_half(new, s):
                pool.wait_ge(sem["h_hi_new"], new + 1)
                nc.gpsimd.tensor_tensor(h_lo[s][:], h[s][:], h_hi[s][:].bitcast(f32), ALU.subtract).then_inc(sem["h_lo_new"], 1)

            for q in range(QUADS):
                power(0, 0, q)
            for q in range(QUADS):
                low_half(q, q)

            def round_of_small_work(r, before, following):
                quads = snap(pool, r * QUADS)

                def mask_of_round():
                    nc.gpsimd.tensor_copy(mask_r[:], mask_all[:, bass.ds(r * RG, RG)]).then_inc(sem["mask_round"], 1)

                def add_identity(q):
                    pool.wait_ge(sem["adjT_ready"], quads + q + 1)
                    nc.gpsimd.tensor_tensor(adjTI[:, cols(q), :], adjT[:, cols(q), :],
                                            per_quad(ident), ALU.add).then_inc(sem["adjTI_made"], 1)

                def second_layer_degrees():
                    pool.wait_ge(sem["degs"], r * QUADS + QUADS)
                    nc.gpsimd.tensor_tensor(degs1[:], deg1[:], eps_deg[:], ALU.add)
                    nc.gpsimd.tensor_scalar(degs3[:], deg3[:], 1.0, 1e-8, ALU.add, ALU.add).then_inc(sem["degs_eps"], 1)
                    pool.wait_ge(sem["degs_eps"], r + 1)
                    nc.gpsimd.tensor_tensor(norm1[:], degs1[:], neg_half[:], ALU.pow).then_inc(sem["norm1_ready"], 1)

                def last_layer_degrees():
                    nc.gpsimd.tensor_tensor(dis[:], degs3[:], neg_half[:], ALU.pow).then_inc(sem["dis_ready"], 1)
                    pool.wait_ge(sem["dis_ready"], r + 1)
                    nc.gpsimd.tensor_tensor(dis_mask[:], dis[:], mask_r[:], ALU.mult).then_inc(sem["norms"], 1)

                def scale_adjT(q):
                    pool.wait_ge(sem["norm1_ready"], r + 1)
                    nc.gpsimd.tensor_tensor(adjT[:, cols(q), :], adjT[:, cols(q), :], per_graph(norm1, q),
                                            ALU.mult).then_inc(sem["adjT_scaled"], 1)

                def scale_adjTI(q):
                    pool.wait_ge(sem["adjTI_made"], quads + q + 1)
                    nc.gpsimd.tensor_tensor(adjTI[:, cols(q), :], adjTI[:, cols(q), :], per_graph(dis, q),
                                            ALU.mult).then_inc(sem["adjTI_scaled"], 1)

                def clear_fused():
                    nc.gpsimd.memset(fused[:], 0.0).then_inc(sem["fused_zero"], 1)

                second_layer = turns([lambda q: power(1, r, q), None, None, None, None, None,
                                      lambda q: power(2, r, q)])
                beside = [()] * STEPS
                for q in range(QUADS):
                    if before:
                        beside[2 + q] += (lambda q=q: power(3, r - 1, q),)
                    if following:
                        beside[5 + q] += (lambda q=q: power(0, r + 1, q),)
                for q in range(QUADS):
                    beside[15 + q // 2] += (lambda q=q: add_identity(q), lambda q=q: scale_adjT(q))
                beside[7] += (lambda: group_power(r),)
                beside[8] += (mask_of_round,)
                beside[9] += (second_layer_degrees,)
                if before:
                    beside[14] = (lambda: pool.wait_ge(sem["out_ready"], r * QUADS),)
                beside[16] += (clear_fused,)
                for k in range(3):
                    beside[17 + k] = (second_layer[k],)
                for k in range(STEPS):
                    if k < STEPS - QUADS:
                        low_half(r * STEPS + (QUADS + k), k % QUADS)
                    for piece in beside[k]:
                        piece()
                for turn in second_layer[3:]:
                    turn()
                last_layer_degrees()
                if following:
                    for q in range(QUADS):
                        low_half(r * STEPS + (STEPS + q), q)
                for q in range(QUADS):
                    scale_adjTI(q)

            every_round(pool, round_of_small_work)
            for q in range(QUADS):
                power(3, ROUNDS - 1, q)

        @block.vector
        def _(dve):
            def graph_stats(L, q, src, parts=128):
                i = 0 if L == 0 else 1
                for j in range(QUAD):
                    last = nc.vector.bn_stats(stats[i][0:parts, q * QUAD + j, :], src[0:parts, q * QUAD + j, :])
                last.then_inc(sem[f"ln{L}_stats"], 1)

            def mean_variance(L, r, q, parts=128):
                i = 0 if L == 0 else 1
                dve.wait_ge(sem[f"ln{L}_stats"], r * QUADS + q + 1)
                pause(dve, "dve_passed")
                for j in range(QUAD):
                    last = nc.vector.bn_aggr(mv[i][0:parts, q * QUAD + j, :], stats[i][0:parts, q * QUAD + j, :])
                last.then_inc(sem[f"ln{L}_mv"], 1)

            def norm_stats(L, r, q, src, parts=128):
                graph_stats(L, q, src, parts)
                mean_variance(L, r, q, parts)

            def edges(r, q):
                if q == 0:
                    dve.wait_ge(sem["adj_loaded"], r * 32 + 32)
                nc.vector.tensor_scalar(edge[:, cols(q), :], adj_in[:, cols(q), :], 0.0, None,
                                        ALU.not_equal).then_inc(sem["edge_ready"], 1)

            def degrees_abs(q):
                nc.vector.tensor_reduce(out=deg1[:, cols(q)], in_=adj_in[:, cols(q), :], op=ALU.add, axis=AX.X,
                                        apply_absolute_value=True)

            def degrees(r, q):
                nc.vector.tensor_reduce(out=deg3[:, cols(q)], in_=adj_in[:, cols(q), :], op=ALU.add, axis=AX.X
                                        ).then_inc(sem["degs"], 1)
                if q == QUADS - 1:
                    dve.wait_ge(sem["degs"], r * QUADS + QUADS)
                    dve.sem_inc(sem["adj_in_free"], 1)

            def group_degrees(r):
                dve.wait_ge(sem["rows_loaded"], (r + 1) * (16 * len(row_loads)))
                for k, (g, b0, G, n) in enumerate(TILES):
                    last = nc.vector.reduce_sum(deg2[0:n, k:k + 1], rows[g][0:n, b0 // G, :], axis=AX.X)
                last.then_inc(sem["group_sum"], 1)
                dve.wait_ge(sem["group_sum"], 3 * r + 1)
                nc.vector.tensor_scalar(deg_zero[:], deg2[:], -1.0, None, ALU.is_equal)
                nc.vector.tensor_scalar(deg_some[:], deg2[:], -1.0, None, ALU.not_equal).then_inc(sem["group_sum"], 1)
                dve.wait_ge(sem["group_sum"], 3 * r + 2)
                nc.vector.scalar_tensor_tensor(deg_safe[:], deg2[:], 1.0, deg_zero[:], ALU.add, ALU.add).then_inc(sem["group_safe"], 1)

            def group_norms(r):
                dve.wait_ge(sem["group_pow"], r + 1)
                nc.vector.tensor_tensor(dinv[:], deg_pow[:], deg_some[:], ALU.mult).then_inc(sem["group_sum"], 1)
                dve.wait_ge(sem["group_sum"], 3 * r + 3)

            def group_blocks(r, half):
                for k, (g, b0, G, n) in list(enumerate(TILES))[(NT // 2) * half:NT // 2 if half == 0 else NT]:
                    m = SIZE[g]
                    last = nc.vector.scalar_tensor_tensor(
                        blocks0[0:n, k, 0:n].rearrange("p (m b) -> p m b", b=G),
                        rows[g][0:n, b0 // G, :].unsqueeze(2).to_broadcast([n, m, G]), dinv[0:n, k:k + 1],
                        gmask[g][0:n, :].unsqueeze(1).to_broadcast([n, m, G]), ALU.mult, ALU.mult)
                last.then_inc(sem["blocks_half"], 1)

            def group_identity(r, half):
                dve.wait_ge(sem["blocks_half"], 2 * r + 1 + half)
                if half:
                    dve.sem_inc(sem["rows_free"], 1)
                for k, (g, b0, G, n) in list(enumerate(TILES))[(NT // 2) * half:NT // 2 if half == 0 else NT]:
                    last = nc.vector.scalar_tensor_tensor(blocks[0:n, k, 0:n], ident[0:n, 0:n], dinv[0:n, k:k + 1],
                                                          blocks0[0:n, k, 0:n], ALU.mult, ALU.add)
                if half:
                    last.then_inc(sem["blocks_ready"], 1)

            def split_h(new, s):
                dve.wait_ge(sem["h_new"], new + 1)
                nc.vector.tensor_copy(h_hi[s][:], h[s][:]).then_inc(sem["h_hi_new"], 1)

            def aggregate_lo(step, s):
                dve.wait_ge(sem["g_hi_ready"], step + 1)
                nc.vector.tensor_tensor(g_lo[s % 2][:], G_BANK[:], g_hi[s % 2][:].bitcast(f32),
                                        ALU.subtract).then_inc(sem["g_lo_ready"], 1)

            def step_of(steps, new, n, following=True, beside=()):
                s, k = n % QUADS, n % 2
                if following:
                    aggregate_lo(steps + n + 1, (n + 1) % QUADS)
                dve.wait_ge(sem["hb_ready"], steps + n + 2)
                dve.wait_ge(sem["r_ready"], steps + n + 2)
                nc.vector.scalar_tensor_tensor(rh[k][:], gr[k][:], 1.0, rh[k][:], ALU.add, ALU.mult
                                               ).then_inc(sem["rh_ready"], 1)
                dve.wait_ge(sem["rh_ready"], steps + n + 1)
                dve.wait_ge(sem["gates_n"], steps + n + 1)
                nc.vector.scalar_tensor_tensor(pre[k][:], rh[k][:], 0.5, I_BANK[:], ALU.mult, ALU.add
                                               ).then_inc(sem["pre_ready"], 1)
                for piece in beside:
                    piece()
                dve.wait_ge(sem["n_ready"], steps + n + 1)
                nc.vector.tensor_tensor(hd[k][:], h[s][:], gn[k][:], ALU.subtract).then_inc(sem["hd_ready"], 1)
                dve.wait_ge(sem["hd_ready"], steps + n + 1)
                dve.wait_ge(sem["z_ready"], steps + n + 2)
                nc.vector.scalar_tensor_tensor(zd[k][:], gz[k][:], 1.0, hd[k][:], ALU.add, ALU.mult).then_inc(sem["zd_ready"], 1)
                dve.wait_ge(sem["zd_ready"], steps + n + 1)
                nc.vector.scalar_tensor_tensor(h[s][:], zd[k][:], 0.5, gn[k][:], ALU.mult, ALU.add).then_inc(sem["h_new"], 1)
                if n < STEPS - QUADS:
                    split_h(new + QUADS + n, s)

            dve.wait_ge(sem["x_loaded"], 32)
            for q in range(QUADS):
                norm_stats(0, 0, q, x_in)
            dve.wait_ge(sem["weights_loaded"], 16 * N_EARLY)
            dve.wait_ge(sem["consts"], 1)
            nc.vector.tensor_tensor(brz2[:], bih[:, 0:2], bhh[:, 0:2], ALU.add).then_inc(sem["dve_turns"], 1)
            for g, G in enumerate(GROUP_GRAPHS):
                n = G * SIZE[g]
                nc.vector.tensor_reduce(out=gmask[g][0:n, :], in_=ident[0:n, 0:n].rearrange("p (m b) -> p b m", b=G),
                                        op=ALU.add, axis=AX.X)
            dve.wait_ge(sem["dve_turns"], 1)
            nc.vector.tensor_scalar(brz[:], brz2[:], 0.5, None, ALU.mult)
            dve.wait_ge(sem["w_turned"], 1)
            nc.vector.tensor_copy(wihT[:], bank[2][:, 0:384].rearrange("e (g c) -> e g c", g=3))
            nc.vector.tensor_copy(whh_hi[:], bank[3][:, 0:384].rearrange("e (g c) -> e g c", g=3)).then_inc(sem["dve_turns"], 1)
            nc.vector.tensor_copy(convT[:, 0:4, :], quad(bank[4]))
            nc.vector.tensor_copy(convT[:, 4, :], bank[5][:, 0:128])
            nc.vector.tensor_copy(w3T[:], bank[5][:, 128:256])
            nc.vector.tensor_copy(mask_all[:], bank[5][:, 256:256 + B])
            dve.wait_ge(sem["dve_turns"], 2)
            nc.vector.tensor_tensor(whh_lo[:], bank[3][:, 0:384].rearrange("e (g c) -> e g c", g=3),
                                    whh_hi[:].bitcast(f32), ALU.subtract).then_inc(sem["w_turned_read"], 1)
            nc.vector.tensor_reduce(out=fmax[:], in_=fw[:], op=ALU.max, axis=AX.X, negate=True).then_inc(sem["dve_setup"], 1)
            for q in range(QUADS):
                split_h(q, q)
            for q in range(QUADS):
                edges(0, q)
            for l in range(LAYERS):
                dve.wait_ge(sem["wc_hi_made"], 1 + l)
                last = nc.vector.tensor_tensor(wc_lo[:, l, :], bank[(0, 1, 6, 7, 2)[l]][:, 0:384],
                                               wc_hi[:, l, :].bitcast(f32), ALU.subtract)
            last.then_inc(sem["setup_done"], 1)
            dve.wait_ge(sem["fexp_done"], 1)
            nc.vector.reduce_sum(fsum[:], fexp[:], axis=AX.X).then_inc(sem["dve_setup"], 1)
            dve.wait_ge(sem["dve_setup"], 2)
            nc.vector.reciprocal(finv[:], fsum[:]).then_inc(sem["dve_setup"], 1)
            dve.wait_ge(sem["dve_setup"], 3)
            nc.vector.tensor_scalar(fshare[:], fexp[:], finv[:], None, ALU.mult)

            def last_layer(done):
                gap, after = [()] * STEPS, [()] * STEPS

                def grouped_residual(q):
                    dve.wait_ge(sem["l2_back"], done * QUADS + (q + 1 - QUADS))
                    nc.vector.tensor_tensor(x_res[0:ZONE, cols(q), :], quad((A_BANK, B_BANK)[q % 2][:, :])[0:ZONE],
                                            x_res[0:ZONE, cols(q), :], ALU.add).then_inc(sem["l2_out"], 1)

                def stats_of(q):
                    dve.wait_ge(sem["l2_out"], done * QUADS + (q + 1 - QUADS))
                    graph_stats(3, q, x_res)

                def scale(q):
                    dve.wait_ge(sem["l3_agg"], done * QUADS + (q + 1 - QUADS))
                    if q == 0:
                        dve.wait_ge(sem["norms"], done)
                    nc.vector.tensor_tensor(scaled[q % 2], quad((B_BANK, A_BANK)[q % 2][:, :]), per_graph(dis_mask, q),
                                            ALU.mult).then_inc(sem["l3_scaled"], 1)

                def finish(q):
                    dve.wait_ge(sem["l3_scaled"], done * QUADS + (q + 1 - QUADS))
                    nc.vector.scalar_tensor_tensor(x_res[:, cols(q), :], scaled[q % 2], 0.0, x_res[:, cols(q), :],
                                                   ALU.max, ALU.add).then_inc(sem["out_ready"], 1)

                for q in range(QUADS):
                    gap[2 + q] += (lambda q=q: mean_variance(3, done - 1, q),)
                    gap[1 + q] += (lambda q=q: grouped_residual(q),)
                    after[1 + q] += (lambda q=q: stats_of(q),)
                    gap[11 + q] += (lambda q=q: scale(q),)
                    after[11 + q] += (lambda q=q: finish(q),)
                return gap, after

            def round_of_elementwise(r, before, following):
                quads = snap(dve, r * QUADS)

                def next_stats(q):
                    if q == 0:
                        dve.wait_ge(sem["x_loaded"], r * 32 + 64)
                    graph_stats(0, q, x_in)

                def l1_residual(q):
                    if q == 0:
                        dve.wait_ge(sem["mask_round"], r + 1)
                        dve.wait_ge(sem["x_res_loaded"], r * 32 + 32)
                    dve.wait_ge(sem["l1_turned"], quads + q + 1)
                    src = (A_BANK, B_BANK)[q % 2]
                    for j in range(QUAD):
                        b = q * QUAD + j
                        last = nc.vector.scalar_tensor_tensor(x_res[:, b, :], src[:, j * 128:(j + 1) * 128],
                                                              mask_r[:, b:b + 1], x_res[:, b, :], ALU.mult, ALU.add)
                    last.then_inc(sem["l1_x"], 1)
                    dve.wait_ge(sem["l1_x"], quads + q + 1)
                    norm_stats(1, r, q, x_res)

                def l1_gate(q):
                    k = q % 2
                    het = (H_BANK, I_BANK)[k]
                    if q == 0:
                        dve.wait_ge(sem["norm1_ready"], r + 1)
                    dve.wait_ge(sem["l1_gate"], quads + q + 1)
                    dve.wait_ge(sem["l1_agg"], quads + q + 1)
                    nc.vector.tensor_tensor(quad(agg_n[k][:, :]), quad(G_BANK[:, :]), per_graph(norm1, q), ALU.mult
                                            ).then_inc(sem["l1_agg_n"], 1)
                    dve.wait_ge(sem["l1_agg_n"], quads + q + 1)
                    dve.wait_ge(sem["l1_het_lin"], quads + q + 1)
                    nc.vector.tensor_tensor(diff[k][:], agg_n[k][:], het[:], ALU.subtract).then_inc(sem["l1_diff"], 1)
                    dve.wait_ge(sem["l1_diff"], quads + q + 1)
                    nc.vector.scalar_tensor_tensor(gated[k][:], gate_th[k][:], 1.0, diff[k][:], ALU.add, ALU.mult
                                                   ).then_inc(sem["l1_gated"], 1)
                    dve.wait_ge(sem["l1_gated"], quads + q + 1)
                    if q >= 2:
                        dve.wait_ge(sem["l1_neg"], quads + q - 1)
                    nc.vector.scalar_tensor_tensor(mix[k][:], gated[k][:], 0.5, het[:], ALU.mult, ALU.add
                                                   ).then_inc(sem["l1_mix"], 1)

                def l1_finish(q):
                    k = q % 2
                    dve.wait_ge(sem["l1_exp"], quads + q + 1)
                    nc.vector.scalar_tensor_tensor(gated[k][:], mix[k][:], 0.0, ex[k][:, :, :].rearrange("p b d -> p (b d)"),
                                                   ALU.max, ALU.add).then_inc(sem["l1_elu"], 1)
                    dve.wait_ge(sem["l1_elu"], quads + q + 1)
                    nc.vector.scalar_tensor_tensor(x_res[:, cols(q), :], quad(gated[k][:, :]), -1.0, x_res[:, cols(q), :],
                                                   ALU.add, ALU.add).then_inc(sem["l1_out"], 1)
                    dve.wait_ge(sem["l1_out"], quads + q + 1)
                    norm_stats(2, r, q, x_res, ZONE)

                second_layer = turns([l1_residual, None, None, None, l1_gate, None, l1_finish, None])

                gap, after = last_layer(r) if before else ([()] * STEPS, [()] * STEPS)
                for q in range(QUADS):
                    if not before:
                        gap[q], after[q] = (lambda q=q: degrees_abs(q),), (lambda q=q: degrees(r, q),)
                    if following:
                        gap[5 + q] += (lambda q=q: next_stats(q),)
                        after[5 + q] += (lambda q=q: mean_variance(0, r + 1, q),)
                after[6] += (lambda: group_degrees(r),)
                after[8] += (lambda: group_norms(r),)
                for half in range(2):
                    gap[9 + half] += (lambda half=half: group_blocks(r, half),)
                    after[9 + half] += (lambda half=half: group_identity(r, half),)
                for k in range(3):
                    after[17 + k] += (second_layer[k],)
                aggregate_lo(r * STEPS, 0)
                for k in range(STEPS):
                    step_of(r * STEPS, r * PRODUCED, k, k + 1 < STEPS, gap[k])
                    for piece in after[k]:
                        piece()

                tiles = snap(dve, r * NT)

                def read_support2(k):
                    n = TILES[k][3]
                    dve.wait_ge(sem["l2_sup2"], tiles + k + 1)
                    nc.vector.tensor_copy(sup2[0:n, k % 2, :], H_BANK[0:n, 0:128]).then_inc(sem["l2_sup2_read"], 1)

                def add_group(k):
                    g, b0, G, n = TILES[k]
                    dve.wait_ge(sem["l2_conv2"], tiles + k + 1)
                    nc.vector.tensor_scalar(conv2[:, k % 2, 0:n], I_BANK[:, 0:n], b2_sb[:, g:g + 1], 0.0,
                                            ALU.add, ALU.max).then_inc(sem["l2_conv2_read"], 1)
                    dve.wait_ge(sem["l2_conv2_read"], tiles + k + 1)
                    if k:
                        dve.wait_ge(sem["l2_added"], tiles + k)
                    else:
                        dve.wait_ge(sem["fused_zero"], r + 1)
                    m0 = 0
                    for a, b in GROUP_RUNS[g]:
                        dst = fused[:, a:b, b0:b0 + G]
                        last = nc.vector.scalar_tensor_tensor(
                            dst, conv2[:, k % 2, m0 * G:(m0 + b - a) * G].rearrange("d (n b) -> d n b", b=G),
                            fshare[:, g:g + 1], dst, ALU.mult, ALU.add)
                        m0 += b - a
                    last.then_inc(sem["l2_added"], 1)

                dve.wait_ge(sem["late_weights_loaded"], 16 * N_LATE)
                grouped = turns([None, None, read_support2, add_group], NT)
                if following:
                    for q in range(QUADS):
                        grouped[2 + q] = both(grouped[2 + q], lambda q=q: edges(r + 1, q))
                        grouped[2 + 2 * q] = both(grouped[2 + 2 * q], lambda q=q: degrees_abs(q))
                        grouped[3 + 2 * q] = both(grouped[3 + 2 * q], lambda q=q: degrees(r + 1, q))
                        grouped[7 + q] = both(grouped[7 + q], lambda q=q: split_h(r * PRODUCED + (PRODUCED + q), q))
                middle_layers(second_layer, None, grouped)

            every_round(dve, round_of_elementwise)
            gap, after = last_layer(ROUNDS)
            for k in range(LAST_LAYER_STEPS):
                for piece in gap[k] + after[k]:
                    piece()


_INS = ['x', 'adj', 'nodemask', 'L0_gnn_weight', 'L0_gnn_w_ih', 'L0_gnn_w_hh', 'L0_gnn_b_ih', 'L0_gnn_b_hh',
        'L1_gnn_theta', 'L1_gnn_W_h', 'L1_gnn_W_t', 'L1_gnn_b_t', 'L2_gnn_W1', 'L2_gnn_b1', 'L2_gnn_W2',
        'L2_gnn_b2', 'L2_gnn_fusion_w', 'L3_gnn_W', 'L3_gnn_b']


def kernel(**inputs):
    import numpy as np
    import concourse.bacc as bacc
    from concourse.bass_utils import run_bass_kernel_spmd

    nc = bacc.Bacc("TRN2", target_bir_lowering=False, num_devices=1)
    arrays, args = {}, []
    for name in _INS:
        a = np.ascontiguousarray(inputs[name])
        arrays[f"in_{name}"] = a
        args.append(nc.dram_tensor(f"in_{name}", a.shape, mybir.dt.from_np(a.dtype), kind="ExternalInput").ap())
    shape = tuple(inputs["x"].shape)
    args.append(nc.dram_tensor("out_x", shape, mybir.dt.float32, kind="ExternalOutput").ap())
    graph_stack(nc, *args)
    result = run_bass_kernel_spmd(nc, [arrays], core_ids=[0])
    return result.results[0]["out_x"]
```
